# Optimizing a Trainium2 kernel written in Bass

```python
import numpy as np
import jax
import jax.numpy as jnp

def _softmax(x, axis=-1):
    return jax.nn.softmax(x, axis=axis)

def _gelu(x):
    return jax.nn.gelu(x, approximate=True)

def _silu(x):
    return jax.nn.silu(x)

def _sigmoid(x):
    return jax.nn.sigmoid(x)

def _layernorm(x, axis=-1, eps=1e-05):
    m = jnp.mean(x, axis=axis, keepdims=True)
    v = jnp.var(x, axis=axis, keepdims=True)
    return (x - m) / jnp.sqrt(v + eps)

def _scatter_add(tgt, idx, src, axis=0):
    return tgt.at[idx].add(src)

def _segment_sum(src, seg, n):
    return jax.ops.segment_sum(src, seg, n)
kernel_name = 'mk_vit_tower_cls_d2_tok_img1024_r4_52c7d8'

def setup_inputs(seed: int=0):
    np.random.seed(seed)
    _w = jnp.asarray

    def _rec_inputs():
        import jax
        import jax.numpy as jnp
        _rk = jax.random.key(seed)
        x = -0.00016672 + 0.999947 * jax.random.normal(jax.random.fold_in(_rk, 1), (16, 3, 96, 96), jnp.float32)
        cls_tok = 0.02 * jax.random.normal(jax.random.fold_in(_rk, 5), (1, 1, 256), jnp.float32)
        return (x, cls_tok)
    x, cls_tok = _rec_inputs()

    def _L0_tok_setup():
        import jax, jax.numpy as jnp
        import numpy as np
        B, C, H, W = (64, 3, 96, 96)
        P = 16
        HP, WP = (H // P, W // P)
        N = HP * WP
        F = C * P * P
        D = 256
        key = jax.random.key(seed)
        k1, k2, k3, k4, k5 = jax.random.split(key, 5)
        data = jax.random.normal(k1, (B, C, H, W), dtype=jnp.float32)
        lim = 1.0 / np.sqrt(F)
        W_lin = jax.random.uniform(k2, (D, F), minval=-lim, maxval=lim, dtype=jnp.float32)
        b_lin = jax.random.uniform(k3, (D,), minval=-lim, maxval=lim, dtype=jnp.float32)
        class_token = jax.random.normal(k4, (1, 1, D), dtype=jnp.float32)
        position_embeddings = jax.random.normal(k5, (1, N + 1, D), dtype=jnp.float32)
        return {'data': data, 'W_lin': W_lin, 'b_lin': b_lin, 'class_token': class_token, 'position_embeddings': position_embeddings}
    _L0_tok_all = _L0_tok_setup()
    _L0_tok_in = {k: v for k, v in _L0_tok_all.items() if k in ('W_lin', 'b_lin', 'class_token', 'position_embeddings')}
    del _L0_tok_all

    def _L0_attn_setup():
        import jax, jax.numpy as jnp
        import numpy as np
        B, S, D_MODEL = (2, 512, 256)
        H, D = (16, 64)
        D_INNER = H * D
        EPS = 1e-05
        key = jax.random.key(seed)
        ks = jax.random.split(key, 10)
        sc = 0.02
        return {'x': jax.random.normal(ks[0], (B, S, D_MODEL), dtype=jnp.float32), 'Wq': jax.random.normal(ks[1], (D_MODEL, D_INNER), dtype=jnp.float32) * sc, 'Wk': jax.random.normal(ks[2], (D_MODEL, D_INNER), dtype=jnp.float32) * sc, 'Wv': jax.random.normal(ks[3], (D_MODEL, D_INNER), dtype=jnp.float32) * sc, 'Wg': jax.random.normal(ks[4], (D_MODEL, D_INNER), dtype=jnp.float32) * sc, 'Wa': jax.random.normal(ks[5], (D_MODEL, H), dtype=jnp.float32) * sc, 'ba': jax.random.normal(ks[6], (H,), dtype=jnp.float32) * sc, 'Wo': jax.random.normal(ks[7], (D_INNER, D_MODEL), dtype=jnp.float32) * sc, 'gn_w': jnp.ones((D_INNER,), dtype=jnp.float32), 'gn_b': jnp.zeros((D_INNER,), dtype=jnp.float32)}
    _L0_attn_all = _L0_attn_setup()
    _L0_attn_in = {k: v for k, v in _L0_attn_all.items() if k in ('Wq', 'Wk', 'Wv', 'Wg', 'Wa', 'ba', 'Wo', 'gn_w', 'gn_b')}
    del _L0_attn_all

    def _L0_ffn_setup():
        import jax, jax.numpy as jnp
        import numpy as np
        B, N, DIM = (2, 512, 256)
        HEADS, DIM_HEAD, EXPERTS = (8, 64, 8)
        SCALE = DIM_HEAD ** (-0.5)
        key = jax.random.key(seed)
        ks = jax.random.split(key, 6)
        dim_inner = HEADS * DIM_HEAD
        return {'x': jax.random.normal(ks[0], (B, N, DIM), jnp.float32), 'w_q': jax.random.normal(ks[1], (DIM, dim_inner), jnp.float32) * 0.02, 'w_k': jax.random.normal(ks[2], (DIM, dim_inner), jnp.float32) * 0.02, 'w_gate': jax.random.normal(ks[3], (DIM, HEADS * EXPERTS), jnp.float32) * 0.02, 'value_experts': jax.random.normal(ks[4], (EXPERTS, HEADS, DIM, DIM_HEAD), jnp.float32) * 0.02, 'output_experts': jax.random.normal(ks[5], (EXPERTS, HEADS, DIM_HEAD, DIM), jnp.float32) * 0.02}
    _L0_ffn_all = _L0_ffn_setup()
    _L0_ffn_in = {k: v for k, v in _L0_ffn_all.items() if k in ('w_q', 'w_k', 'w_gate', 'value_experts', 'output_experts')}
    del _L0_ffn_all

    def _L1_attn_setup():
        import jax, jax.numpy as jnp
        import numpy as np
        E = 256
        H = 16
        HD = E // H
        R = 8
        T, B = (512, 2)

        def _dora_linear(x, m, V, A, Bm, b):
            Vu = V + Bm @ A
            W = m / (jnp.linalg.norm(Vu) + 1e-08) * Vu
            return x @ W.T + b
        key = jax.random.key(seed)
        ks = jax.random.split(key, 16)
        query = jax.random.normal(ks[0], (T, B, E), dtype=jnp.float32)
        kk = jax.random.normal(ks[1], (T, B, E), dtype=jnp.float32)
        vv = jax.random.normal(ks[2], (T, B, E), dtype=jnp.float32)

        def make_dora(k1, k2, k3, k4):
            w = jax.random.normal(k1, (E, E), dtype=jnp.float32) * E ** (-0.5)
            m = jnp.linalg.norm(w)
            V = w / m
            A = jax.random.normal(k2, (R, E), dtype=jnp.float32) * E ** (-0.5)
            Bm = jax.random.normal(k3, (E, R), dtype=jnp.float32) * 0.01
            b = jax.random.normal(k4, (E,), dtype=jnp.float32) * 0.01
            return (m, V, A, Bm, b)
        mag_q, dir_q, A_q, B_q, bias_q = make_dora(ks[3], ks[4], ks[5], ks[6])
        mag_v, dir_v, A_v, B_v, bias_v = make_dora(ks[7], ks[8], ks[9], ks[10])
        k_w = jax.random.normal(ks[11], (E, E), dtype=jnp.float32) * E ** (-0.5)
        k_b = jax.random.normal(ks[12], (E,), dtype=jnp.float32) * 0.01
        out_w = jax.random.normal(ks[13], (E, E), dtype=jnp.float32) * E ** (-0.5)
        out_b = jax.random.normal(ks[14], (E,), dtype=jnp.float32) * 0.01
        return dict(query=query, key=kk, value=vv, mag_q=mag_q, dir_q=dir_q, A_q=A_q, B_q=B_q, bias_q=bias_q, mag_v=mag_v, dir_v=dir_v, A_v=A_v, B_v=B_v, bias_v=bias_v, k_w=k_w, k_b=k_b, out_w=out_w, out_b=out_b)
    _L1_attn_all = _L1_attn_setup()
    _L1_attn_in = {k: v for k, v in _L1_attn_all.items() if k in ('key', 'value', 'mag_q', 'dir_q', 'A_q', 'B_q', 'bias_q', 'mag_v', 'dir_v', 'A_v', 'B_v', 'bias_v', 'k_w', 'k_b', 'out_w', 'out_b')}
    del _L1_attn_all

    def _L1_ffn_setup():
        import jax, jax.numpy as jnp
        import numpy as np
        N_EXPERT_CAPACITY = 2
        key = jax.random.key(seed)
        k1, k2, k3, k4 = jax.random.split(key, 4)
        B, S, D, E, F = (8, 256, 256, 8, 512)
        x = jax.random.normal(k1, (B, S, D), dtype=jnp.float32)
        choice_w = jax.random.uniform(k2, (E, D), dtype=jnp.float32, minval=-1.0, maxval=1.0) * (1.0 / np.sqrt(D))
        w1 = jax.random.uniform(k3, (E, D, F), dtype=jnp.float32, minval=-1.0, maxval=1.0) * (1.0 / np.sqrt(D))
        w2 = jax.random.uniform(k4, (E, F, D), dtype=jnp.float32, minval=-1.0, maxval=1.0) * (1.0 / np.sqrt(F))
        return {'x': x, 'choice_w': choice_w, 'w1': w1, 'w2': w2}
    _L1_ffn_all = _L1_ffn_setup()
    _L1_ffn_in = {k: v for k, v in _L1_ffn_all.items() if k in ('choice_w', 'w1', 'w2')}
    del _L1_ffn_all
    return {'x': x, 'cls_tok': cls_tok, 'L0_tok_W_lin': _L0_tok_in['W_lin'], 'L0_tok_b_lin': _L0_tok_in['b_lin'], 'L0_tok_class_token': _L0_tok_in['class_token'], 'L0_tok_position_embeddings': _L0_tok_in['position_embeddings'], 'L0_attn_Wq': _L0_attn_in['Wq'], 'L0_attn_Wk': _L0_attn_in['Wk'], 'L0_attn_Wv': _L0_attn_in['Wv'], 'L0_attn_Wg': _L0_attn_in['Wg'], 'L0_attn_Wa': _L0_attn_in['Wa'], 'L0_attn_ba': _L0_attn_in['ba'], 'L0_attn_Wo': _L0_attn_in['Wo'], 'L0_attn_gn_w': _L0_attn_in['gn_w'], 'L0_attn_gn_b': _L0_attn_in['gn_b'], 'L0_ffn_w_q': _L0_ffn_in['w_q'], 'L0_ffn_w_k': _L0_ffn_in['w_k'], 'L0_ffn_w_gate': _L0_ffn_in['w_gate'], 'L0_ffn_value_experts': _L0_ffn_in['value_experts'], 'L0_ffn_output_experts': _L0_ffn_in['output_experts'], 'L1_attn_key': _L1_attn_in['key'], 'L1_attn_value': _L1_attn_in['value'], 'L1_attn_mag_q': _L1_attn_in['mag_q'], 'L1_attn_dir_q': _L1_attn_in['dir_q'], 'L1_attn_A_q': _L1_attn_in['A_q'], 'L1_attn_B_q': _L1_attn_in['B_q'], 'L1_attn_bias_q': _L1_attn_in['bias_q'], 'L1_attn_mag_v': _L1_attn_in['mag_v'], 'L1_attn_dir_v': _L1_attn_in['dir_v'], 'L1_attn_A_v': _L1_attn_in['A_v'], 'L1_attn_B_v': _L1_attn_in['B_v'], 'L1_attn_bias_v': _L1_attn_in['bias_v'], 'L1_attn_k_w': _L1_attn_in['k_w'], 'L1_attn_k_b': _L1_attn_in['k_b'], 'L1_attn_out_w': _L1_attn_in['out_w'], 'L1_attn_out_b': _L1_attn_in['out_b'], 'L1_ffn_choice_w': _L1_ffn_in['choice_w'], 'L1_ffn_w1': _L1_ffn_in['w1'], 'L1_ffn_w2': _L1_ffn_in['w2']}

def reference(x, cls_tok, L0_tok_W_lin, L0_tok_b_lin, L0_tok_class_token, L0_tok_position_embeddings, L0_attn_Wq, L0_attn_Wk, L0_attn_Wv, L0_attn_Wg, L0_attn_Wa, L0_attn_ba, L0_attn_Wo, L0_attn_gn_w, L0_attn_gn_b, L0_ffn_w_q, L0_ffn_w_k, L0_ffn_w_gate, L0_ffn_value_experts, L0_ffn_output_experts, L1_attn_key, L1_attn_value, L1_attn_mag_q, L1_attn_dir_q, L1_attn_A_q, L1_attn_B_q, L1_attn_bias_q, L1_attn_mag_v, L1_attn_dir_v, L1_attn_A_v, L1_attn_B_v, L1_attn_bias_v, L1_attn_k_w, L1_attn_k_b, L1_attn_out_w, L1_attn_out_b, L1_ffn_choice_w, L1_ffn_w1, L1_ffn_w2):
    import jax
    import jax.numpy as jnp

    def _L0_tok_ref(data, W_lin, b_lin, class_token, position_embeddings):
        import jax, jax.numpy as jnp
        import numpy as np
        B, C, H, W = (64, 3, 96, 96)
        P = 16
        HP, WP = (H // P, W // P)
        N = HP * WP
        F = C * P * P
        D = 256
        b = data.shape[0]
        x = data.reshape(b, C, HP, P, WP, P)
        x = x.transpose(0, 2, 4, 1, 3, 5).reshape(b, N, F)
        x = jnp.einsum('bnf,df->bnd', x, W_lin) + b_lin
        cls = jnp.broadcast_to(class_token, (b, 1, D))
        out = jnp.concatenate([cls, x], axis=1) + position_embeddings
        return out

    def _L0_attn_ref(x, Wq, Wk, Wv, Wg, Wa, ba, Wo, gn_w, gn_b):
        import jax, jax.numpy as jnp
        import numpy as np
        B, S, D_MODEL = (2, 512, 256)
        H, D = (16, 64)
        D_INNER = H * D
        EPS = 1e-05
        b, s, _ = x.shape
        q = jax.nn.silu(jnp.einsum('bsm,md->bsd', x, Wq).reshape(b, s, H, D).transpose(0, 2, 1, 3))
        k = jax.nn.silu(jnp.einsum('bsm,md->bsd', x, Wk).reshape(b, s, H, D).transpose(0, 2, 1, 3))
        v = jnp.einsum('bsm,md->bsd', x, Wv).reshape(b, s, H, D).transpose(0, 2, 1, 3)
        log_alpha = -jax.nn.softplus(jnp.einsum('bsm,mh->bsh', x, Wa) + ba)
        cum = jnp.cumsum(log_alpha, axis=1).transpose(0, 2, 1)
        diff = cum[:, :, :, None] - cum[:, :, None, :]
        causal = jnp.tril(jnp.ones((s, s), dtype=bool))
        decay = jnp.exp(jnp.where(causal, diff, -jnp.inf))
        attn = jnp.einsum('bhid,bhjd->bhij', q, k) * decay
        o = jnp.einsum('bhij,bhjd->bhid', attn, v)
        o = o.transpose(0, 2, 1, 3)
        mean = jnp.mean(o, axis=(1, 3), keepdims=True)
        var = jnp.var(o, axis=(1, 3), keepdims=True)
        o = (o - mean) / jnp.sqrt(var + EPS)
        o = o * gn_w.reshape(H, D) + gn_b.reshape(H, D)
        o = o.reshape(b, s, H * D)
        gate = jax.nn.sigmoid(jnp.einsum('bsm,md->bsd', x, Wg))
        return jnp.einsum('bsd,dm->bsm', o * gate, Wo)

    def _L0_ffn_ref(x, w_q, w_k, w_gate, value_experts, output_experts):
        import jax, jax.numpy as jnp
        import numpy as np
        B, N, DIM = (2, 512, 256)
        HEADS, DIM_HEAD, EXPERTS = (8, 64, 8)
        SCALE = DIM_HEAD ** (-0.5)
        b, n, _ = x.shape
        q = (x @ w_q).reshape(b, n, HEADS, DIM_HEAD).transpose(0, 2, 1, 3)
        k = (x @ w_k).reshape(b, n, HEADS, DIM_HEAD).transpose(0, 2, 1, 3)
        gates = jax.nn.sigmoid((x @ w_gate).reshape(b, n, HEADS, EXPERTS).transpose(0, 2, 1, 3))
        sel = jnp.argmax(gates, axis=-1)
        gm = jax.nn.one_hot(sel, EXPERTS, dtype=x.dtype) * gates
        values = jnp.einsum('bhne,ehdk,bnd->bhnk', gm, value_experts, x)
        sim = jnp.einsum('bhid,bhjd->bhij', q * SCALE, k)
        causal_mask = jnp.triu(jnp.ones((n, n), dtype=bool), 1)
        sim = jnp.where(causal_mask, jnp.finfo(sim.dtype).min, sim)
        attn = jax.nn.softmax(sim, axis=-1)
        out = jnp.einsum('bhij,bhjk->bhik', attn, values)
        out = jnp.einsum('bhne,ehkd,bhnk->bhnd', gm, output_experts, out)
        return out.sum(axis=1)

    def _L1_attn_ref(query, key, value, mag_q, dir_q, A_q, B_q, bias_q, mag_v, dir_v, A_v, B_v, bias_v, k_w, k_b, out_w, out_b):
        import jax, jax.numpy as jnp
        import numpy as np
        E = 256
        H = 16
        HD = E // H
        R = 8
        T, B = (512, 2)

        def _dora_linear(x, m, V, A, Bm, b):
            Vu = V + Bm @ A
            W = m / (jnp.linalg.norm(Vu) + 1e-08) * Vu
            return x @ W.T + b
        Tq, Bq, _ = query.shape
        q = _dora_linear(query, mag_q, dir_q, A_q, B_q, bias_q)
        k = query @ k_w.T + k_b
        v = _dora_linear(query, mag_v, dir_v, A_v, B_v, bias_v)
        q = q.reshape(Tq, Bq * H, HD).transpose(1, 0, 2)
        k = k.reshape(Tq, Bq * H, HD).transpose(1, 0, 2)
        v = v.reshape(Tq, Bq * H, HD).transpose(1, 0, 2)
        scale = HD ** (-0.5)
        attn = jnp.einsum('nqd,nkd->nqk', q, k) * scale
        attn = jax.nn.softmax(attn, axis=-1)
        out = jnp.einsum('nqk,nkd->nqd', attn, v)
        out = out.transpose(1, 0, 2).reshape(Tq, Bq, E)
        out = out @ out_w.T + out_b
        return out

    def _L1_ffn_ref(x, choice_w, w1, w2):
        import jax, jax.numpy as jnp
        import numpy as np
        N_EXPERT_CAPACITY = 2
        B, S, D = x.shape
        E = choice_w.shape[0]
        k = S * N_EXPERT_CAPACITY // E
        probs = jax.nn.softmax(jnp.einsum('bsd,ed->bse', x, choice_w), axis=-1)
        G, I = jax.lax.top_k(jnp.swapaxes(probs, -1, -2), k)
        x_in = jnp.take_along_axis(x[:, None, :, :], I[..., None], axis=2)
        h = jax.nn.silu(jnp.einsum('bekd,edf->bekf', x_in, w1))
        x_mlp = jnp.einsum('bekf,efd->bekd', h, w2)
        b_idx = jnp.arange(B)[:, None, None]
        out = jnp.zeros_like(x).at[b_idx, I].add(G[..., None] * x_mlp)
        return out
    h = _L0_tok_ref(x, L0_tok_W_lin, L0_tok_b_lin, L0_tok_class_token, L0_tok_position_embeddings)
    h = jnp.concatenate([jnp.broadcast_to(cls_tok, (h.shape[0], 1, h.shape[2])), h], axis=1)
    h = h + _L0_attn_ref(_layernorm(h, axis=-1), L0_attn_Wq, L0_attn_Wk, L0_attn_Wv, L0_attn_Wg, L0_attn_Wa, L0_attn_ba, L0_attn_Wo, L0_attn_gn_w, L0_attn_gn_b)
    h = h + _L0_ffn_ref(_layernorm(h, axis=-1), L0_ffn_w_q, L0_ffn_w_k, L0_ffn_w_gate, L0_ffn_value_experts, L0_ffn_output_experts)
    h = h + _L1_attn_ref(_layernorm(h, axis=-1), L1_attn_key, L1_attn_value, L1_attn_mag_q, L1_attn_dir_q, L1_attn_A_q, L1_attn_B_q, L1_attn_bias_q, L1_attn_mag_v, L1_attn_dir_v, L1_attn_A_v, L1_attn_B_v, L1_attn_bias_v, L1_attn_k_w, L1_attn_k_b, L1_attn_out_w, L1_attn_out_b)
    h = h + _L1_ffn_ref(_layernorm(h, axis=-1), L1_ffn_choice_w, L1_ffn_w1, L1_ffn_w2)
    return h

_drawn_inputs = setup_inputs


def setup_inputs(seed=0):
    import zlib

    import numpy as np

    out = dict(_drawn_inputs(seed))
    spreads = {'L0_attn_gn_w': (1.0, 0.2), 'L0_attn_gn_b': (0.0, 0.1)}
    factors = {'L0_attn_ba': 32.49,
     'L0_ffn_w_q': 8.0,
     'L0_ffn_w_k': 8.0,
     'L1_attn_bias_q': 64.0,
     'L1_attn_bias_v': 8.0,
     'L1_attn_k_b': 64.0,
     'L1_attn_out_b': 8.0}
    for name, (base, spread) in spreads.items():
        noise = np.random.default_rng([zlib.crc32(name.encode()), seed]).standard_normal(out[name].shape)
        drawn = base * np.exp(spread * noise) if base else spread * noise
        out[name] = jnp.asarray(drawn.astype(out[name].dtype))
    for name, factor in factors.items():
        out[name] = (out[name] * factor).astype(out[name].dtype)
    return out
```

```python
from contextlib import ExitStack

import numpy as np
import concourse.bass as bass
from concourse import mybir

F32 = mybir.dt.float32
BF16 = mybir.dt.bfloat16
I32 = mybir.dt.int32
ALU = mybir.AluOpType
ACT = mybir.ActivationFunctionType
AXX = mybir.AxisListType.X

B, S, D = 16, 38, 256
T = B * S
HB, HT = B // 2, T // 2
NP = 36
KC = D // 128
FC0 = 6
GROUPS = ((0, 114), (114, 114), (228, 76))
GMAX = 114
H0, C0 = 16, 8
H1, E0, C1 = 8, 8, 4
H2, HD2 = 16, 16
SG = ((0, 128), (128, 128), (256, 128), (384, 128), (512, 96))
E3, F3, CAP = 8, 512, S * 2 // 8
RING = 6
NX = 20000
EPS = 1e-5

VEC = dict(b_lin=(0, 2), cls=(2, 2), class_tok=(4, 2), bias_q=(6, 2), k_b=(8, 2), out_b=(10, 2),
           gn_w=(12, 8), gn_b=(20, 8), mag_q=(28, 1), mag_v=(29, 1), even=(30, 1), odd=(31, 1))
NVEC = 32
CST = dict(ident=(0, 128), mean=(128, 128), ones=(256, 128), gn_block=(384, 128), after=(512, 128),
           neg_upto=(640, 128), pos_of=(768, S), image_of=(806, 6 * B), iota=(902, CAP), desc=(911, E0))
NCST = 919
CSB = dict(ident=(0, 128), causal_t=(128, 4 * GMAX), causal_t2=(584, 4 * 76), causal=(888, 4 * GMAX),
           causal2=(1344, 4 * 76), same_pos=(1648, 512), select=(2160, 4096))
NCSB = 6256


def segments(n_cols):
    return ((114, 0, 2), (76, 2, 3))


def psum_order():
    out = []
    add = lambda reader, *name: out.append((name, reader))
    halves = (0, 1)

    def norm(n):
        for hf in halves:
            add("dve", "mean", n, hf)
        for hf in halves:
            add("act", "var", n, hf)

    for hf in halves:
        for mc in range(KC):
            add("dve", "tok", hf, mc)
    norm(0)
    for w in range(2):
        for kc in range(KC):
            add("dve", "dora", w, kc)
    add("dve", "fro")

    def project0(hf):
        add("dve", "la", hf)
        for c in range(C0):
            add("act", "q0", hf, c)
            add("act", "k0", hf, c)
        for g in range(3):
            for n in range(2):
                add("dve", "v0", hf, g, n)

    def attend0(hf):
        for n in range(7):
            if n < 6:
                for par in range(2):
                    add("act", "decay", hf, n, par)
                for par in range(2):
                    add("dve", "score0", hf, n, par)
            if n >= 1:
                add("act", "pv0", hf, n - 1)
        for c in range(C0):
            add("act", "g0", hf, c)

    def close0(hf):
        add("dve", "gn", hf)
        for mc in range(KC):
            add("dve", "wo", hf, mc)

    project0(0)
    attend0(0)
    project0(1)
    close0(0)
    attend0(1)
    close0(1)
    norm(1)
    for hf in halves:
        for c in range(C1):
            add("act", "q1", hf, c)
            add("act", "k1", hf, c)
        add("act", "gate1", hf)
        for g in range(3):
            for par in range(2):
                add("dve", "score1", hf, g, par)
        add("act", "onehot_t", hf)
        for g in range(3):
            for e in range(E0):
                add("act" if e == 0 else "dve", "val", hf, g, e)
            if g >= 1:
                add("act", "pv1", hf, g - 1)
            for par in range(2):
                add("act", "pt1", hf, g, par)
        add("act", "pv1", hf, 2)
        for i in range(E0 * C1):
            add("dve", "sel", hf, i)
    norm(2)
    for hf in halves:
        for mc in range(KC):
            add("act", "q2", hf, mc)
            add("act", "k2", hf, mc)
    for sg in range(5):
        add("dve", "v2", sg)
    for part in range(2):
        for j in range(4):
            add("dve", "score2", j, part)
    for sg in range(5):
        for qd in range(SG[sg][1] // 32):
            add("dve", "pv2", sg, qd)
    for sg in range(5):
        add("act", "o2t", sg)
    for hf in halves:
        for mc in range(KC):
            add("dve", "out2", hf, mc)
    norm(3)
    for hf in halves:
        add("dve", "route", hf)
    add("dve", "probs_t")
    for b2 in range(8):
        add("act", "x_tok", b2)
    add("dve", "rank_t")
    for kc in range(KC):
        for b4 in range(4):
            add("dve", "gather", kc, b4)
    for hf in halves:
        add("act", "scatter_t", hf)
    for e in range(E3 + 1):
        if e < E3:
            for f2 in range(2):
                add("act", "hid", e, f2)
        if e >= 1:
            add("dve", "y", e - 1)
    for b2 in range(8):
        add("act", "y_tok", b2)
    for hf in halves:
        for mc in range(KC):
            add("dve", "res3", hf, mc)
    return out


PSUM_TILES = psum_order()
TILE_NO = {name: i for i, (name, _) in enumerate(PSUM_TILES)}
READ_NO = {}
_counts = {"act": 0, "dve": 0}
for _name, _reader in PSUM_TILES:
    _counts[_reader] += 1
    READ_NO[_name] = (_reader, _counts[_reader])


def build(nc, io):
    with ExitStack() as ctx:
        def sem(name):
            return ctx.enter_context(nc.semaphore(name))

        def sb(name, shape, dt=F32):
            return ctx.enter_context(nc.sbuf_tensor(name, shape, dt))

        h = sb("h", [128, KC, T])
        hn = sb("hn", [128, KC, T])
        hc = sb("hc", [128, 2, KC, HT])
        sq = sb("sq", [128, 2, KC, HT])
        std = sb("std", [128, 2, HT])
        rstd = sb("rstd", [128, HT])
        cst = sb("cst", [128, NCST])
        csb_bits = sb("csb", [128, NCSB], mybir.dt.uint16)
        csb = csb_bits[:, :].bitcast(BF16)
        vec = sb("vec", [128, NVEC])
        rows = sb("rows", [128, 16 + 256])
        tokadd = sb("tokadd", [128, KC, S])
        eps_col = sb("eps_col", [128, 1])
        one_col = sb("one_col", [128, 1])
        kb_even_odd = sb("kb_even_odd", [128, 2, KC])
        region_a = sb("region_a", [128, 10240 + 32])
        region_v = sb("region_v", [128, 8192])
        region_x = sb("region_x", [128, NX])
        small_w = sb("small_w", [128, 2 * 1024 + 128 + 4 * 512 + 16])

        ident = cst[:, 0:128]

        def const(name):
            o, n = CST[name]
            return cst[:, o:o + n]

        def constb(name):
            o, n = CSB[name]
            return csb[:, o:o + n]

        def col(name, i=0):
            o = VEC[name][0] + i
            return vec[:, o:o + 1]

        def cols(name):
            o, n = VEC[name]
            return vec[:, o:o + n]

        class Cut:
            def __init__(self, region, at=0):
                self.region, self.at = region, at

            def __call__(self, n, pattern=None, dt=None, **sizes):
                piece = self.region[:, self.at:self.at + n]
                self.at += n
                if dt is not None:
                    piece = piece.bitcast(dt)
                return piece.rearrange(pattern, **sizes) if pattern else piece

        cut = Cut(region_a)
        wq0, wk0, wv0, wg0 = (cut(2048, "p (k n) -> p k n", k=KC) for _ in range(4))
        wo0 = cut(2048, "p (c n) -> p c n", c=C0)
        wa0 = cut(32, "p (k n) -> p k n", k=KC)
        out_exp = region_a[:, 0:8192].rearrange("p (e c n) -> p e c n", e=E0, c=C1)

        cut = Cut(region_v)
        patches = cut(FC0 * B * NP, "p (k n) -> p k n", k=FC0)
        wlin = cut(FC0 * D, "p (k n) -> p k n", k=FC0)
        val_exp = region_v[:, 0:8192].rearrange("p (k e n) -> p k e n", k=KC, e=E0)
        w2 = region_v[:, 0:8192].rearrange("p (e f n) -> p e f n", e=E3, f=4)

        cut = Cut(small_w)
        wq1, wk1 = (cut(1024, "p (k n) -> p k n", k=KC) for _ in range(2))
        wgate1 = cut(128, "p (k n) -> p k n", k=KC)
        dora_w = [cut(512, "p (k n) -> p k n", k=KC) for _ in range(2)]
        wk2, wout2 = (cut(512, "p (k n) -> p k n", k=KC) for _ in range(2))
        choice3 = cut(16, "p (k n) -> p k n", k=KC)

        cut = Cut(region_x)
        q0, k0, g0, osb = (cut(C0 * HT, "p (c n) -> p c n", c=C0) for _ in range(4))
        v0 = cut(3 * 1024, "p (g n) -> p g n", g=3)
        gsq = cut(4 * HT)
        steps = [cut(8 * GMAX) for _ in range(2)]
        decay = [cut(4 * GMAX) for _ in range(3)]
        att_space = region_x[:, cut.at:cut.at + 16 * GMAX]
        att = [cut(4 * GMAX) for _ in range(4)]
        la = cut(48, "p (g n) -> p g n", g=3)
        la_abs = cut(48, "p (g n) -> p g n", g=3)
        la_exp = cut(48, "p (g n) -> p g n", g=3)
        la_ln = cut(48, "p (g n) -> p g n", g=3)
        gsum = cut(128)
        gmean = cut(128)
        gvar = cut(64)
        gstd = cut(64)
        gscale = cut(64)
        gshift = cut(64)
        cut = Cut(region_x)
        q1, k1, gout = (cut(C1 * HT, "p (c n) -> p c n", c=C1) for _ in range(3))
        vals = cut(3 * 512, "p (g n) -> p g n", g=3)
        prob1 = [cut(4 * GMAX) for _ in range(6)]
        prob1t = [cut(4 * GMAX) for _ in range(4)]
        gated = [cut(HT) for _ in range(4)]
        gate = cut(192, "p (g n) -> p g n", g=3)
        onehot = cut(192, "p (g n) -> p g n", g=3)
        ohwork = cut(192, "p (g n) -> p g n", g=3)
        gmax = cut(24, "p (g n) -> p g n", g=3)
        ohmax = cut(24, "p (g n) -> p g n", g=3)
        negmax1 = cut(24)
        sum1 = cut(24)
        onehot_t = cut(HT // 2, dt=BF16)
        end1 = cut.at
        w1 = Cut(region_x, NX - 8192)(8192, "p (k e n) -> p k e n", k=KC, e=E3)
        assert end1 <= NX - 8192
        cut = Cut(region_x)
        q2, keven, kodd, o2t = (cut(KC * T, "p (k n) -> p k n", k=KC) for _ in range(4))
        v2 = cut(5 * H2 * 17, "p (g h n) -> p g h n", g=5, h=H2)
        prob2 = [[cut(n) for _ in range(4)] for n in (512, 128)]
        cut_a = Cut(region_a)
        prob2t = [[cut_a(n) for _ in range(4)] for n in (512, 128)]
        o2 = cut(5 * D, "p (g n) -> p g n", g=5)
        rden2 = cut(5 * H2, "p (g n) -> p g n", g=5)
        negmax2 = cut(128)
        assert cut.at <= NX - 8192
        cut = Cut(region_x)
        probs = cut(6 * E3, "p (g n) -> p g n", g=6)
        pwork = cut(6 * E3, "p (g n) -> p g n", g=6)
        psum3 = cut(6, "p (g n) -> p g n", g=6)
        pspread = [cut(128) for _ in range(2)]
        pt = cut(2 * S)
        above_at = cut.at
        above = cut(S * S, "p (a b) -> p a b", a=S)
        equal = cut(S * S, "p (a b) -> p a b", a=S)
        before = cut(S * S, "p (a b) -> p a b", a=S)
        ptt = cut(256)
        pick = cut(B * E3 * CAP)
        pickw = cut(B * E3 * CAP)
        x_tok = cut(B * D, "p (b n) -> p b n", b=B)
        assert cut.at <= NX - 8192
        x_in = Cut(region_x, above_at)(KC * E3 * B * CAP, "p (k e b c) -> p k e b c", k=KC, e=E3, b=B)
        cut = Cut(region_a)
        y_t = cut(KC * B * E3 * CAP, "p (k b e c) -> p k b e c", k=KC, b=B, e=E3)
        y_tok = cut(B * D, "p (b n) -> p b n", b=B)
        scatter_t = cut(T)
        hid = [cut(4 * B * CAP, "p (f n) -> p f n", f=4) for _ in range(2)]
        res = cut(2 * HT * KC, "p (k n) -> p k n", k=KC)
        assert cut.at <= 10240
        fro = sb("fro", [128, 16])
        lora = att_space[0:8, 0:4 * D]
        junk = gsq[:, 0:D]

        ring = [ctx.enter_context(nc.psum_tensor(f"ring{i}", [128, 512], F32)) for i in range(RING)]
        acc = [ctx.enter_context(nc.psum_tensor(f"acc{i}", [128, 512], F32)) for i in range(2)]

        loaded = {n: sem(f"loaded_{n}") for n in (
            "cst", "csb", "vec", "rows", "pos", "patches", "wlin", "wa", "wq", "wk", "wv", "wg", "wo",
            "lora", "dora0", "dora1", "q1", "k1", "gate1", "k2", "out2", "choice", "val", "oexp",
            "w1", "w2", "before")}
        tiles_filled = sem("tiles_filled")
        act_evac = sem("act_evac")
        dve_evac = sem("dve_evac")
        consts_set = sem("consts_set")
        tok_added = sem("tok_added")
        squared = sem("squared")
        normed = sem("normed")
        dve_step = sem("dve_step")
        act_step = sem("act_step")
        pool_step = sem("pool_step")
        la_abs_done = sem("la_abs_done")
        la_ln_done = sem("la_ln_done")
        la_done = sem("la_done")
        steps_done = sem("steps_done")
        gsq_done = sem("gsq_done")
        gsq_read = sem("gsq_read")
        gvar_done = sem("gvar_done")
        gstd_done = sem("gstd_done")
        gn_scaled = sem("gn_scaled")
        gn_shifted = sem("gn_shifted")
        gn_gated = sem("gn_gated")
        onehot_done = sem("onehot_done")
        exp1_done = sem("exp1_done")
        scale1_done = sem("scale1_done")
        prob1_done = sem("prob1_done")
        vals_done = sem("vals_done")
        experts_done = sem("experts_done")
        experts_added = sem("experts_added")
        dora_done = sem("dora_done")
        dora_sq = sem("dora_sq")
        fro_done = sem("fro_done")
        exp2_done = sem("exp2_done")
        prob2t_done = sem("prob2t_done")
        exp3_done = sem("exp3_done")
        shifted3 = sem("shifted3")
        probs_done = sem("probs_done")
        spread_done = sem("spread_done")
        rank_done = sem("rank_done")
        pick_done = sem("pick_done")
        pickw_done = sem("pickw_done")
        stored = sem("stored")
        gated_used = sem("gated_used")
        spread_used = sem("spread_used")

        def filled(*name):
            return TILE_NO[name] + 1

        def evacuated(*name):
            return READ_NO[name][1]

        def bank(*name):
            return ring[TILE_NO[name] % RING]

        def chunk_tokens(g, hf):
            off, n = GROUPS[g]
            return hf * HT + off, n

        def images(ap, n=HB):
            return ap.rearrange("p (b s) -> p b s", s=S)

        block = ctx.enter_context(nc.Block())

        @block.sync
        def _(sp):

            def load(name, dst):
                sp.dma_start(dst, io[name]).then_inc(loaded[name], 16)

            load("patches", patches)
            load("wlin", wlin)
            load("wa", wa0)
            load("wq", wq0)
            load("wk", wk0)
            load("wv", wv0)
            load("wg", wg0)
            load("wo", wo0)
            load("q1", wq1)
            load("k1", wk1)
            load("gate1", wgate1)
            load("k2", wk2)
            load("out2", wout2)
            load("choice", choice3)
            sp.wait_ge(tiles_filled, filled("tok", 1, KC - 1))
            load("val", val_exp)
            sp.wait_ge(tiles_filled, filled("wo", 1, KC - 1))
            load("oexp", out_exp)
            load("w1", w1)
            sp.wait_ge(tiles_filled, filled("val", 1, 2, E0 - 1))
            load("w2", w2)
            sp.wait_ge(tiles_filled, filled("out2", 1, KC - 1))
            load("before", before.rearrange("p a b -> p (a b)"))
            for hf in range(2):
                sp.wait_ge(dve_evac, evacuated("res3", hf, KC - 1))
                for kc in range(KC):
                    sp.dma_start(io["out"][kc * 128:(kc + 1) * 128, hf * HT:(hf + 1) * HT],
                                 res[:, kc, hf * HT:(hf + 1) * HT]).then_inc(stored, 16)
            sp.wait_ge(stored, 16 * 2 * KC)

        @block.tensor
        def _(pe):
            mm = nc.tensor.matmul
            next_tile = [0]

            def open_tile(*name):
                n = next_tile[0]
                assert PSUM_TILES[n][0] == name, (PSUM_TILES[n], name)
                next_tile[0] += 1
                if n >= RING:
                    before_it, reader = PSUM_TILES[n - RING]
                    if reader == "act":
                        pe.wait_ge(act_evac, evacuated(*before_it))
                    else:
                        pe.wait_ge(dve_evac, evacuated(*before_it))
                return ring[n % RING]

            def norm(n):
                pe.wait_ge(loaded["cst"], 16)
                for hf in range(2):
                    if n == 0:
                        pe.wait_ge(tok_added, 1)
                        pe.wait_ge(dve_evac, evacuated("tok", hf, KC - 1))
                    elif n == 1:
                        pe.wait_ge(dve_evac, evacuated("wo", hf, KC - 1))
                    elif n == 2:
                        pe.wait_ge(experts_added, hf + 1)
                    else:
                        pe.wait_ge(dve_evac, evacuated("out2", 1, KC - 1))
                    p = open_tile("mean", n, hf)
                    for kc in range(KC):
                        last = mm(p[:, 0:HT], const("mean"), h[:, kc, hf * HT:(hf + 1) * HT],
                                  start=(kc == 0), stop=(kc == KC - 1))
                    last.then_inc(tiles_filled, 1)
                for hf in range(2):
                    pe.wait_ge(squared, 2 * n + hf + 1)
                    p = open_tile("var", n, hf)
                    for kc in range(KC):
                        last = mm(p[:, 0:HT], const("mean"), sq[:, hf, kc, :],
                                  start=(kc == 0), stop=(kc == KC - 1))
                    last.then_inc(tiles_filled, 1)

            def project(name, w, rhs, n_out=1):
                p = open_tile(*name)
                for kc in range(KC):
                    last = mm(p[:, 0:rhs.shape[2]], w[:, kc, :], rhs[:, kc, :],
                              start=(kc == 0), stop=(kc == KC - 1))
                last.then_inc(tiles_filled, 1)

            pe.wait_ge(loaded["patches"], 16)
            pe.wait_ge(loaded["wlin"], 16)
            for hf in range(2):
                for mc in range(KC):
                    p = open_tile("tok", hf, mc)
                    for fc in range(FC0):
                        last = mm(p[:, 0:HB * NP], wlin[:, fc, mc * 128:(mc + 1) * 128],
                                  patches[:, fc, hf * HB * NP:(hf + 1) * HB * NP],
                                  start=(fc == 0), stop=(fc == FC0 - 1))
                    last.then_inc(tiles_filled, 1)
            norm(0)
            pe.wait_ge(loaded["lora"], 16)
            for w in range(2):
                for kc in range(KC):
                    p = open_tile("dora", w, kc)
                    mm(p[:, 0:D], lora[:, (2 * w) * D + kc * 128:(2 * w) * D + (kc + 1) * 128],
                       lora[:, (2 * w + 1) * D:(2 * w + 2) * D], start=True, stop=True).then_inc(tiles_filled, 1)
            pe.wait_ge(dora_sq, 4)
            p = open_tile("fro")
            mm(p[:, 0:4], const("ones"), fro[:, 0:4], start=True, stop=True).then_inc(tiles_filled, 1)

            def project0(hf):
                pe.wait_ge(normed, hf + 1)
                tok = hn[:, :, hf * HT:(hf + 1) * HT]
                pe.wait_ge(loaded["wa"], 16)
                p = open_tile("la", hf)
                for g in range(3):
                    t0, n = chunk_tokens(g, hf)
                    for kc in range(KC):
                        last = mm(p[0:n, g * 16:g * 16 + 16], hn[:, kc, t0:t0 + n], wa0[:, kc, :],
                                  start=(kc == 0), stop=(kc == KC - 1))
                last.then_inc(tiles_filled, 1)
                pe.wait_ge(loaded["wq"], 16)
                pe.wait_ge(loaded["wk"], 16)
                for c in range(C0):
                    project(("q0", hf, c), wq0[:, :, c * 128:(c + 1) * 128], tok)
                    project(("k0", hf, c), wk0[:, :, c * 128:(c + 1) * 128], tok)
                pe.wait_ge(loaded["wv"], 16)
                for g in range(3):
                    t0, n = chunk_tokens(g, hf)
                    for half in range(2):
                        p = open_tile("v0", hf, g, half)
                        for kc in range(KC):
                            last = mm(p[0:n, :], hn[:, kc, t0:t0 + n], wv0[:, kc, half * 512:(half + 1) * 512],
                                      start=(kc == 0), stop=(kc == KC - 1))
                        last.then_inc(tiles_filled, 1)

            def attend0(hf):
                pe.wait_ge(loaded["csb"], 16)
                pe.wait_ge(act_evac, evacuated("k0", hf, C0 - 1))
                for n in range(7):
                    if n < 6:
                        g, upper = n // 2, n % 2
                        off, r = GROUPS[g]
                        pe.wait_ge(steps_done, 6 * hf + n + 1)
                        st = steps[n % 2][:, 0:8 * r].rearrange("p (h i) -> p h i", h=8)
                        neg = constb("causal_t" if r == GMAX else "causal_t2")
                        for par in range(2):
                            p = open_tile("decay", hf, n, par)
                            mm(p[0:r, 0:4 * r], const("after")[0:r, 0:r], st[0:r, par::2, :], start=True, stop=False)
                            mm(p[0:r, 0:4 * r], constb("ident")[0:r, 0:r], neg[0:r, :],
                               start=False, stop=True).then_inc(tiles_filled, 1)
                        for par in range(2):
                            p = open_tile("score0", hf, n, par)
                            base = 64 * par
                            for x in range(4):
                                c = 4 * upper + x
                                last = mm(p[0:r, x * r:(x + 1) * r], k0[base:base + 64, c, off:off + r],
                                          q0[base:base + 64, c, off:off + r], start=True, stop=True)
                            last.then_inc(tiles_filled, 1)
                    if n >= 1:
                        m = n - 1
                        g, upper = m // 2, m % 2
                        off, r = GROUPS[g]
                        pe.wait_ge(dve_evac, evacuated("v0", hf, g, upper))
                        pe.wait_ge(dve_evac, evacuated("score0", hf, m, 1))
                        p = open_tile("pv0", hf, m)
                        for par in range(2):
                            a = att[(2 * m + par) % 4]
                            for x in range(4):
                                hd = 2 * (4 * upper + x) + par
                                last = mm(p[64 * par:64 * par + 64, x * r:(x + 1) * r],
                                          v0[0:r, g, hd * 64:(hd + 1) * 64], a[0:r, x * r:(x + 1) * r],
                                          start=True, stop=True)
                        last.then_inc(tiles_filled, 1)
                pe.wait_ge(loaded["wg"], 16)
                for c in range(C0):
                    project(("g0", hf, c), wg0[:, :, c * 128:(c + 1) * 128], hn[:, :, hf * HT:(hf + 1) * HT])

            def close0(hf):
                pe.wait_ge(gsq_read, 2 * hf + 2)
                p = open_tile("gn", hf)
                mm(p[:, 0:128], const("gn_block"), gsum, start=True, stop=True).then_inc(tiles_filled, 1)
                pe.wait_ge(loaded["wo"], 16)
                pe.wait_ge(gn_gated, 2 * hf + 2)
                for mc in range(KC):
                    p = open_tile("wo", hf, mc)
                    for c in range(C0):
                        last = mm(p[:, 0:HT], wo0[:, c, mc * 128:(mc + 1) * 128], osb[:, c, :],
                                  start=(c == 0), stop=(c == C0 - 1))
                    last.then_inc(tiles_filled, 1)

            project0(0)
            attend0(0)
            project0(1)
            close0(0)
            attend0(1)
            close0(1)
            norm(1)

            for hf in range(2):
                pe.wait_ge(normed, 2 + hf + 1)
                tok = hn[:, :, hf * HT:(hf + 1) * HT]
                pe.wait_ge(loaded["q1"], 16)
                pe.wait_ge(loaded["k1"], 16)
                for c in range(C1):
                    project(("q1", hf, c), wq1[:, :, c * 128:(c + 1) * 128], tok)
                    project(("k1", hf, c), wk1[:, :, c * 128:(c + 1) * 128], tok)
                pe.wait_ge(loaded["gate1"], 16)
                p = open_tile("gate1", hf)
                for g in range(3):
                    t0, n = chunk_tokens(g, hf)
                    for kc in range(KC):
                        last = mm(p[0:n, g * 64:g * 64 + 64], hn[:, kc, t0:t0 + n], wgate1[:, kc, :],
                                  start=(kc == 0), stop=(kc == KC - 1))
                last.then_inc(tiles_filled, 1)
                pe.wait_ge(act_evac, evacuated("k1", hf, C1 - 1))
                for g in range(3):
                    off, r = GROUPS[g]
                    neg = constb("causal" if r == GMAX else "causal2")
                    for par in range(2):
                        base = 64 * par
                        p = open_tile("score1", hf, g, par)
                        mm(p[0:r, 0:4 * r], constb("ident")[0:r, 0:r], neg[0:r, :], start=True, stop=True)
                        for x in range(C1):
                            last = mm(p[0:r, x * r:(x + 1) * r], q1[base:base + 64, x, off:off + r],
                                      k1[base:base + 64, x, off:off + r], start=False, stop=True,
                                      skip_group_check=True)
                        last.then_inc(tiles_filled, 1)
                pe.wait_ge(onehot_done, hf + 1)
                p = open_tile("onehot_t", hf)
                for g in range(3):
                    off, r = GROUPS[g]
                    last = nc.tensor.transpose(p[0:64, off:off + r], onehot[0:r, g, :], ident[0:r, 0:r])
                last.then_inc(tiles_filled, 1)

                def pv1(g):
                    off, r = GROUPS[g]
                    pe.wait_ge(vals_done, 3 * hf + g + 1)
                    pe.wait_ge(act_evac, evacuated("pt1", hf, g, 1))
                    p = open_tile("pv1", hf, g)
                    for par in range(2):
                        a = prob1t[(2 * g + par) % 4]
                        for x in range(C1):
                            hd = 2 * x + par
                            last = mm(p[64 * par:64 * par + 64, x * r:(x + 1) * r],
                                      vals[0:r, g, hd * 64:(hd + 1) * 64], a[0:r, x * r:(x + 1) * r],
                                      start=True, stop=True)
                    last.then_inc(tiles_filled, 1)

                pe.wait_ge(loaded["val"], 16)
                for g in range(3):
                    t0, r = chunk_tokens(g, hf)
                    for e in range(E0):
                        p = open_tile("val", hf, g, e)
                        for kc in range(KC):
                            last = mm(p[0:r, :], hn[:, kc, t0:t0 + r], val_exp[:, kc, e, :],
                                      start=(kc == 0), stop=(kc == KC - 1))
                        last.then_inc(tiles_filled, 1)
                    if g >= 1:
                        pv1(g - 1)
                    for par in range(2):
                        pe.wait_ge(prob1_done, 6 * hf + 2 * g + par + 1)
                        p = open_tile("pt1", hf, g, par)
                        for x in range(C1):
                            last = nc.tensor.transpose(p[0:r, x * r:(x + 1) * r],
                                                       prob1[2 * g + par][0:r, x * r:(x + 1) * r], ident[0:r, 0:r])
                        last.then_inc(tiles_filled, 1)
                pv1(2)
                pe.wait_ge(loaded["oexp"], 16)
                pe.wait_ge(act_evac, evacuated("onehot_t", hf))
                pe.wait_ge(act_evac, evacuated("pv1", hf, 2))
                if hf:
                    pe.wait_ge(experts_added, hf)
                n = E0 * C1
                for i in range(n + 3):
                    if i < n:
                        p = open_tile("sel", hf, i)
                        sel = constb("select")[0:64, i * 128:(i + 1) * 128]
                        mm(p[:, 0:HT], sel, onehot_t[0:64, 0:HT], start=True, stop=True).then_inc(tiles_filled, 1)
                    if i >= 3:
                        j = i - 3
                        pe.wait_ge(dve_evac, evacuated("sel", hf, j))
                        for mc in range(KC):
                            last = mm(acc[mc][:, 0:HT], out_exp[:, j // C1, j % C1, mc * 128:(mc + 1) * 128],
                                      gated[j % 4], start=(j == 0), stop=(j == n - 1))
                        if j == n - 1:
                            last.then_inc(experts_done, 1)
                        else:
                            last.then_inc(gated_used, 1)
            norm(2)

            pe.wait_ge(normed, 6)
            pe.wait_ge(dora_done, 1)
            pe.wait_ge(loaded["k2"], 16)
            for hf in range(2):
                tok = hn[:, :, hf * HT:(hf + 1) * HT]
                for mc in range(KC):
                    project(("q2", hf, mc), dora_w[0][:, :, mc * 128:(mc + 1) * 128], tok)
                    project(("k2", hf, mc), wk2[:, :, mc * 128:(mc + 1) * 128], tok)
            for sg, (t0, r) in enumerate(SG):
                p = open_tile("v2", sg)
                for kc in range(KC):
                    last = mm(p[0:r, 0:D], hn[:, kc, t0:t0 + r], dora_w[1][:, kc, :],
                              start=(kc == 0), stop=(kc == KC - 1))
                last.then_inc(tiles_filled, 1)
            pe.wait_ge(act_evac, evacuated("k2", 1, KC - 1))
            for part in range(2):
                rows2, groups2 = (128, range(4)) if part == 0 else (96, range(4, 5))
                n = 128 * len(groups2)
                for j in range(4):
                    p = open_tile("score2", j, part)
                    mm(p[0:rows2, 0:n], constb("ident")[0:rows2, 0:rows2], constb("same_pos")[0:rows2, 0:n],
                       start=True, stop=True)
                    for sg in groups2:
                        for qd in range(SG[sg][1] // 32):
                            t0 = SG[sg][0] + 32 * qd
                            for x in range(4):
                                k = kodd if x % 2 else keven
                                o = 128 * (sg % 4) + 32 * x
                                last = mm(p[32 * qd:32 * qd + 32, o:o + 32],
                                          q2[32 * j:32 * j + 32, x // 2, t0:t0 + 32],
                                          k[32 * j:32 * j + 32, x // 2, t0:t0 + 32],
                                          start=False, stop=True, skip_group_check=True)
                    last.then_inc(tiles_filled, 1)
            pe.wait_ge(dve_evac, evacuated("v2", 4))
            for sg in range(5):
                part = sg // 4
                pe.wait_ge(prob2t_done, 4 * part + 4)
                for qd in range(SG[sg][1] // 32):
                    p = open_tile("pv2", sg, qd)
                    rows2 = slice(32 * qd, 32 * qd + 32)
                    for hd in range(H2):
                        j, x = hd % 8 // 2, 2 * (hd // 8) + hd % 2
                        o = 128 * (sg % 4) + 32 * x
                        last = mm(p[rows2, hd * 17:hd * 17 + 17], prob2t[part][j][rows2, o:o + 32],
                                  v2[rows2, sg, hd, :], start=True, stop=True)
                    last.then_inc(tiles_filled, 1)
            for sg, (t0, r) in enumerate(SG):
                pe.wait_ge(dve_evac, evacuated("pv2", sg, r // 32 - 1))
                p = open_tile("o2t", sg)
                for kc in range(KC):
                    last = nc.tensor.transpose(p[:, kc * r:(kc + 1) * r], o2[0:r, sg, kc * 128:(kc + 1) * 128],
                                               ident[0:r, 0:r])
                last.then_inc(tiles_filled, 1)
            pe.wait_ge(loaded["out2"], 16)
            pe.wait_ge(act_evac, evacuated("o2t", 4))
            for hf in range(2):
                for mc in range(KC):
                    project(("out2", hf, mc), wout2[:, :, mc * 128:(mc + 1) * 128],
                            o2t[:, :, hf * HT:(hf + 1) * HT])
            norm(3)

            pe.wait_ge(loaded["choice"], 16)
            for hf in range(2):
                pe.wait_ge(normed, 6 + hf + 1)
                p = open_tile("route", hf)
                for g in range(3):
                    t0, n = chunk_tokens(g, hf)
                    for kc in range(KC):
                        last = mm(p[0:n, g * E3:(g + 1) * E3], hn[:, kc, t0:t0 + n], choice3[:, kc, :],
                                  start=(kc == 0), stop=(kc == KC - 1))
                last.then_inc(tiles_filled, 1)
            p = open_tile("probs_t")
            for g in range(6):
                r = GROUPS[g % 3][1]
                pe.wait_ge(spread_done, g + 1)
                last = mm(p[:, 0:S], pspread[g % 2][0:r, :], const("pos_of")[0:r, :], start=(g == 0), stop=(g == 5))
                last.then_inc(tiles_filled if g == 5 else spread_used, 1)
            for b2 in range(8):
                p = open_tile("x_tok", b2)
                for i in range(2):
                    for kc in range(KC):
                        b = 2 * b2 + i
                        last = nc.tensor.transpose(p[0:S, i * D + kc * 128:i * D + (kc + 1) * 128],
                                                   hn[:, kc, b * S:(b + 1) * S], ident)
                last.then_inc(tiles_filled, 1)
            pe.wait_ge(rank_done, 1)
            p = open_tile("rank_t")
            for i in range(2):
                last = nc.tensor.transpose(p[0:S, i * 128:(i + 1) * 128], pt[:, i * S:(i + 1) * S], ident)
            last.then_inc(tiles_filled, 1)
            pe.wait_ge(pick_done, 1)
            pe.wait_ge(act_evac, evacuated("x_tok", 7))
            for kc in range(KC):
                for b4 in range(4):
                    p = open_tile("gather", kc, b4)
                    for i in range(4):
                        b = 4 * b4 + i
                        last = mm(p[:, i * 72:(i + 1) * 72], x_tok[0:S, b, kc * 128:(kc + 1) * 128],
                                  pick[0:S, b * 72:(b + 1) * 72], start=True, stop=True)
                    last.then_inc(tiles_filled, 1)
            pe.wait_ge(pickw_done, 1)
            for hf in range(2):
                p = open_tile("scatter_t", hf)
                for i in range(HB):
                    b = HB * hf + i
                    last = nc.tensor.transpose(p[0:72, i * S:(i + 1) * S], pickw[0:S, b * 72:(b + 1) * 72],
                                               ident[0:S, 0:S])
                last.then_inc(tiles_filled, 1)
            pe.wait_ge(loaded["w1"], 16)
            pe.wait_ge(loaded["w2"], 16)
            pe.wait_ge(dve_evac, evacuated("gather", KC - 1, 3))
            n = B * CAP
            for e in range(E3 + 1):
                if e < E3:
                    for f2 in range(2):
                        p = open_tile("hid", e, f2)
                        for i in range(2):
                            f = 2 * f2 + i
                            for kc in range(KC):
                                last = mm(p[:, i * n:(i + 1) * n], w1[:, kc, e, f * 128:(f + 1) * 128],
                                          x_in[:, kc, e, :, :].rearrange("p b c -> p (b c)"),
                                          start=(kc == 0), stop=(kc == KC - 1))
                        last.then_inc(tiles_filled, 1)
                if e >= 1:
                    pe.wait_ge(act_evac, evacuated("hid", e - 1, 1))
                    p = open_tile("y", e - 1)
                    for mc in range(KC):
                        for f in range(4):
                            last = mm(p[:, mc * n:(mc + 1) * n], w2[:, e - 1, f, mc * 128:(mc + 1) * 128],
                                      hid[(e - 1) % 2][:, f, :], start=(f == 0), stop=(f == 3))
                    last.then_inc(tiles_filled, 1)
            pe.wait_ge(dve_evac, evacuated("y", E3 - 1))
            for b2 in range(8):
                p = open_tile("y_tok", b2)
                for i in range(2):
                    for kc in range(KC):
                        b = 2 * b2 + i
                        last = nc.tensor.transpose(p[0:72, i * D + kc * 128:i * D + (kc + 1) * 128],
                                                   y_t[:, kc, b, :, :].rearrange("p e c -> p (e c)"), ident)
                last.then_inc(tiles_filled, 1)
            pe.wait_ge(act_evac, evacuated("scatter_t", 1))
            for hf in range(2):
                pe.wait_ge(act_evac, evacuated("y_tok", 4 * hf + 3))
                for mc in range(KC):
                    p = open_tile("res3", hf, mc)
                    for i in range(HB):
                        b = HB * hf + i
                        last = mm(p[:, i * S:(i + 1) * S], y_tok[0:72, b, mc * 128:(mc + 1) * 128],
                                  scatter_t[0:72, b * S:(b + 1) * S], start=True, stop=True)
                    last.then_inc(tiles_filled, 1)

        @block.scalar
        def _(act):
            stepped = [0]
            A = nc.scalar.activation

            def load(name, dst):
                act.dma_start(dst, io[name]).then_inc(loaded[name], 16)

            load("vec", vec[:, :])
            load("pos", tokadd[:, :, 1:S])
            load("cst", cst[:, :])
            load("rows", rows[:, :])
            load("csb", csb_bits[:, :])
            load("lora", lora)
            load("dora0", dora_w[0])
            load("dora1", dora_w[1])

            def norm(n):
                act.wait_ge(consts_set, 1)
                for hf in range(2):
                    act.wait_ge(dve_evac, evacuated("mean", n, hf))
                    if n:
                        act.wait_ge(tiles_filled, filled("var", n - 1, hf))
                    A(sq[:, hf], hc[:, hf], ACT.Square).then_inc(squared, 1)
                for hf in range(2):
                    act.wait_ge(tiles_filled, filled("var", n, hf))
                    p = bank("var", n, hf)
                    if n:
                        act.wait_ge(normed, 2 * (n - 1) + hf + 1)
                    A(std[:, hf], p[:, 0:HT], ACT.Sqrt, bias=eps_col[:, 0:1]).then_inc(act_evac, 1)

            norm(0)
            act.wait_ge(dve_evac, evacuated("dora", 1, 1))
            for w in range(2):
                for kc in range(KC):
                    A(junk[:, :], dora_w[w][:, kc, :], ACT.Square,
                      accum_out=fro[:, 2 * w + kc:2 * w + kc + 1]).then_inc(dora_sq, 1)
                    act.wait_ge(dora_sq, 2 * w + kc + 1)
            act.wait_ge(fro_done, 1)
            A(fro[:, 6:8], fro[:, 4:6], ACT.Sqrt).then_inc(dora_sq, 1)

            def project0(hf):
                act.wait_ge(la_abs_done, hf + 1)
                for r, a, b in segments(16):
                    last = A(la_exp[0:r, a:b], la_abs[0:r, a:b], ACT.Exp, scale=-1.0)
                last.then_inc(act_step, 1)
                stepped[0] += 1
                act.wait_ge(act_step, stepped[0])
                for r, a, b in segments(16):
                    last = A(la_ln[0:r, a:b], la_exp[0:r, a:b], ACT.Ln, bias=one_col[0:r, 0:1])
                last.then_inc(la_ln_done, 1)
                for c in range(C0):
                    for name, dst in (("q0", q0), ("k0", k0)):
                        act.wait_ge(tiles_filled, filled(name, hf, c))
                        p = bank(name, hf, c)
                        A(dst[:, c, :], p[:, 0:HT], ACT.Silu).then_inc(act_evac, 1)

            def attend0(hf):
                for n in range(7):
                    if n < 6:
                        r = GROUPS[n // 2][1]
                        for par in range(2):
                            m = 2 * n + par
                            if m >= 3:
                                act.wait_ge(dve_evac, evacuated("score0", hf, (m - 3) // 2, (m - 3) % 2))
                            elif hf:
                                act.wait_ge(dve_evac, evacuated("score0", 0, (m + 9) // 2, (m + 9) % 2))
                            act.wait_ge(tiles_filled, filled("decay", hf, n, par))
                            p = bank("decay", hf, n, par)
                            A(decay[m % 3][0:r, 0:4 * r], p[0:r, 0:4 * r], ACT.Exp).then_inc(act_evac, 1)
                    if n >= 1:
                        g, upper = (n - 1) // 2, (n - 1) % 2
                        off, r = GROUPS[g]
                        if hf:
                            act.wait_ge(tiles_filled, filled("wo", 0, KC - 1))
                        act.wait_ge(tiles_filled, filled("pv0", hf, n - 1))
                        p = bank("pv0", hf, n - 1)
                        A(osb[:, 4 * upper:4 * upper + 4, off:off + r],
                          p[:, 0:4 * r].rearrange("p (c i) -> p c i", c=4), ACT.Copy).then_inc(act_evac, 1)
                for c in range(C0):
                    act.wait_ge(tiles_filled, filled("g0", hf, c))
                    p = bank("g0", hf, c)
                    A(g0[:, c, :], p[:, 0:HT], ACT.Sigmoid).then_inc(act_evac, 1)
                for i in range(2):
                    act.wait_ge(act_evac, evacuated("pv0", hf, 5))
                    if hf or i:
                        act.wait_ge(gsq_read, 2 * hf + i)
                    A(gsq, osb[:, 4 * i:4 * i + 4, :], ACT.Square).then_inc(gsq_done, 1)

            def close0(hf):
                act.wait_ge(gvar_done, hf + 1)
                A(gstd, gvar, ACT.Sqrt, bias=eps_col[:, 0:1]).then_inc(gstd_done, 1)

            project0(0)
            attend0(0)
            project0(1)
            close0(0)
            attend0(1)
            close0(1)
            norm(1)
            for hf in range(2):
                for c in range(C1):
                    for name, dst in (("q1", q1), ("k1", k1)):
                        act.wait_ge(tiles_filled, filled(name, hf, c))
                        p = bank(name, hf, c)
                        A(dst[:, c, :], p[:, 0:HT], ACT.Copy).then_inc(act_evac, 1)
                if hf:
                    act.wait_ge(onehot_done, hf)
                act.wait_ge(tiles_filled, filled("gate1", hf))
                p = bank("gate1", hf)
                segs = segments(64)
                for i, (r, a, b) in enumerate(segs):
                    last = A(gate[0:r, a:b, :], p[0:r, a * 64:b * 64].rearrange("p (g n) -> p g n", n=64), ACT.Sigmoid)
                last.then_inc(act_evac, 1)
                for g in range(3):
                    r = GROUPS[g][1]
                    for par in range(2):
                        act.wait_ge(dve_evac, evacuated("score1", hf, g, par))
                        A(prob1[2 * g + par][0:r, 0:4 * r], prob1[2 * g + par][0:r, 0:4 * r], ACT.Exp,
                          scale=64 ** -0.5).then_inc(exp1_done, 1)
                if hf:
                    act.wait_ge(tiles_filled, filled("sel", 0, E0 * C1 - 1))
                    act.wait_ge(dve_evac, evacuated("sel", 0, E0 * C1 - 1))
                act.wait_ge(tiles_filled, filled("onehot_t", hf))
                p = bank("onehot_t", hf)
                A(onehot_t[0:64, 0:HT], p[0:64, 0:HT], ACT.Copy).then_inc(act_evac, 1)

                def pv1(g):
                    off, r = GROUPS[g]
                    act.wait_ge(tiles_filled, filled("pv1", hf, g))
                    p = bank("pv1", hf, g)
                    A(gout[:, :, off:off + r], p[:, 0:4 * r].rearrange("p (c i) -> p c i", c=C1),
                      ACT.Copy).then_inc(act_evac, 1)

                for g in range(3):
                    r = GROUPS[g][1]
                    if hf:
                        act.wait_ge(tiles_filled, filled("pv1", 0, g))
                    act.wait_ge(tiles_filled, filled("val", hf, g, 0))
                    p = bank("val", hf, g, 0)
                    A(vals[0:r, g, :], p[0:r, :], ACT.Copy).then_inc(act_evac, 1)
                    if g >= 1:
                        pv1(g - 1)
                    for par in range(2):
                        act.wait_ge(tiles_filled, filled("pt1", hf, g, par))
                        p = bank("pt1", hf, g, par)
                        A(prob1t[(2 * g + par) % 4][0:r, 0:4 * r], p[0:r, 0:4 * r], ACT.Copy).then_inc(act_evac, 1)
                pv1(2)
            norm(2)
            act.wait_ge(dora_done, 1)
            for hf in range(2):
                t0 = hf * HT
                for mc in range(KC):
                    act.wait_ge(tiles_filled, filled("q2", hf, mc))
                    p = bank("q2", hf, mc)
                    A(q2[:, mc, t0:t0 + HT], p[:, 0:HT], ACT.Identity, bias=col("bias_q", mc),
                      scale=fro[:, 8:9]).then_inc(act_evac, 1)
                    act.wait_ge(tiles_filled, filled("k2", hf, mc))
                    p = bank("k2", hf, mc)
                    A(keven[:, mc, t0:t0 + HT], p[:, 0:HT], ACT.Identity, bias=kb_even_odd[:, 0, mc:mc + 1],
                      scale=col("even"))
                    A(kodd[:, mc, t0:t0 + HT], p[:, 0:HT], ACT.Identity, bias=kb_even_odd[:, 1, mc:mc + 1],
                      scale=col("odd")).then_inc(act_evac, 1)
            for part in range(2):
                rows2, n = (128, 512) if part == 0 else (96, 128)
                for j in range(4):
                    act.wait_ge(dve_evac, evacuated("score2", j, part))
                    pr = prob2[part][j][0:rows2, 0:n]
                    A(pr, pr, ACT.Exp, scale=HD2 ** -0.5).then_inc(exp2_done, 1)
            for sg, (t0, r) in enumerate(SG):
                act.wait_ge(tiles_filled, filled("o2t", sg))
                p = bank("o2t", sg)
                A(o2t[:, :, t0:t0 + r], p[:, 0:2 * r].rearrange("p (k i) -> p k i", k=KC),
                  ACT.Copy).then_inc(act_evac, 1)
            norm(3)
            for hf in range(2):
                act.wait_ge(shifted3, hf + 1)
                for r, a, b in segments(8):
                    last = A(pwork[0:r, 3 * hf + a:3 * hf + b, :], pwork[0:r, 3 * hf + a:3 * hf + b, :], ACT.Exp)
                last.then_inc(exp3_done, 1)
            for b2 in range(8):
                act.wait_ge(tiles_filled, filled("x_tok", b2))
                p = bank("x_tok", b2)
                A(x_tok[0:S, 2 * b2:2 * b2 + 2, :], p[0:S, :].rearrange("p (b n) -> p b n", b=2),
                  ACT.Copy).then_inc(act_evac, 1)
            for hf in range(2):
                act.wait_ge(tiles_filled, filled("scatter_t", hf))
                p = bank("scatter_t", hf)
                A(scatter_t[0:72, hf * HT:(hf + 1) * HT], p[0:72, 0:HT], ACT.Copy).then_inc(act_evac, 1)
            for e in range(E3):
                for f2 in range(2):
                    if e >= 2:
                        act.wait_ge(tiles_filled, filled("y", e - 2))
                    act.wait_ge(tiles_filled, filled("hid", e, f2))
                    p = bank("hid", e, f2)
                    A(hid[e % 2][:, 2 * f2:2 * f2 + 2, :],
                      p[:, 0:2 * B * CAP].rearrange("p (f n) -> p f n", f=2), ACT.Silu).then_inc(act_evac, 1)
            for b2 in range(8):
                act.wait_ge(tiles_filled, filled("y_tok", b2))
                p = bank("y_tok", b2)
                A(y_tok[0:72, 2 * b2:2 * b2 + 2, :], p[0:72, :].rearrange("p (b n) -> p b n", b=2),
                  ACT.Copy).then_inc(act_evac, 1)

        @block.vector
        def _(dve):
            V = nc.vector
            stepped = [0]

            def settle(ins):
                ins.then_inc(dve_step, 1)
                stepped[0] += 1
                dve.wait_ge(dve_step, stepped[0])

            def norm(n, position_major=False):
                for hf in range(2):
                    dve.wait_ge(tiles_filled, filled("mean", n, hf))
                    p = bank("mean", n, hf)
                    if n:
                        dve.wait_ge(normed, 2 * (n - 1) + hf + 1)
                        dve.wait_ge(squared, 2 * (n - 1) + hf + 1)
                    V.tensor_tensor(hc[:, hf], h[:, :, hf * HT:(hf + 1) * HT],
                                    p[:, 0:HT].unsqueeze(1).to_broadcast([128, KC, HT]),
                                    ALU.subtract).then_inc(dve_evac, 1)
                for hf in range(2):
                    dve.wait_ge(act_evac, evacuated("var", n, hf))
                    if n or hf:
                        dve.wait_ge(normed, 2 * n + hf)
                    settle(V.reciprocal(rstd[:, :], std[:, hf]))
                    dve.wait_ge(dve_evac, evacuated("mean", n, hf))
                    if position_major:
                        for kc in range(KC):
                            o = hn[:, kc, :].rearrange("p (s b) -> p b s", b=B)[:, hf * HB:(hf + 1) * HB, :]
                            last = V.tensor_tensor(o, images(hc[:, hf, kc]), images(rstd[:, :]), ALU.mult)
                    else:
                        last = V.tensor_tensor(hn[:, :, hf * HT:(hf + 1) * HT], hc[:, hf],
                                               rstd[:, :].unsqueeze(1).to_broadcast([128, KC, HT]), ALU.mult)
                    last.then_inc(normed, 1)

            dve.wait_ge(loaded["vec"], 16)
            dve.wait_ge(loaded["pos"], 16)
            V.tensor_copy(tokadd[:, :, 0:1], cols("cls").unsqueeze(2))
            V.tensor_tensor(tokadd[:, :, 1:2], tokadd[:, :, 1:2], cols("class_tok").unsqueeze(2), ALU.add)
            for kc in range(KC):
                last = V.tensor_scalar(tokadd[:, kc, 2:S], tokadd[:, kc, 2:S], col("b_lin", kc), None, ALU.add)
            settle(last)
            for kc in range(KC):
                last = V.tensor_copy(h[:, kc, :].rearrange("p (b s) -> p b s", s=S)[:, :, 0:2],
                                     tokadd[:, kc, 0:2].unsqueeze(1).to_broadcast([128, B, 2]))
            last.then_inc(tok_added, 1)
            dve.wait_ge(tok_added, 1)
            for hf in range(2):
                for mc in range(KC):
                    dve.wait_ge(tiles_filled, filled("tok", hf, mc))
                    p = bank("tok", hf, mc)
                    o = h[:, mc, :].rearrange("p (b s) -> p b s", s=S)[:, hf * HB:(hf + 1) * HB, 2:S]
                    V.tensor_tensor(o, p[:, 0:HB * NP].rearrange("p (b s) -> p b s", s=NP),
                                    tokadd[:, mc, 2:S].unsqueeze(1).to_broadcast([128, HB, NP]),
                                    ALU.add).then_inc(dve_evac, 1)
            dve.wait_ge(dve_evac, evacuated("tok", 1, KC - 1))
            norm(0)
            for w in range(2):
                dve.wait_ge(loaded[f"dora{w}"], 16)
                for kc in range(KC):
                    dve.wait_ge(tiles_filled, filled("dora", w, kc))
                    p = bank("dora", w, kc)
                    V.tensor_tensor(dora_w[w][:, kc, :], dora_w[w][:, kc, :], p[:, 0:D], ALU.add).then_inc(dve_evac, 1)
            dve.wait_ge(tiles_filled, filled("fro"))
            p = bank("fro")
            V.tensor_copy(fro[:, 10:14], p[:, 0:4]).then_inc(dve_evac, 1)
            dve.wait_ge(dve_evac, evacuated("fro"))
            f2 = fro[:, 10:14].rearrange("p (w k) -> p w k", w=2)
            V.tensor_tensor(fro[:, 4:6], f2[:, :, 0], f2[:, :, 1], ALU.add).then_inc(fro_done, 1)
            V.tensor_scalar(kb_even_odd[:, 0, :], cols("k_b"), col("even"), None, ALU.mult)
            V.tensor_scalar(kb_even_odd[:, 1, :], cols("k_b"), col("odd"), None, ALU.mult)
            dve.wait_ge(dora_sq, 5)
            settle(V.tensor_scalar(fro[:, 6:8], fro[:, 6:8], 1e-8, None, ALU.add))
            settle(V.reciprocal(fro[:, 6:8], fro[:, 6:8]))
            mags = vec[:, VEC["mag_q"][0]:VEC["mag_q"][0] + 2]
            V.tensor_tensor(fro[:, 8:10], fro[:, 6:8], mags, ALU.mult).then_inc(dora_done, 1)

            def project0(hf):
                dve.wait_ge(loaded["rows"], 16)
                if hf:
                    dve.wait_ge(steps_done, 6 * hf)
                dve.wait_ge(tiles_filled, filled("la", hf))
                p = bank("la", hf)
                for r, a, b in segments(16):
                    last = V.tensor_tensor(la[0:r, a:b, :], p[0:r, a * 16:b * 16].rearrange("p (g n) -> p g n", n=16),
                                           rows[0:r, 0:16].unsqueeze(1).to_broadcast([r, b - a, 16]), ALU.add)
                last.then_inc(dve_evac, 1)
                dve.wait_ge(dve_evac, evacuated("la", hf))
                for r, a, b in segments(16):
                    last = V.scalar_tensor_tensor(la_abs[0:r, a:b, :], la[0:r, a:b, :], -1.0, la[0:r, a:b, :],
                                                  ALU.mult, ALU.max)
                last.then_inc(la_abs_done, 1)
                dve.wait_ge(la_ln_done, hf + 1)
                for r, a, b in segments(16):
                    last = V.scalar_tensor_tensor(la[0:r, a:b, :], la[0:r, a:b, :], 0.0, la_ln[0:r, a:b, :],
                                                  ALU.max, ALU.add)
                last.then_inc(la_done, 1)
                for g in range(3):
                    r = GROUPS[g][1]
                    for half in range(2):
                        dve.wait_ge(tiles_filled, filled("v0", hf, g, half))
                        p = bank("v0", hf, g, half)
                        V.tensor_copy(v0[0:r, g, half * 512:(half + 1) * 512], p[0:r, :]).then_inc(dve_evac, 1)

            def attend0(hf):
                for n in range(6):
                    r = GROUPS[n // 2][1]
                    for par in range(2):
                        m = 2 * n + par
                        dve.wait_ge(act_evac, evacuated("decay", hf, n, par))
                        if n >= 2:
                            dve.wait_ge(tiles_filled, filled("pv0", hf, n - 2))
                        dve.wait_ge(tiles_filled, filled("score0", hf, n, par))
                        p = bank("score0", hf, n, par)
                        V.tensor_tensor(att[m % 4][0:r, 0:4 * r], p[0:r, 0:4 * r], decay[m % 3][0:r, 0:4 * r],
                                        ALU.mult).then_inc(dve_evac, 1)
                dve.wait_ge(act_evac, evacuated("pv0", hf, 5))
                if hf:
                    dve.wait_ge(dve_evac, evacuated("gn", 0))
                o4 = osb.rearrange("p c (b s) -> p (c b) s", s=S)
                V.tensor_reduce(gsum[:, 0:64], o4, AXX, ALU.add)
                for i in range(2):
                    dve.wait_ge(gsq_done, 2 * hf + i + 1)
                    V.tensor_reduce(gsum[:, 64 + 32 * i:96 + 32 * i], gsq.rearrange("p (c s) -> p c s", s=S),
                                    AXX, ALU.add).then_inc(gsq_read, 1)

            def close0(hf):
                dve.wait_ge(tiles_filled, filled("gn", hf))
                p = bank("gn", hf)
                V.tensor_copy(gmean, p[:, 0:128]).then_inc(dve_evac, 1)
                dve.wait_ge(dve_evac, evacuated("gn", hf))
                settle(V.tensor_tensor(gvar, gmean[:, 0:64], gmean[:, 0:64], ALU.mult))
                settle(V.tensor_tensor(gvar, gmean[:, 64:128], gvar, ALU.subtract))
                V.tensor_scalar(gvar, gvar, 0.0, None, ALU.max).then_inc(gvar_done, 1)
                dve.wait_ge(gstd_done, hf + 1)
                settle(V.reciprocal(gstd, gstd))
                by_chunk = lambda a: a.rearrange("p (c b) -> p c b", c=C0)
                wide = lambda name: cols(name).unsqueeze(2).to_broadcast([128, C0, HB])
                settle(V.tensor_tensor(by_chunk(gscale), by_chunk(gstd), wide("gn_w"), ALU.mult))
                settle(V.tensor_tensor(gshift, gmean[:, 0:64], gscale, ALU.mult))
                settle(V.tensor_tensor(by_chunk(gshift), wide("gn_b"), by_chunk(gshift), ALU.subtract))
                for i in range(2):
                    o = osb[:, 4 * i:4 * i + 4, :].rearrange("p c (b s) -> p (c b) s", s=S)
                    V.tensor_tensor(o, o, gscale[:, 32 * i:32 * i + 32].unsqueeze(2).to_broadcast([128, 32, S]),
                                    ALU.mult).then_inc(gn_scaled, 1)
                for i in range(2):
                    dve.wait_ge(act_evac, evacuated("g0", hf, C0 - 1))
                    dve.wait_ge(gn_shifted, 2 * hf + i + 1)
                    o = osb[:, 4 * i:4 * i + 4, :]
                    V.tensor_tensor(o, o, g0[:, 4 * i:4 * i + 4, :], ALU.mult).then_inc(gn_gated, 1)
                for mc in range(KC):
                    dve.wait_ge(tiles_filled, filled("wo", hf, mc))
                    p = bank("wo", hf, mc)
                    hh = h[:, mc, hf * HT:(hf + 1) * HT]
                    V.tensor_tensor(hh, hh, p[:, 0:HT], ALU.add).then_inc(dve_evac, 1)

            project0(0)
            attend0(0)
            project0(1)
            close0(0)
            attend0(1)
            close0(1)
            dve.wait_ge(dve_evac, evacuated("wo", 1, KC - 1))
            norm(1)

            for hf in range(2):
                def score1(g):
                    r = GROUPS[g][1]
                    for par in range(2):
                        i = 2 * g + par
                        dve.wait_ge(tiles_filled, filled("score1", hf, g, par))
                        p = bank("score1", hf, g, par)
                        p3 = p[0:r, 0:4 * r].rearrange("p (x j) -> p x j", x=4)
                        nm = negmax1[0:r, 4 * i:4 * i + 4]
                        settle(V.tensor_reduce(nm, p3, AXX, ALU.max, negate=True))
                        if hf:
                            dve.wait_ge(tiles_filled, filled("pt1", 0, g, par))
                        V.tensor_tensor(prob1[i][0:r, 0:4 * r].rearrange("p (x j) -> p x j", x=4), p3,
                                        nm.unsqueeze(2).to_broadcast([r, 4, r]), ALU.add).then_inc(dve_evac, 1)

                def choose():
                    dve.wait_ge(act_evac, evacuated("gate1", hf))
                    if hf:
                        dve.wait_ge(tiles_filled, filled("onehot_t", 0))
                        dve.wait_ge(vals_done, 3)
                    for r, a, b in segments(64):
                        n = b - a
                        eight = lambda t: t[0:r, a:b, :].rearrange("p g (h e) -> p (g h) e", e=E0)
                        flat = lambda t: t[0:r, a:b, :].rearrange("p g n -> p (g n)")
                        settle(V.tensor_reduce(flat(gmax), eight(gate), AXX, ALU.max))
                        settle(V.tensor_tensor(eight(ohwork), eight(gate),
                                               flat(gmax).unsqueeze(2).to_broadcast([r, 8 * n, E0]), ALU.is_equal))
                        settle(V.tensor_tensor(eight(ohwork), eight(ohwork),
                                               const("desc")[0:r, :].unsqueeze(1).to_broadcast([r, 8 * n, E0]), ALU.mult))
                        settle(V.tensor_reduce(flat(ohmax), eight(ohwork), AXX, ALU.max))
                        last = V.tensor_tensor(eight(onehot), eight(ohwork),
                                               flat(ohmax).unsqueeze(2).to_broadcast([r, 8 * n, E0]), ALU.is_equal)
                    last.then_inc(onehot_done, 1)

                choose()
                score1(0)
                score1(1)
                score1(2)
                dve.wait_ge(onehot_done, hf + 1)
                for g in range(3):
                    r = GROUPS[g][1]
                    for par in range(2):
                        i = 2 * g + par
                        dve.wait_ge(exp1_done, 6 * hf + i + 1)
                        sm = sum1[0:r, 4 * i:4 * i + 4]
                        settle(V.tensor_reduce(sm, prob1[i][0:r, 0:4 * r].rearrange("p (x j) -> p x j", x=4),
                                               AXX, ALU.add))
                        settle(V.reciprocal(sm, sm))
                        V.tensor_tensor(sm, sm, gmax[0:r, g, par::2], ALU.mult).then_inc(scale1_done, 1)
                for g in range(3):
                    r = GROUPS[g][1]
                    for e in range(1, E0):
                        dve.wait_ge(tiles_filled, filled("val", hf, g, e))
                        p = bank("val", hf, g, e)
                        dve.wait_ge(act_evac if e == 1 else dve_evac, evacuated("val", hf, g, e - 1))
                        eight = lambda t: t.rearrange("p (h k) -> p h k", h=H1)
                        mask = onehot[0:r, g, e::E0].bitcast(I32).unsqueeze(2).to_broadcast([r, H1, 64])
                        V.copy_predicated(eight(vals[0:r, g, :]), mask, eight(p[0:r, :])).then_inc(dve_evac, 1)
                dve.wait_ge(act_evac, evacuated("pv1", hf, 2))
                for i in range(E0 * C1):
                    if i >= 4:
                        dve.wait_ge(gated_used, 31 * hf + i - 3)
                    elif hf:
                        dve.wait_ge(experts_done, 1)
                    dve.wait_ge(tiles_filled, filled("sel", hf, i))
                    p = bank("sel", hf, i)
                    V.tensor_tensor(gated[i % 4], gout[:, i % C1, :], p[:, 0:HT], ALU.mult).then_inc(dve_evac, 1)
                dve.wait_ge(experts_done, hf + 1)
                for mc in range(KC):
                    hh = h[:, mc, hf * HT:(hf + 1) * HT]
                    last = V.tensor_tensor(hh, hh, acc[mc][:, 0:HT], ALU.add)
                last.then_inc(experts_added, 1)
            dve.wait_ge(experts_added, 2)
            norm(2, position_major=True)
            dve.wait_ge(dora_done, 1)
            dve.wait_ge(tiles_filled, filled("q2", 0, 0))
            V.memset(v2[:, :, :, 16:17], 1.0)
            for sg, (t0, r) in enumerate(SG):
                dve.wait_ge(tiles_filled, filled("v2", sg))
                p = bank("v2", sg)
                V.scalar_tensor_tensor(v2[0:r, sg, :, 0:16], p[0:r, 0:D].rearrange("p (h n) -> p h n", h=H2),
                                       fro[0:r, 9:10], rows[0:r, 16:16 + D].rearrange("p (h n) -> p h n", h=H2),
                                       ALU.mult, ALU.add).then_inc(dve_evac, 1)

            for part in range(2):
                rows2, n = (128, 512) if part == 0 else (96, 128)
                for j in range(4):
                    dve.wait_ge(tiles_filled, filled("score2", j, part))
                    p = bank("score2", j, part)
                    p3 = p[0:rows2, 0:n].rearrange("p (x j) -> p x j", j=32)
                    nm = negmax2[0:rows2, 16 * j + 64 * part:16 * j + 64 * part + n // 32]
                    settle(V.tensor_reduce(nm, p3, AXX, ALU.max, negate=True))
                    V.tensor_tensor(prob2[part][j][0:rows2, 0:n].rearrange("p (x j) -> p x j", j=32), p3,
                                    nm.unsqueeze(2).to_broadcast([rows2, n // 32, 32]), ALU.add).then_inc(dve_evac, 1)
                for j in range(4):
                    dve.wait_ge(exp2_done, 4 * part + j + 1)
                    V.transpose(prob2t[part][j][0:rows2, 0:n], prob2[part][j][0:rows2, 0:n]).then_inc(prob2t_done, 1)
            for sg in range(5):
                for qd in range(SG[sg][1] // 32):
                    dve.wait_ge(tiles_filled, filled("pv2", sg, qd))
                    p = bank("pv2", sg, qd)
                    rows2 = slice(32 * qd, 32 * qd + 32)
                    p3 = p[rows2, 0:H2 * 17].rearrange("p (h n) -> p h n", n=17)
                    settle(V.reciprocal(rden2[rows2, sg, :], p3[:, :, 16]))
                    V.tensor_tensor(o2[rows2, sg, :].rearrange("p (h n) -> p h n", h=H2), p3[:, :, 0:16],
                                    rden2[rows2, sg, :].unsqueeze(2).to_broadcast([32, H2, 16]),
                                    ALU.mult).then_inc(dve_evac, 1)
            for hf in range(2):
                for mc in range(KC):
                    dve.wait_ge(tiles_filled, filled("out2", hf, mc))
                    p = bank("out2", hf, mc)
                    hh = h[:, mc, :].rearrange("p (b s) -> p s b", s=S)[:, 19 * hf:19 * hf + 19, :]
                    V.scalar_tensor_tensor(hh, p[:, 0:HT].rearrange("p (s b) -> p s b", b=B), col("out_b", mc), hh,
                                           ALU.add, ALU.add).then_inc(dve_evac, 1)
            dve.wait_ge(dve_evac, evacuated("out2", 1, KC - 1))
            norm(3)
            for hf in range(2):
                dve.wait_ge(tiles_filled, filled("route", hf))
                p = bank("route", hf)
                for r, a, b in segments(8):
                    n = b - a
                    last = V.tensor_copy(probs[0:r, 3 * hf + a:3 * hf + b, :],
                                         p[0:r, a * 8:b * 8].rearrange("p (g n) -> p g n", n=8))
                last.then_inc(dve_evac, 1)
                dve.wait_ge(dve_evac, evacuated("route", hf))
                for r, a, b in segments(8):
                    n = b - a
                    g = slice(3 * hf + a, 3 * hf + b)
                    settle(V.tensor_reduce(psum3[0:r, g, 0], probs[0:r, g, :], AXX, ALU.max))
                    last = V.tensor_tensor(pwork[0:r, g, :], probs[0:r, g, :],
                                           psum3[0:r, g, :].to_broadcast([r, n, 8]), ALU.subtract)
                last.then_inc(shifted3, 1)
            for hf in range(2):
                dve.wait_ge(exp3_done, hf + 1)
                for r, a, b in segments(8):
                    n = b - a
                    g = slice(3 * hf + a, 3 * hf + b)
                    settle(V.tensor_reduce(psum3[0:r, g, 0], pwork[0:r, g, :], AXX, ALU.add))
                    settle(V.reciprocal(psum3[0:r, g, :], psum3[0:r, g, :]))
                    last = V.tensor_tensor(probs[0:r, g, :], pwork[0:r, g, :],
                                           psum3[0:r, g, :].to_broadcast([r, n, 8]), ALU.mult)
                last.then_inc(probs_done, 1)
            dve.wait_ge(tiles_filled, filled("probs_t"))
            p = bank("probs_t")
            V.tensor_copy(pt[:, 0:S], p[:, 0:S]).then_inc(dve_evac, 1)
            dve.wait_ge(dve_evac, evacuated("probs_t"))
            mine = pt[:, 0:S].unsqueeze(2).to_broadcast([128, S, S])
            other = pt[:, 0:S].unsqueeze(1).to_broadcast([128, S, S])
            V.tensor_tensor(above, other, mine, ALU.is_gt)
            settle(V.tensor_tensor(equal, other, mine, ALU.is_equal))
            dve.wait_ge(loaded["before"], 16)
            settle(V.tensor_tensor(equal, equal, before, ALU.mult))
            settle(V.tensor_tensor(above, above, equal, ALU.add))
            V.tensor_reduce(pt[:, S:2 * S], above, AXX, ALU.add).then_inc(rank_done, 1)
            dve.wait_ge(tiles_filled, filled("rank_t"))
            p = bank("rank_t")
            V.tensor_copy(ptt[0:S, :], p[0:S, 0:256]).then_inc(dve_evac, 1)
            dve.wait_ge(dve_evac, evacuated("rank_t"))
            V.tensor_tensor(pick[0:S, :].rearrange("p (a c) -> p a c", c=CAP),
                            ptt[0:S, 128:256].unsqueeze(2).to_broadcast([S, 128, CAP]),
                            const("iota")[0:S, :].unsqueeze(1).to_broadcast([S, 128, CAP]),
                            ALU.is_equal).then_inc(pick_done, 1)
            for kc in range(KC):
                for b4 in range(4):
                    dve.wait_ge(tiles_filled, filled("gather", kc, b4))
                    p = bank("gather", kc, b4)
                    V.tensor_copy(x_in[:, kc, :, 4 * b4:4 * b4 + 4, :].rearrange("p e b c -> p b e c"),
                                  p[:, 0:288].rearrange("p (b e c) -> p b e c", b=4, e=E3)).then_inc(dve_evac, 1)
            for e in range(E3):
                dve.wait_ge(tiles_filled, filled("y", e))
                p = bank("y", e)
                V.tensor_copy(y_t[:, :, :, e, :], p[:, 0:2 * B * CAP].rearrange("p (k b c) -> p k b c", k=KC, b=B)
                              ).then_inc(dve_evac, 1)
            for hf in range(2):
                for mc in range(KC):
                    dve.wait_ge(tiles_filled, filled("res3", hf, mc))
                    p = bank("res3", hf, mc)
                    V.tensor_tensor(res[:, mc, hf * HT:(hf + 1) * HT], h[:, mc, hf * HT:(hf + 1) * HT], p[:, 0:HT],
                                    ALU.add).then_inc(dve_evac, 1)

        @block.gpsimd
        def _(pool):
            G = nc.gpsimd
            G.memset(eps_col[:, :], EPS)
            G.memset(one_col[:, :], 1.0).then_inc(consts_set, 1)
            pool.wait_ge(loaded["cst"], 16)

            def decay_steps(hf, n):
                g, upper = n // 2, n % 2
                r = GROUPS[g][1]
                pool.wait_ge(la_done, hf + 1)
                if n >= 2:
                    pool.wait_ge(tiles_filled, filled("decay", hf, n - 2, 1))
                elif hf:
                    pool.wait_ge(tiles_filled, filled("decay", 0, n + 4, 1))
                G.tensor_tensor(steps[n % 2][0:r, 0:8 * r].rearrange("p (h i) -> p h i", h=8),
                                la[0:r, g, 8 * upper:8 * upper + 8].unsqueeze(2).to_broadcast([r, 8, r]),
                                const("neg_upto")[0:r, 0:r].unsqueeze(1).to_broadcast([r, 8, r]),
                                ALU.mult).then_inc(steps_done, 1)

            def shift(hf):
                for i in range(2):
                    pool.wait_ge(gn_scaled, 2 * hf + i + 1)
                    o = osb[:, 4 * i:4 * i + 4, :].rearrange("p c (b s) -> p (c b) s", s=S)
                    G.tensor_tensor(o, o, gshift[:, 32 * i:32 * i + 32].unsqueeze(2).to_broadcast([128, 32, S]),
                                    ALU.add).then_inc(gn_shifted, 1)

            for n in range(6):
                decay_steps(0, n)
            decay_steps(1, 0)
            decay_steps(1, 1)
            shift(0)
            for n in range(2, 6):
                decay_steps(1, n)
            shift(1)
            for hf in range(2):
                for i in range(6):
                    r = GROUPS[i // 2][1]
                    pool.wait_ge(scale1_done, 6 * hf + i + 1)
                    p3 = prob1[i][0:r, 0:4 * r].rearrange("p (x j) -> p x j", x=4)
                    G.tensor_tensor(p3, p3, sum1[0:r, 4 * i:4 * i + 4].unsqueeze(2).to_broadcast([r, 4, r]),
                                    ALU.mult).then_inc(prob1_done, 1)
                for g in range(3):
                    r = GROUPS[g][1]
                    pool.wait_ge(dve_evac, evacuated("val", hf, g, E0 - 1))
                    v3 = vals[0:r, g, :].rearrange("p (h k) -> p h k", h=H1)
                    G.tensor_tensor(v3, v3, gmax[0:r, g, :].unsqueeze(2).to_broadcast([r, H1, 64]),
                                    ALU.mult).then_inc(vals_done, 1)
            for g in range(6):
                r = GROUPS[g % 3][1]
                pool.wait_ge(probs_done, g // 3 + 1)
                if g >= 2:
                    pool.wait_ge(spread_used, g - 1)
                G.tensor_tensor(pspread[g % 2][0:r, :].rearrange("p (b e) -> p b e", e=E3),
                                probs[0:r, g, :].unsqueeze(1).to_broadcast([r, B, E3]),
                                const("image_of")[0:r, g * B:(g + 1) * B].unsqueeze(2).to_broadcast([r, B, E3]),
                                ALU.mult).then_inc(spread_done, 1)
            pool.wait_ge(pick_done, 1)
            G.tensor_tensor(pickw[0:S, :].rearrange("p (a c) -> p a c", c=CAP),
                            pick[0:S, :].rearrange("p (a c) -> p a c", c=CAP),
                            ptt[0:S, 0:128].unsqueeze(2).to_broadcast([S, 128, CAP]), ALU.mult).then_inc(pickw_done, 1)


def constants():
    f = np.zeros((128, NCST), np.float32)
    b = np.zeros((128, NCSB), np.float32)

    def put(a, table, name, v):
        o, n = table[name]
        a[:v.shape[0], o:o + n] = v.reshape(v.shape[0], -1)

    i = np.arange(128)
    put(f, CST, "ident", np.eye(128))
    put(f, CST, "mean", np.full((128, 128), 1.0 / D))
    put(f, CST, "ones", np.ones((128, 128)))
    put(f, CST, "gn_block", (i[:, None] // 64 == i[None] // 64) / (64.0 * S))
    put(f, CST, "after", i[:, None] > i[None])
    put(f, CST, "neg_upto", -1.0 * (i[:, None] <= i[None]))
    t = np.arange(GMAX)
    put(f, CST, "pos_of", t[:, None] % S == np.arange(S)[None])
    first = [(hf * HT + off) // S for hf in range(2) for off, _ in GROUPS]
    put(f, CST, "image_of", np.stack([t[:, None] // S + b0 == np.arange(B)[None] for b0 in first], 1))
    put(f, CST, "iota", np.tile(np.arange(CAP), (128, 1)))
    put(f, CST, "desc", np.tile(E0 - np.arange(E0), (128, 1)))
    put(b, CSB, "ident", np.eye(128))
    for suffix, r in (("", GMAX), ("2", 76)):
        t = np.arange(r)
        seen = (t[:, None] // S == t[None] // S) & (t[:, None] >= t[None])
        put(b, CSB, "causal" + suffix, np.tile(np.where(seen, 0, -1e30), (1, 4)))
        put(b, CSB, "causal_t" + suffix, np.tile(np.where(seen.T, 0, -30000.0), (1, 4)))
    put(b, CSB, "same_pos", np.tile(np.where(i[:, None] % 32 // B == np.arange(32)[None] // B, 0, -1e30), (1, 16)))
    sel = np.zeros((H1, E0, E0, C1, 2, 64))
    for e in range(E0):
        for hd in range(H1):
            sel[hd, e, e, hd // 2, hd % 2, :] = 1
    put(b, CSB, "select", sel.reshape(64, -1))
    before = np.tile((np.arange(S)[None] < np.arange(S)[:, None]).reshape(1, -1), (128, 1)).astype(np.float32)
    bits = (b.view(np.uint32) >> 16).astype(np.uint16)
    return f, bits, before


def feat(a):
    return a.reshape(-1, 128, a.shape[-1]).transpose(1, 0, 2)


def lay_out(i):
    g = {k: np.asarray(v) for k, v in i.items()}
    f, b, before = constants()
    x = g["x"].reshape(B, 3, 6, 16, 6, 16).transpose(1, 3, 5, 0, 2, 4).reshape(768, B * NP)
    vec = np.zeros((128, NVEC), np.float32)

    def put(name, v):
        o, n = VEC[name]
        vec[:, o:o + n] = v

    def chunks(v):
        return v.reshape(-1, 128).T

    put("b_lin", chunks(g["L0_tok_b_lin"]))
    put("cls", chunks(g["cls_tok"]))
    put("class_tok", chunks(g["L0_tok_class_token"]))
    put("bias_q", chunks(g["L1_attn_bias_q"]))
    put("k_b", chunks(g["L1_attn_k_b"]))
    put("out_b", chunks(g["L1_attn_out_b"]))
    put("gn_w", chunks(g["L0_attn_gn_w"]))
    put("gn_b", chunks(g["L0_attn_gn_b"]))
    put("mag_q", g["L1_attn_mag_q"])
    put("mag_v", g["L1_attn_mag_v"])
    even = (np.arange(128) // HD2 % 2 == 0).astype(np.float32)[:, None]
    put("even", even)
    put("odd", 1 - even)
    rows = np.broadcast_to(np.concatenate([g["L0_attn_ba"], g["L1_attn_bias_v"]])[None], (128, 16 + D))
    lora = np.concatenate([g["L1_attn_A_q"], g["L1_attn_B_q"].T, g["L1_attn_A_v"], g["L1_attn_B_v"].T], 1)
    out = {
        "cst": f, "csb": b, "before": before, "vec": vec, "rows": rows, "lora": lora,
        "pos": feat(g["L0_tok_position_embeddings"][0].T),
        "patches": feat(x), "wlin": feat(g["L0_tok_W_lin"].T),
        "wa": feat(g["L0_attn_Wa"]), "wq": feat(g["L0_attn_Wq"]), "wk": feat(g["L0_attn_Wk"]),
        "wv": feat(g["L0_attn_Wv"]), "wg": feat(g["L0_attn_Wg"]), "wo": feat(g["L0_attn_Wo"]),
        "dora0": feat(g["L1_attn_dir_q"].T), "dora1": feat(g["L1_attn_dir_v"].T),
        "q1": feat(g["L0_ffn_w_q"]), "k1": feat(g["L0_ffn_w_k"]), "gate1": feat(g["L0_ffn_w_gate"]),
        "k2": feat(g["L1_attn_k_w"].T), "out2": feat(g["L1_attn_out_w"].T),
        "choice": feat(g["L1_ffn_choice_w"].T),
        "val": feat(g["L0_ffn_value_experts"].transpose(2, 0, 1, 3).reshape(D, -1)).reshape(128, KC, E0, 512),
        "oexp": g["L0_ffn_output_experts"].reshape(E0, C1, 128, D).transpose(2, 0, 1, 3),
        "w1": feat(g["L1_ffn_w1"].transpose(1, 0, 2).reshape(D, -1)).reshape(128, KC, E3, F3),
        "w2": g["L1_ffn_w2"].reshape(E3, 4, 128, D).transpose(2, 0, 1, 3),
    }
    return {k: np.ascontiguousarray(v) for k, v in out.items()}


def kernel(**inputs):
    import concourse.bacc as bacc
    from concourse.bass_utils import run_bass_kernel_spmd

    nc = bacc.Bacc("TRN2", target_bir_lowering=False, num_devices=1)
    arrays = lay_out(inputs)
    io = {n: nc.dram_tensor(f"in_{n}", a.shape, mybir.dt.from_np(a.dtype), kind="ExternalInput").ap()
          for n, a in arrays.items()}
    io["out"] = nc.dram_tensor("out_t", (D, T), F32, kind="ExternalOutput").ap()
    build(nc, io)
    r = run_bass_kernel_spmd(nc, [{f"in_{n}": a for n, a in arrays.items()}], core_ids=[0])
    return r.results[0]["out_t"].reshape(D, B, S).transpose(1, 2, 0)
```

```python
from contextlib import ExitStack

import numpy as np
import concourse.bass as bass
from concourse import mybir

F32 = mybir.dt.float32
F32R = mybir.dt.float32r
BF16 = mybir.dt.bfloat16
I32 = mybir.dt.int32
ALU = mybir.AluOpType
ACT = mybir.ActivationFunctionType
AXX = mybir.AxisListType.X

B, S, D = 16, 38, 256
T = B * S
HB, HT = B // 2, T // 2
NP = 36
KC = D // 128
FC0 = 6
GROUPS = ((0, 114), (114, 114), (228, 76))
GMAX = 114
H0, C0 = 16, 8
H1, E0, C1 = 8, 8, 4
H2, HD2 = 16, 16
SG = ((0, 128), (128, 128), (256, 128), (384, 128), (512, 96))
E3, F3, CAP = 8, 512, S * 2 // 8
GRP = ((0, 114), (114, 114), (304, 114), (418, 114), (228, 76), (532, 76))
RING = 4
RAW, SPLIT, PIECE = 3, 5, 1024
NX = 20300
NACT = 4 * T
EPS = 1e-5

VEC = dict(b_lin=(0, 2), cls=(2, 2), class_tok=(4, 2), bias_q=(6, 2), k_b=(8, 2), out_b=(10, 2),
           gn_w=(12, 8), gn_b=(20, 8), mag_q=(28, 1), mag_v=(29, 1), even=(30, 1), odd=(31, 1))
NVEC = 32
CST = dict(ident=(0, 128), mean=(128, 128), ones=(256, 128), gn_block=(384, 128), after=(512, 128),
           neg_upto=(640, 128), pos_of=(768, S), image_of=(806, 6 * B), iota=(902, CAP), desc=(911, E0),
           position=(919, S))
NCST = 957
CSB = dict(ident=(0, 128), causal_t=(128, 4 * GMAX), causal_t2=(584, 4 * 76), causal=(888, 4 * GMAX),
           causal2=(1344, 4 * 76), same_pos=(1648, 512), select=(2160, 4096))
NCSB = 6256


def segments(n_cols):
    return ((114, 0, 2), (76, 2, 3))


def psum_order():
    out = []
    add = lambda reader, *name: out.append((name, reader))
    halves = (0, 1)

    def norm(n):
        for hf in halves:
            add("dve", "mean", n, hf)
        for hf in halves:
            add("act", "var", n, hf)

    for hf in halves:
        for mc in range(KC):
            add("dve", "tok", hf, mc)
    norm(0)
    for w in range(2):
        for kc in range(KC):
            add("dve", "dora", w, kc)
    add("dve", "fro")
    add("dve", "la")
    for c in range(C0 + 1):
        if c < C0:
            if c % 4 == 0:
                for gi in range(6):
                    add("dve", "v0", c // 4, gi)
            for name in ("q0", "k0"):
                for hf in halves:
                    add("dve", name, c, hf)
            for i in range(3):
                add("act", "decay", c, i)
        if c >= 1:
            for hf in halves:
                add("act", "pv0", c - 1, hf)
        if c < C0:
            for i in range(4):
                add("dve", "score0", c, i)
            for hf in halves:
                add("act", "g0", c, hf)
        if c >= 1:
            add("dve", "gn", c - 1)
    norm(1)
    add("act", "gate1")

    def scores1(c):
        for name in ("q1", "k1"):
            for hf in halves:
                add("act", name, c, hf)
        for i in range(4):
            add("dve", "score1", c, i)

    scores1(0)
    for hf in halves:
        add("act", "onehot_t", hf)
    def values1(c, eq):
        for gi in range(6):
            add("dve", "val", c, eq, gi)

    values1(0, 0)
    for c in range(C1):
        values1(c, 1)
        for i in range(3):
            add("act", "pt1", c, i)
        if c + 1 < C1:
            scores1(c + 1)
        for hf in halves:
            add("act", "pv1", c, hf)
        if c + 1 < C1:
            values1(c + 1, 0)
        for e in range(E0):
            for hf in halves:
                add("dve", "sel", c, e, hf)
    norm(2)
    for hf in halves:
        for mc in range(KC):
            add("act", "q2", hf, mc)
            add("act", "k2", hf, mc)
    for sg in range(5):
        add("dve", "v2", sg)
    for part in range(2):
        for j in range(4):
            add("dve", "score2", j, part)
    for sg in range(5):
        for qd in range(SG[sg][1] // 32):
            add("dve", "pv2", sg, qd)
    for sg in range(5):
        add("act", "o2t", sg)
    for hf in halves:
        for mc in range(KC):
            add("dve", "out2", hf, mc)
    norm(3)
    for hf in halves:
        add("dve", "route", hf)
    add("dve", "probs_t")
    for b2 in range(8):
        add("act", "x_tok", b2)
    add("dve", "rank_t")
    for kc in range(KC):
        for b4 in range(4):
            add("dve", "gather", kc, b4)
    for hf in halves:
        add("act", "scatter_t", hf)
    for e in range(E3 + 1):
        if e < E3:
            for f2 in range(2):
                add("act", "hid", e, f2)
        if e >= 1:
            add("dve", "y", e - 1)
    for b2 in range(8):
        add("act", "y_tok", b2)
    for hf in halves:
        for mc in range(KC):
            add("dve", "res3", hf, mc)
    return out


PSUM_TILES = psum_order()
TILE_NO = {name: i for i, (name, _) in enumerate(PSUM_TILES)}
READ_NO = {}
_counts = {"act": 0, "dve": 0}
for _name, _reader in PSUM_TILES:
    _counts[_reader] += 1
    READ_NO[_name] = (_reader, _counts[_reader])


def pieces():
    out = []
    for c in range(C0):
        if c % 4 == 0:
            out.append((("v0", c // 4), KC * 512))
        out.append((("qkgo", c), 3 * KC * 128 + D))
    out += [(("qk1", 0), 2 * KC * 128), (("val", 0, 0), KC * 4 * 128)]
    for c in range(C1):
        out.append((("val", c, 1), KC * 4 * 128))
        if c + 1 < C1:
            out += [(("qk1", c + 1), 2 * KC * 128), (("val", c + 1, 0), KC * 4 * 128)]
        out += [(("oexp", c, eq), 4 * D) for eq in range(2)]
    return out


PIECES = pieces()
PIECE_NO = {name: n for n, (name, _) in enumerate(PIECES)}
FIRST_AT = [sum(w for _, w in PIECES[:n]) for n in range(len(PIECES) + 1)]
SPLITS0 = {0: (), 1: (5,), 2: (), 3: (6,), 4: (7,), 5: (8,), 6: (9, 10), 7: (11,), 8: (12,), 9: (13,)}
SPLITS1 = ((16, 17, 18), (19, 20, 21)), ((22, 23), (24, 25, 26)), ((27, 28), (29,)), ((), ())


def build(nc, io):
    with ExitStack() as ctx:
        def sem(name):
            return ctx.enter_context(nc.semaphore(name))

        def sb(name, shape, dt=F32):
            return ctx.enter_context(nc.sbuf_tensor(name, shape, dt))

        h = sb("h", [128, KC, T])
        hn = sb("hn", [128, KC, T])
        hn_hi = sb("hn_hi", [128, KC, T], F32R)
        hn_lo = sb("hn_lo", [128, KC, T], F32R)
        raw = sb("raw", [128, RAW, PIECE])
        w_hi = sb("w_hi", [128, SPLIT, PIECE], F32R)
        w_lo = sb("w_lo", [128, SPLIT, PIECE], F32R)
        act_hi = sb("act_hi", [128, NACT], F32R)
        act_lo = sb("act_lo", [128, NACT], F32R)
        cst = sb("cst", [128, NCST])
        csb_bits = sb("csb", [128, NCSB], mybir.dt.uint16)
        csb = csb_bits[:, :].bitcast(BF16)
        vec = sb("vec", [128, NVEC])
        rows = sb("rows", [128, 16 + 256])
        tokadd = sb("tokadd", [128, KC, S])
        eps_col = sb("eps_col", [128, 1])
        one_col = sb("one_col", [128, 1])
        kb_even_odd = sb("kb_even_odd", [128, 2, KC])
        half_b = sb("half_b", [128, C0])
        minus_half = sb("minus_half", [128, B])
        region_x = sb("region_x", [128, NX])
        small_w = sb("small_w", [128, 128 + 32 + 4 * 512 + 16])

        ident = cst[:, 0:128]

        def const(name):
            o, n = CST[name]
            return cst[:, o:o + n]

        def constb(name):
            o, n = CSB[name]
            return csb[:, o:o + n]

        def col(name, i=0):
            o = VEC[name][0] + i
            return vec[:, o:o + 1]

        def cols(name):
            o, n = VEC[name]
            return vec[:, o:o + n]

        class Cut:
            def __init__(self, region, at=0):
                self.region, self.at = region, at

            def __call__(self, n, pattern=None, dt=None, **sizes):
                piece = self.region[:, self.at:self.at + n]
                self.at += n
                if dt is not None:
                    piece = piece.bitcast(dt)
                return piece.rearrange(pattern, **sizes) if pattern else piece

        cut = Cut(small_w)
        wgate1 = cut(128, "p (k n) -> p k n", k=KC)
        wa0 = cut(32, "p (k n) -> p k n", k=KC)
        dora_w = [cut(512, "p (k n) -> p k n", k=KC) for _ in range(2)]
        wk2, wout2 = (cut(512, "p (k n) -> p k n", k=KC) for _ in range(2))
        choice3 = cut(16, "p (k n) -> p k n", k=KC)

        cut = Cut(region_x)
        hc, sq = (cut(2 * KC * HT, "p (f k n) -> p f k n", f=2, k=KC) for _ in range(2))
        std = cut(2 * HT, "p (f n) -> p f n", f=2)
        rstd = cut(HT)
        patches = cut(FC0 * B * NP, "p (k n) -> p k n", k=FC0)
        wlin = cut(FC0 * D, "p (k n) -> p k n", k=FC0)
        cut = Cut(region_x)
        q0, k0 = ([cut(T) for _ in range(2)] for _ in range(2))
        tanh_qk = [cut(HT) for _ in range(4)]
        tanh_g = [cut(T) for _ in range(3)]
        osb = [cut(T) for _ in range(2)]
        gsq = cut(T)

        def by_group(piece):
            return (piece[:, 0:4 * GMAX], piece[:, 4 * GMAX:8 * GMAX], piece[:, 8 * GMAX:8 * GMAX + 4 * 76])

        steps = [by_group(cut(1216)) for _ in range(2)]
        decay = by_group(cut(1216))
        att = by_group(cut(1216))
        v0 = [cut(6 * 512, "p (g n) -> p g n", g=6) for _ in range(2)]
        la, la_abs, la_exp, la_ln = (cut(96, "p (g n) -> p g n", g=6) for _ in range(4))
        gsum, gmean = cut(32), cut(32)
        gvar, gstd, gtmp = (cut(16) for _ in range(3))
        gscale, gshift = ([cut(16) for _ in range(2)] for _ in range(2))
        lora = region_x[0:8, cut.at:cut.at + 4 * D]
        cut(4 * D)
        junk = gsq[:, 0:D]
        assert cut.at <= NX
        fro = sb("fro", [128, 16])
        cut = Cut(region_x)
        q1, k1 = ([cut(T) for _ in range(2)] for _ in range(2))
        prob1 = [by_group(cut(1216)) for _ in range(2)]
        prob1t = by_group(cut(1216))
        vals = [cut(6 * 128, "p (g n) -> p g n", g=6) for _ in range(2)]
        gout, gout_hi, gout_lo = cut(T), cut(T), cut(T)
        gate, onehot, ohwork = (cut(6 * 64, "p (g n) -> p g n", g=6) for _ in range(3))
        gmax, ohmax = (cut(48, "p (g n) -> p g n", g=6) for _ in range(2))
        negmax1, sum1 = cut(32), [cut(16) for _ in range(2)]
        onehot_t = cut(T // 2, dt=BF16)
        cut = Cut(region_x)
        q2, keven, kodd, o2t = (cut(KC * T, "p (k n) -> p k n", k=KC) for _ in range(4))
        v2 = cut(5 * H2 * 17, "p (g h n) -> p g h n", g=5, h=H2)
        prob2 = [[cut(n) for _ in range(4)] for n in (512, 128)]
        prob2t = [[cut(n) for _ in range(4)] for n in (512, 128)]
        o2 = cut(5 * D, "p (g n) -> p g n", g=5)
        rden2 = cut(5 * H2, "p (g n) -> p g n", g=5)
        negmax2 = cut(128)
        assert cut.at <= NX
        cut = Cut(region_x)
        probs = cut(6 * E3, "p (g n) -> p g n", g=6)
        pwork = cut(6 * E3, "p (g n) -> p g n", g=6)
        psum3 = cut(6, "p (g n) -> p g n", g=6)
        pspread = [cut(128) for _ in range(2)]
        pt = cut(2 * S)
        above_space = region_x[:, cut.at:cut.at + 2 * S * S]
        above = cut(S * S, "p (a b) -> p a b", a=S)
        equal = cut(S * S, "p (a b) -> p a b", a=S)
        ptt = cut(256)
        pick = cut(B * E3 * CAP)
        pickw = cut(B * E3 * CAP)
        x_tok = cut(B * D, "p (b n) -> p b n", b=B)
        y_tok = x_tok
        y_t = cut(KC * B * E3 * CAP, "p (k b e c) -> p k b e c", k=KC, b=B, e=E3)
        scatter_t = cut(T)
        hid = [cut(4 * B * CAP) for _ in range(2)]
        res = cut(2 * HT * KC, "p (k n) -> p k n", k=KC)
        before = cut(S * S, "p (a b) -> p a b", a=S)
        assert cut.at <= NX
        x_in = above_space[:, 0:KC * E3 * B * CAP].rearrange("p (k e b c) -> p k e b c", k=KC, e=E3, b=B)
        w_mlp = [cut(PIECE) for _ in range(3)] + [raw[:, i, :] for i in range(RAW)]
        assert cut.at <= NX

        ring = [ctx.enter_context(nc.psum_tensor(f"ring{i}", [128, 512], F32)) for i in range(RING)]
        acc = [[ctx.enter_context(nc.psum_tensor(f"acc{i}{hf}", [128, 512], F32)) for hf in range(2)]
               for i in range(KC)]

        loaded = {n: sem(f"loaded_{n}") for n in (
            "cst", "csb", "vec", "rows", "pos", "patches", "wlin", "wa", "lora", "dora0", "dora1",
            "gate1", "k2", "out2", "choice")}
        piece_loaded = [sem(f"piece_loaded{i}") for i in range(RAW)]
        mlp_loaded = [sem(f"mlp_loaded{i}") for i in range(6)]
        hi_done = sem("hi_done")
        lo_done = sem("lo_done")
        hn_hi_done = sem("hn_hi_done")
        hn_lo_done = sem("hn_lo_done")
        tiles_filled = sem("tiles_filled")
        act_evac = sem("act_evac")
        dve_evac = sem("dve_evac")
        consts_set = sem("consts_set")
        tok_added = sem("tok_added")
        squared = sem("squared")
        normed = sem("normed")
        dve_step = sem("dve_step")
        act_step = sem("act_step")
        pool_step = sem("pool_step")
        la_abs_done = sem("la_abs_done")
        la_ln_done = sem("la_ln_done")
        la_done = sem("la_done")
        tanh_done = sem("tanh_done")
        steps_done = sem("steps_done")
        gsq_done = sem("gsq_done")
        gsq_read = sem("gsq_read")
        gvar_done = sem("gvar_done")
        gscale_done = sem("gscale_done")
        gn_scaled = sem("gn_scaled")
        gn_shifted = sem("gn_shifted")
        gn_gated = sem("gn_gated")
        og_hi_done = sem("og_hi_done")
        og_lo_done = sem("og_lo_done")
        wo_mms = sem("wo_mms")
        wo_added = sem("wo_added")
        onehot_done = sem("onehot_done")
        exp1_done = sem("exp1_done")
        scale1_done = sem("scale1_done")
        prob1_done = sem("prob1_done")
        vals_done = sem("vals_done")
        gout_split = sem("gout_split")
        expert_mms = sem("expert_mms")
        experts_added = sem("experts_added")
        dora_done = sem("dora_done")
        dora_sq = sem("dora_sq")
        fro_done = sem("fro_done")
        exp2_done = sem("exp2_done")
        prob2t_done = sem("prob2t_done")
        exp3_done = sem("exp3_done")
        shifted3 = sem("shifted3")
        probs_done = sem("probs_done")
        spread_done = sem("spread_done")
        rank_done = sem("rank_done")
        pick_done = sem("pick_done")
        pickw_done = sem("pickw_done")
        stored = sem("stored")
        gout_hi_done = sem("gout_hi_done")
        before_set = sem("before_set")
        spread_used = sem("spread_used")

        def filled(*name):
            return TILE_NO[name] + 1

        def evacuated(*name):
            return READ_NO[name][1]

        def bank(*name):
            return ring[TILE_NO[name] % RING]

        def last_use(n):
            name = PIECES[n][0]
            kind, i = name[0], name[1]
            if kind == "qkgo":
                return wo_mms, i + 1
            if kind == "oexp":
                return expert_mms, E0 * i + 4 * name[2] + 4
            last = {"v0": ("v0", i, 5), "qk1": ("k1", i, 1),
                    "val": ("val", *name[1:], 5)}[kind]
            return tiles_filled, filled(*last)

        def chunk_tokens(g, hf):
            off, n = GROUPS[g]
            return hf * HT + off, n

        def part1(parts, i):
            if i < 2:
                return parts[i][0:GMAX, :]
            return parts[2][0:76, 152 * (i - 2):152 * (i - 1)]

        def images(ap, n=HB):
            return ap.rearrange("p (b s) -> p b s", s=S)

        block = ctx.enter_context(nc.Block())

        @block.sync
        def _(sp):

            def load(name, dst):
                sp.dma_start(dst, io[name]).then_inc(loaded[name], 16)

            load("patches", patches)
            load("wlin", wlin)
            load("wa", wa0)
            load("gate1", wgate1)
            load("k2", wk2)
            load("out2", wout2)
            load("choice", choice3)
            for n, (_, width) in enumerate(PIECES):
                if n >= RAW:
                    sp.wait_ge(lo_done, n - RAW + 1)
                sp.dma_start(raw[:, n % RAW, 0:width],
                             io["pieces"][:, FIRST_AT[n]:FIRST_AT[n + 1]]).then_inc(piece_loaded[n % RAW], 16)
            for m in range(2 * E3):
                if m == 0:
                    sp.wait_ge(wo_added, 2)
                elif 3 <= m < 6:
                    sp.wait_ge(lo_done, max(n for n in range(len(PIECES)) if n % RAW == m - 3) + 1)
                elif m >= 6:
                    last = ("y", (m - 6) // 2) if m % 2 else ("hid", (m - 6) // 2, 1)
                    sp.wait_ge(tiles_filled, filled(*last))
                sp.dma_start(w_mlp[m % 6], io["mlp"][:, m * PIECE:(m + 1) * PIECE]).then_inc(mlp_loaded[m % 6], 16)
            for hf in range(2):
                sp.wait_ge(dve_evac, evacuated("res3", hf, KC - 1))
                for kc in range(KC):
                    sp.dma_start(io["out"][kc * 128:(kc + 1) * 128, hf * HT:(hf + 1) * HT],
                                 res[:, kc, hf * HT:(hf + 1) * HT]).then_inc(stored, 16)
            sp.wait_ge(stored, 16 * 2 * KC)

        @block.tensor
        def _(pe):
            mm = nc.tensor.matmul
            next_tile = [0]

            def open_tile(*name):
                n = next_tile[0]
                assert PSUM_TILES[n][0] == name, (PSUM_TILES[n], name)
                next_tile[0] += 1
                if n >= RING:
                    before_it, reader = PSUM_TILES[n - RING]
                    if reader == "act":
                        pe.wait_ge(act_evac, evacuated(*before_it))
                    else:
                        pe.wait_ge(dve_evac, evacuated(*before_it))
                return ring[n % RING]

            def norm(n):
                pe.wait_ge(loaded["cst"], 16)
                for hf in range(2):
                    if n == 0:
                        pe.wait_ge(tok_added, 1)
                        pe.wait_ge(dve_evac, evacuated("tok", hf, KC - 1))
                    elif n == 1:
                        pe.wait_ge(wo_added, hf + 1)
                    elif n == 2:
                        pe.wait_ge(experts_added, hf + 1)
                    else:
                        pe.wait_ge(dve_evac, evacuated("out2", 1, KC - 1))
                    p = open_tile("mean", n, hf)
                    for kc in range(KC):
                        last = mm(p[:, 0:HT], const("mean"), h[:, kc, hf * HT:(hf + 1) * HT],
                                  start=(kc == 0), stop=(kc == KC - 1))
                    last.then_inc(tiles_filled, 1)
                for hf in range(2):
                    pe.wait_ge(squared, 2 * n + hf + 1)
                    p = open_tile("var", n, hf)
                    for kc in range(KC):
                        last = mm(p[:, 0:HT], const("mean"), sq[:, hf, kc, :],
                                  start=(kc == 0), stop=(kc == KC - 1))
                    last.then_inc(tiles_filled, 1)

            def project(name, w, rhs, n_out=1):
                p = open_tile(*name)
                for kc in range(KC):
                    last = mm(p[:, 0:rhs.shape[2]], w[:, kc, :], rhs[:, kc, :],
                              start=(kc == 0), stop=(kc == KC - 1))
                last.then_inc(tiles_filled, 1)

            pe.wait_ge(loaded["patches"], 16)
            pe.wait_ge(loaded["wlin"], 16)
            for hf in range(2):
                for mc in range(KC):
                    p = open_tile("tok", hf, mc)
                    for fc in range(FC0):
                        last = mm(p[:, 0:HB * NP], wlin[:, fc, mc * 128:(mc + 1) * 128],
                                  patches[:, fc, hf * HB * NP:(hf + 1) * HB * NP],
                                  start=(fc == 0), stop=(fc == FC0 - 1))
                    last.then_inc(tiles_filled, 1)
            norm(0)
            pe.wait_ge(loaded["lora"], 16)
            for w in range(2):
                for kc in range(KC):
                    p = open_tile("dora", w, kc)
                    mm(p[:, 0:D], lora[:, (2 * w) * D + kc * 128:(2 * w) * D + (kc + 1) * 128],
                       lora[:, (2 * w + 1) * D:(2 * w + 2) * D], start=True, stop=True).then_inc(tiles_filled, 1)
            pe.wait_ge(dora_sq, 4)
            p = open_tile("fro")
            mm(p[:, 0:4], const("ones"), fro[:, 0:4], start=True, stop=True).then_inc(tiles_filled, 1)

            def three(out, w, x, cols_w, cols_x, start, stop):
                mm(out, w[0][cols_w], x[0][cols_x], start=start, stop=False)
                mm(out, w[0][cols_w], x[1][cols_x], start=False, stop=False)
                return mm(out, w[1][cols_w], x[0][cols_x], start=False, stop=stop)

            hn2 = (hn_hi, hn_lo)

            def piece(*name):
                n = PIECE_NO[name]
                pe.wait_ge(lo_done, n + 1)
                return w_hi[:, n % SPLIT, :], w_lo[:, n % SPLIT, :]

            def project2(name, w, at):
                hf = name[-1]
                p = open_tile(*name)
                for kc in range(KC):
                    last = three(p[:, 0:HT], w, hn2, (slice(None), slice(at + 128 * kc, at + 128 * kc + 128)),
                                 (slice(None), kc, slice(hf * HT, (hf + 1) * HT)), kc == 0, kc == KC - 1)
                last.then_inc(tiles_filled, 1)

            pe.wait_ge(normed, 2)
            pe.wait_ge(loaded["wa"], 16)
            p = open_tile("la")
            for gi, (t0, n) in enumerate(GRP):
                for kc in range(KC):
                    last = mm(p[0:n, gi * 16:gi * 16 + 16], hn[:, kc, t0:t0 + n], wa0[:, kc, :],
                              start=(kc == 0), stop=(kc == KC - 1))
            last.then_inc(tiles_filled, 1)
            pe.wait_ge(hn_lo_done, 2)

            def wo(c):
                w = piece("qkgo", c)
                pe.wait_ge(og_lo_done, c + 1)
                o = 608 * (c % 4)
                for mc in range(KC):
                    for hf in range(2):
                        last = three(acc[mc][hf][:, 0:HT], w, (act_hi, act_lo),
                                     (slice(None), slice(768 + 128 * mc, 896 + 128 * mc)),
                                     (slice(None), slice(o + hf * HT, o + (hf + 1) * HT)), c == 0, c == C0 - 1)
                last.then_inc(wo_mms, 1)

            for c in range(C0 + 3):
                if c < C0:
                    if c % 4 == 0:
                        w = piece("v0", c // 4)
                        for gi, (t0, r) in enumerate(GRP):
                            p = open_tile("v0", c // 4, gi)
                            for kc in range(KC):
                                tok = (slice(None), kc, slice(t0, t0 + r))
                                col512 = (slice(None), slice(512 * kc, 512 * kc + 512))
                                last = three(p[0:r, :], hn2, w, tok, col512, kc == 0, kc == KC - 1)
                            last.then_inc(tiles_filled, 1)
                    w = piece("qkgo", c)
                    for hf in range(2):
                        project2(("q0", c, hf), w, 0)
                    for hf in range(2):
                        project2(("k0", c, hf), w, 256)
                    pe.wait_ge(loaded["csb"], 16)
                    for i in range(3):
                        r = GMAX if i < 2 else 76
                        neg = constb("causal_t" if i < 2 else "causal_t2")
                        pe.wait_ge(steps_done, 3 * c + i + 1)
                        p = open_tile("decay", c, i)
                        mm(p[0:r, 0:4 * r], const("after")[0:r, 0:r], steps[c % 2][i][0:r, 0:4 * r],
                           start=True, stop=False)
                        mm(p[0:r, 0:4 * r], constb("ident")[0:r, 0:r], neg[0:r, :],
                           start=False, stop=True).then_inc(tiles_filled, 1)
                if c >= 3:
                    wo(c - 3)
                if 1 <= c <= C0:
                    l = c - 1
                    pe.wait_ge(dve_evac, evacuated("v0", l // 4, 5))
                    pe.wait_ge(dve_evac, evacuated("score0", l, 3))
                    for hf in range(2):
                        p = open_tile("pv0", l, hf)
                        for par in range(2):
                            for gi, (t0, r) in enumerate(GRP):
                                if t0 // HT == hf:
                                    big = gi < 4
                                    a = att[par] if big else att[2]
                                    o = (gi if big else 2 * par + gi - 4) * r
                                    hd = 128 * (l % 4) + 64 * par
                                    last = mm(p[64 * par:64 * par + 64, t0 - hf * HT:t0 - hf * HT + r],
                                              v0[l // 4][0:r, gi, hd:hd + 64], a[0:r, o:o + r],
                                              start=True, stop=True)
                        last.then_inc(tiles_filled, 1)
                if c < C0:
                    pe.wait_ge(dve_evac, evacuated("k0", c, 1))
                    for i in range(4):
                        par, small = i % 2, i // 2
                        p = open_tile("score0", c, i)
                        for x, (t0, r) in enumerate(GRP[4:] if small else GRP[:4]):
                            last = mm(p[0:r, x * r:(x + 1) * r], k0[c % 2][64 * par:64 * par + 64, t0:t0 + r],
                                      q0[c % 2][64 * par:64 * par + 64, t0:t0 + r], start=True, stop=True)
                        last.then_inc(tiles_filled, 1)
                    for hf in range(2):
                        project2(("g0", c, hf), w, 512)
                if 1 <= c <= C0:
                    pe.wait_ge(gsq_read, c)
                    p = open_tile("gn", c - 1)
                    mm(p[:, 0:32], const("gn_block"), gsum, start=True, stop=True).then_inc(tiles_filled, 1)
            norm(1)

            pe.wait_ge(normed, 4)
            pe.wait_ge(loaded["gate1"], 16)
            p = open_tile("gate1")
            for gi, (t0, n) in enumerate(GRP):
                for kc in range(KC):
                    last = mm(p[0:n, gi * 64:gi * 64 + 64], hn[:, kc, t0:t0 + n], wgate1[:, kc, :],
                              start=(kc == 0), stop=(kc == KC - 1))
            last.then_inc(tiles_filled, 1)
            pe.wait_ge(hn_lo_done, 4)

            def scores1(c):
                w = piece("qk1", c)
                for hf in range(2):
                    project2(("q1", c, hf), w, 0)
                for hf in range(2):
                    project2(("k1", c, hf), w, 256)
                pe.wait_ge(act_evac, evacuated("k1", c, 1))
                for i in range(4):
                    par, small = i % 2, i // 2
                    groups = GRP[4:] if small else GRP[:4]
                    r = groups[0][1]
                    n = len(groups) * r
                    neg = constb("causal2" if small else "causal")
                    p = open_tile("score1", c, i)
                    mm(p[0:r, 0:n], constb("ident")[0:r, 0:r], neg[0:r, 0:n], start=True, stop=True)
                    for x, (t0, r) in enumerate(groups):
                        last = mm(p[0:r, x * r:(x + 1) * r], q1[c % 2][64 * par:64 * par + 64, t0:t0 + r],
                                  k1[c % 2][64 * par:64 * par + 64, t0:t0 + r], start=False, stop=True,
                                  skip_group_check=True)
                    last.then_inc(tiles_filled, 1)

            def through_expert(c, e):
                w = piece("oexp", c, e // 4)
                pe.wait_ge(dve_evac, evacuated("sel", c, e, 1))
                i = E0 * c + e
                o = 608 * (i % 4)
                for mc in range(KC):
                    at = D * (e % 4) + 128 * mc
                    for hf in range(2):
                        last = three(acc[mc][hf][:, 0:HT], w, (act_hi, act_lo), (slice(None), slice(at, at + 128)),
                                     (slice(None), slice(o + hf * HT, o + (hf + 1) * HT)),
                                     i == 0, i == E0 * C1 - 1)
                last.then_inc(expert_mms, 1)

            def values1(c, eq):
                w = piece("val", c, eq)
                for gi, (t0, r) in enumerate(GRP):
                    p = open_tile("val", c, eq, gi)
                    for kc in range(KC):
                        last = three(p[0:r, :], hn2, w, (slice(None), kc, slice(t0, t0 + r)),
                                     (slice(None), slice(512 * kc, 512 * kc + 512)), kc == 0, kc == KC - 1)
                    last.then_inc(tiles_filled, 1)

            scores1(0)
            pe.wait_ge(onehot_done, 1)
            for hf in range(2):
                p = open_tile("onehot_t", hf)
                for gi, (t0, r) in enumerate(GRP):
                    if t0 // HT == hf:
                        o = t0 - hf * HT
                        last = nc.tensor.transpose(p[0:64, o:o + r], onehot[0:r, gi, :], ident[0:r, 0:r])
                last.then_inc(tiles_filled, 1)
            values1(0, 0)
            for c in range(C1):
                values1(c, 1)
                pe.wait_ge(prob1_done, 4 * c + 4)
                for i in range(3):
                    r = 76 if i == 2 else GMAX
                    p = open_tile("pt1", c, i)
                    for x in range(4):
                        last = nc.tensor.transpose(p[0:r, x * r:(x + 1) * r], prob1[c % 2][i][0:r, x * r:(x + 1) * r],
                                                   ident[0:r, 0:r])
                    last.then_inc(tiles_filled, 1)
                if c + 1 < C1:
                    scores1(c + 1)
                pe.wait_ge(vals_done, c + 1)
                pe.wait_ge(act_evac, evacuated("pt1", c, 2))
                for hf in range(2):
                    p = open_tile("pv1", c, hf)
                    for par in range(2):
                        for gi, (t0, r) in enumerate(GRP):
                            if t0 // HT == hf:
                                big = gi < 4
                                a = prob1t[par] if big else prob1t[2]
                                o = (gi if big else 2 * par + gi - 4) * r
                                last = mm(p[64 * par:64 * par + 64, t0 - hf * HT:t0 - hf * HT + r],
                                          vals[c % 2][0:r, gi, 64 * par:64 * par + 64], a[0:r, o:o + r],
                                          start=True, stop=True)
                    last.then_inc(tiles_filled, 1)
                if c + 1 < C1:
                    values1(c + 1, 0)
                pe.wait_ge(act_evac, evacuated("onehot_t", 1))
                if c == 0:
                    pe.wait_ge(wo_added, 2)
                for e in range(E0):
                    sel = constb("select")[0:64, (e * C1 + c) * 128:(e * C1 + c + 1) * 128]
                    for hf in range(2):
                        p = open_tile("sel", c, e, hf)
                        mm(p[:, 0:HT], sel, onehot_t[0:64, hf * HT:(hf + 1) * HT],
                           start=True, stop=True).then_inc(tiles_filled, 1)
                    if e >= 1:
                        through_expert(c, e - 1)
                through_expert(c, E0 - 1)
            norm(2)

            pe.wait_ge(normed, 6)
            pe.wait_ge(dora_done, 1)
            pe.wait_ge(loaded["k2"], 16)
            for hf in range(2):
                tok = hn[:, :, hf * HT:(hf + 1) * HT]
                for mc in range(KC):
                    project(("q2", hf, mc), dora_w[0][:, :, mc * 128:(mc + 1) * 128], tok)
                    project(("k2", hf, mc), wk2[:, :, mc * 128:(mc + 1) * 128], tok)
            for sg, (t0, r) in enumerate(SG):
                p = open_tile("v2", sg)
                for kc in range(KC):
                    last = mm(p[0:r, 0:D], hn[:, kc, t0:t0 + r], dora_w[1][:, kc, :],
                              start=(kc == 0), stop=(kc == KC - 1))
                last.then_inc(tiles_filled, 1)
            pe.wait_ge(act_evac, evacuated("k2", 1, KC - 1))
            for part in range(2):
                rows2, groups2 = (128, range(4)) if part == 0 else (96, range(4, 5))
                n = 128 * len(groups2)
                for j in range(4):
                    p = open_tile("score2", j, part)
                    mm(p[0:rows2, 0:n], constb("ident")[0:rows2, 0:rows2], constb("same_pos")[0:rows2, 0:n],
                       start=True, stop=True)
                    for sg in groups2:
                        for qd in range(SG[sg][1] // 32):
                            t0 = SG[sg][0] + 32 * qd
                            for x in range(4):
                                k = kodd if x % 2 else keven
                                o = 128 * (sg % 4) + 32 * x
                                last = mm(p[32 * qd:32 * qd + 32, o:o + 32],
                                          q2[32 * j:32 * j + 32, x // 2, t0:t0 + 32],
                                          k[32 * j:32 * j + 32, x // 2, t0:t0 + 32],
                                          start=False, stop=True, skip_group_check=True)
                    last.then_inc(tiles_filled, 1)
            pe.wait_ge(dve_evac, evacuated("v2", 4))
            for sg in range(5):
                part = sg // 4
                pe.wait_ge(prob2t_done, 4 * part + 4)
                for qd in range(SG[sg][1] // 32):
                    p = open_tile("pv2", sg, qd)
                    rows2 = slice(32 * qd, 32 * qd + 32)
                    for hd in range(H2):
                        j, x = hd % 8 // 2, 2 * (hd // 8) + hd % 2
                        o = 128 * (sg % 4) + 32 * x
                        last = mm(p[rows2, hd * 17:hd * 17 + 17], prob2t[part][j][rows2, o:o + 32],
                                  v2[rows2, sg, hd, :], start=True, stop=True)
                    last.then_inc(tiles_filled, 1)
            for sg, (t0, r) in enumerate(SG):
                pe.wait_ge(dve_evac, evacuated("pv2", sg, r // 32 - 1))
                p = open_tile("o2t", sg)
                for kc in range(KC):
                    last = nc.tensor.transpose(p[:, kc * r:(kc + 1) * r], o2[0:r, sg, kc * 128:(kc + 1) * 128],
                                               ident[0:r, 0:r])
                last.then_inc(tiles_filled, 1)
            pe.wait_ge(loaded["out2"], 16)
            pe.wait_ge(act_evac, evacuated("o2t", 4))
            for hf in range(2):
                for mc in range(KC):
                    project(("out2", hf, mc), wout2[:, :, mc * 128:(mc + 1) * 128],
                            o2t[:, :, hf * HT:(hf + 1) * HT])
            norm(3)

            pe.wait_ge(loaded["choice"], 16)
            for hf in range(2):
                pe.wait_ge(normed, 6 + hf + 1)
                p = open_tile("route", hf)
                for g in range(3):
                    t0, n = chunk_tokens(g, hf)
                    for kc in range(KC):
                        last = mm(p[0:n, g * E3:(g + 1) * E3], hn[:, kc, t0:t0 + n], choice3[:, kc, :],
                                  start=(kc == 0), stop=(kc == KC - 1))
                last.then_inc(tiles_filled, 1)
            p = open_tile("probs_t")
            for g in range(6):
                r = GROUPS[g % 3][1]
                pe.wait_ge(spread_done, g + 1)
                last = mm(p[:, 0:S], pspread[g % 2][0:r, :], const("pos_of")[0:r, :], start=(g == 0), stop=(g == 5))
                last.then_inc(tiles_filled if g == 5 else spread_used, 1)
            for b2 in range(8):
                p = open_tile("x_tok", b2)
                for i in range(2):
                    for kc in range(KC):
                        b = 2 * b2 + i
                        last = nc.tensor.transpose(p[0:S, i * D + kc * 128:i * D + (kc + 1) * 128],
                                                   hn[:, kc, b * S:(b + 1) * S], ident)
                last.then_inc(tiles_filled, 1)
            pe.wait_ge(rank_done, 1)
            p = open_tile("rank_t")
            for i in range(2):
                last = nc.tensor.transpose(p[0:S, i * 128:(i + 1) * 128], pt[:, i * S:(i + 1) * S], ident)
            last.then_inc(tiles_filled, 1)
            pe.wait_ge(pick_done, 1)
            pe.wait_ge(act_evac, evacuated("x_tok", 7))
            for kc in range(KC):
                for b4 in range(4):
                    p = open_tile("gather", kc, b4)
                    for i in range(4):
                        b = 4 * b4 + i
                        last = mm(p[:, i * 72:(i + 1) * 72], x_tok[0:S, b, kc * 128:(kc + 1) * 128],
                                  pick[0:S, b * 72:(b + 1) * 72], start=True, stop=True)
                    last.then_inc(tiles_filled, 1)
            pe.wait_ge(pickw_done, 1)
            for hf in range(2):
                p = open_tile("scatter_t", hf)
                for i in range(HB):
                    b = HB * hf + i
                    last = nc.tensor.transpose(p[0:72, i * S:(i + 1) * S], pickw[0:S, b * 72:(b + 1) * 72],
                                               ident[0:S, 0:S])
                last.then_inc(tiles_filled, 1)
            pe.wait_ge(dve_evac, evacuated("gather", KC - 1, 3))
            n = B * CAP
            for e in range(E3 + 1):
                if e < E3:
                    m = 2 * e
                    pe.wait_ge(mlp_loaded[m % 6], 16 * (m // 6 + 1))
                    for f2 in range(2):
                        p = open_tile("hid", e, f2)
                        for i in range(2):
                            for kc in range(KC):
                                at = F3 * kc + 128 * (2 * f2 + i)
                                last = mm(p[:, i * n:(i + 1) * n], w_mlp[m % 6][:, at:at + 128], x_in[:, kc, e],
                                          start=(kc == 0), stop=(kc == KC - 1))
                        last.then_inc(tiles_filled, 1)
                if e >= 1:
                    m = 2 * e - 1
                    pe.wait_ge(mlp_loaded[m % 6], 16 * (m // 6 + 1))
                    pe.wait_ge(act_evac, evacuated("hid", e - 1, 1))
                    p = open_tile("y", e - 1)
                    for mc in range(KC):
                        for f in range(4):
                            at = D * f + 128 * mc
                            last = mm(p[:, mc * n:(mc + 1) * n], w_mlp[m % 6][:, at:at + 128],
                                      hid[(e - 1) % 2][:, f * n:(f + 1) * n], start=(f == 0), stop=(f == 3))
                    last.then_inc(tiles_filled, 1)
            pe.wait_ge(dve_evac, evacuated("y", E3 - 1))
            for b2 in range(8):
                p = open_tile("y_tok", b2)
                for i in range(2):
                    for kc in range(KC):
                        b = 2 * b2 + i
                        last = nc.tensor.transpose(p[0:72, i * D + kc * 128:i * D + (kc + 1) * 128],
                                                   y_t[:, kc, b, :, :].rearrange("p e c -> p (e c)"), ident)
                last.then_inc(tiles_filled, 1)
            pe.wait_ge(act_evac, evacuated("scatter_t", 1))
            for hf in range(2):
                pe.wait_ge(act_evac, evacuated("y_tok", 4 * hf + 3))
                for mc in range(KC):
                    p = open_tile("res3", hf, mc)
                    for i in range(HB):
                        b = HB * hf + i
                        last = mm(p[:, i * S:(i + 1) * S], y_tok[0:72, b, mc * 128:(mc + 1) * 128],
                                  scatter_t[0:72, b * S:(b + 1) * S], start=True, stop=True)
                    last.then_inc(tiles_filled, 1)

        @block.scalar
        def _(act):
            stepped = [0]
            A = nc.scalar.activation

            def load(name, dst):
                act.dma_start(dst, io[name]).then_inc(loaded[name], 16)

            load("vec", vec[:, :])
            load("pos", tokadd[:, :, 1:S])
            load("cst", cst[:, :])
            load("rows", rows[:, :])
            load("lora", lora)
            load("csb", csb_bits[:, :])
            load("dora0", dora_w[0])
            load("dora1", dora_w[1])

            def norm(n):
                act.wait_ge(consts_set, 1)
                for hf in range(2):
                    act.wait_ge(dve_evac, evacuated("mean", n, hf))
                    if n:
                        act.wait_ge(tiles_filled, filled("var", n - 1, hf))
                    A(sq[:, hf], hc[:, hf], ACT.Square).then_inc(squared, 1)
                for hf in range(2):
                    act.wait_ge(tiles_filled, filled("var", n, hf))
                    p = bank("var", n, hf)
                    if n:
                        act.wait_ge(normed, 2 * (n - 1) + hf + 1)
                    A(std[:, hf], p[:, 0:HT], ACT.Sqrt, bias=eps_col[:, 0:1]).then_inc(act_evac, 1)

            def split(n):
                act.wait_ge(piece_loaded[n % RAW], 16 * (n // RAW + 1))
                if n >= SPLIT:
                    s, v = last_use(n - SPLIT)
                    act.wait_ge(s, v)
                width = PIECES[n][1]
                A(w_hi[:, n % SPLIT, 0:width], raw[:, n % RAW, 0:width], ACT.Copy).then_inc(hi_done, 1)

            def split_norm(n):
                for hf in range(2):
                    act.wait_ge(normed, 2 * n + hf + 1)
                    A(hn_hi[:, :, hf * HT:(hf + 1) * HT], hn[:, :, hf * HT:(hf + 1) * HT],
                      ACT.Copy).then_inc(hn_hi_done, 1)

            split(0)
            norm(0)
            split_norm(0)
            for n in range(1, SPLIT):
                split(n)
            act.wait_ge(dve_evac, evacuated("dora", 1, 1))
            for w in range(2):
                for kc in range(KC):
                    A(junk[:, :], dora_w[w][:, kc, :], ACT.Square,
                      accum_out=fro[:, 2 * w + kc:2 * w + kc + 1]).then_inc(dora_sq, 1)
                    act.wait_ge(dora_sq, 2 * w + kc + 1)
            act.wait_ge(fro_done, 1)
            A(fro[:, 6:8], fro[:, 4:6], ACT.Sqrt).then_inc(dora_sq, 1)

            act.wait_ge(la_abs_done, 1)
            for r, a, b in ((GMAX, 0, 4), (76, 4, 6)):
                last = A(la_exp[0:r, a:b], la_abs[0:r, a:b], ACT.Exp, scale=-1.0)
            last.then_inc(act_step, 1)
            act.wait_ge(act_step, 1)
            for r, a, b in ((GMAX, 0, 4), (76, 4, 6)):
                last = A(la_ln[0:r, a:b], la_exp[0:r, a:b], ACT.Ln, bias=one_col[0:r, 0:1])
            last.then_inc(la_ln_done, 1)
            for c in range(C0 + 2):
                if c < C0:
                    for i in range(4):
                        name, hf = ("q0", "k0")[i // 2], i % 2
                        if c:
                            act.wait_ge(dve_evac, evacuated(name, c - 1, hf))
                        act.wait_ge(tiles_filled, filled(name, c, hf))
                        A(tanh_qk[i], bank(name, c, hf)[:, 0:HT], ACT.Tanh, scale=0.5).then_inc(tanh_done, 1)
                    for i in range(3):
                        r = GMAX if i < 2 else 76
                        if c:
                            act.wait_ge(dve_evac, evacuated("score0", c - 1, min(i + 1, 3) if i else 0))
                        act.wait_ge(tiles_filled, filled("decay", c, i))
                        A(decay[i][0:r, :], bank("decay", c, i)[0:r, 0:4 * r], ACT.Exp).then_inc(act_evac, 1)
                if 1 <= c <= C0:
                    for hf in range(2):
                        if c >= 3:
                            act.wait_ge(og_lo_done, c - 2)
                        act.wait_ge(tiles_filled, filled("pv0", c - 1, hf))
                        A(osb[(c - 1) % 2][:, hf * HT:(hf + 1) * HT], bank("pv0", c - 1, hf)[:, 0:HT],
                          ACT.Copy).then_inc(act_evac, 1)
                    act.wait_ge(act_evac, evacuated("pv0", c - 1, 1))
                    if c >= 2:
                        act.wait_ge(gsq_read, c - 1)
                    A(gsq, osb[(c - 1) % 2], ACT.Square).then_inc(gsq_done, 1)
                for n in SPLITS0[c]:
                    split(n)
                if c < C0:
                    for hf in range(2):
                        if c >= 3:
                            act.wait_ge(gn_gated, c - 2)
                        act.wait_ge(tiles_filled, filled("g0", c, hf))
                        A(tanh_g[c % 3][:, hf * HT:(hf + 1) * HT], bank("g0", c, hf)[:, 0:HT], ACT.Tanh,
                          scale=0.5).then_inc(act_evac, 1)
                if c >= 2:
                    l = c - 2
                    act.wait_ge(gn_gated, l + 1)
                    if l >= 4:
                        act.wait_ge(wo_mms, l - 3)
                    o = 608 * (l % 4)
                    A(act_hi[:, o:o + T], osb[l % 2], ACT.Copy).then_inc(og_hi_done, 1)
            norm(1)
            split(14)
            split_norm(1)
            act.wait_ge(tiles_filled, filled("gate1"))
            p = bank("gate1")
            for r, a, b in ((GMAX, 0, 4), (76, 4, 6)):
                last = A(gate[0:r, a:b, :], p[0:r, a * 64:b * 64].rearrange("p (g n) -> p g n", n=64), ACT.Sigmoid)
            last.then_inc(act_evac, 1)

            def scores1(c):
                for name, dst in (("q1", q1), ("k1", k1)):
                    for hf in range(2):
                        act.wait_ge(tiles_filled, filled(name, c, hf))
                        A(dst[c % 2][:, hf * HT:(hf + 1) * HT], bank(name, c, hf)[:, 0:HT],
                          ACT.Copy).then_inc(act_evac, 1)
                for i in range(4):
                    pr = part1(prob1[c % 2], i)
                    act.wait_ge(dve_evac, evacuated("score1", c, i))
                    A(pr, pr, ACT.Exp, scale=64 ** -0.5).then_inc(exp1_done, 1)

            scores1(0)
            for hf in range(2):
                act.wait_ge(tiles_filled, filled("onehot_t", hf))
                A(onehot_t[0:64, hf * HT:(hf + 1) * HT], bank("onehot_t", hf)[0:64, 0:HT],
                  ACT.Copy).then_inc(act_evac, 1)
            split(15)
            for c in range(C1):
                for i in range(3):
                    r = GMAX if i < 2 else 76
                    if c:
                        act.wait_ge(tiles_filled, filled("pv1", c - 1, 1))
                    act.wait_ge(tiles_filled, filled("pt1", c, i))
                    A(prob1t[i][0:r, :], bank("pt1", c, i)[0:r, 0:4 * r], ACT.Copy).then_inc(act_evac, 1)
                if c + 1 < C1:
                    scores1(c + 1)
                for hf in range(2):
                    if c:
                        act.wait_ge(gout_split, c)
                    act.wait_ge(tiles_filled, filled("pv1", c, hf))
                    A(gout[:, hf * HT:(hf + 1) * HT], bank("pv1", c, hf)[:, 0:HT], ACT.Copy).then_inc(act_evac, 1)
                act.wait_ge(act_evac, evacuated("pv1", c, 1))
                if c:
                    act.wait_ge(dve_evac, evacuated("sel", c - 1, E0 - 1, 1))
                A(gout_hi.bitcast(F32R), gout, ACT.Copy).then_inc(gout_hi_done, 1)
                for some in SPLITS1[c]:
                    for n in some:
                        split(n)
            norm(2)
            act.wait_ge(dora_done, 1)
            for hf in range(2):
                t0 = hf * HT
                for mc in range(KC):
                    act.wait_ge(tiles_filled, filled("q2", hf, mc))
                    p = bank("q2", hf, mc)
                    A(q2[:, mc, t0:t0 + HT], p[:, 0:HT], ACT.Identity, bias=col("bias_q", mc),
                      scale=fro[:, 8:9]).then_inc(act_evac, 1)
                    act.wait_ge(tiles_filled, filled("k2", hf, mc))
                    p = bank("k2", hf, mc)
                    A(keven[:, mc, t0:t0 + HT], p[:, 0:HT], ACT.Identity, bias=kb_even_odd[:, 0, mc:mc + 1],
                      scale=col("even"))
                    A(kodd[:, mc, t0:t0 + HT], p[:, 0:HT], ACT.Identity, bias=kb_even_odd[:, 1, mc:mc + 1],
                      scale=col("odd")).then_inc(act_evac, 1)
            for part in range(2):
                rows2, n = (128, 512) if part == 0 else (96, 128)
                for j in range(4):
                    act.wait_ge(dve_evac, evacuated("score2", j, part))
                    pr = prob2[part][j][0:rows2, 0:n]
                    A(pr, pr, ACT.Exp, scale=HD2 ** -0.5).then_inc(exp2_done, 1)
            for sg, (t0, r) in enumerate(SG):
                act.wait_ge(tiles_filled, filled("o2t", sg))
                p = bank("o2t", sg)
                A(o2t[:, :, t0:t0 + r], p[:, 0:2 * r].rearrange("p (k i) -> p k i", k=KC),
                  ACT.Copy).then_inc(act_evac, 1)
            norm(3)
            for hf in range(2):
                act.wait_ge(shifted3, hf + 1)
                for r, a, b in segments(8):
                    last = A(pwork[0:r, 3 * hf + a:3 * hf + b, :], pwork[0:r, 3 * hf + a:3 * hf + b, :], ACT.Exp)
                last.then_inc(exp3_done, 1)
            for b2 in range(8):
                act.wait_ge(tiles_filled, filled("x_tok", b2))
                p = bank("x_tok", b2)
                A(x_tok[0:S, 2 * b2:2 * b2 + 2, :], p[0:S, :].rearrange("p (b n) -> p b n", b=2),
                  ACT.Copy).then_inc(act_evac, 1)
            for hf in range(2):
                act.wait_ge(tiles_filled, filled("scatter_t", hf))
                p = bank("scatter_t", hf)
                A(scatter_t[0:72, hf * HT:(hf + 1) * HT], p[0:72, 0:HT], ACT.Copy).then_inc(act_evac, 1)
            for e in range(E3):
                for f2 in range(2):
                    if e >= 2:
                        act.wait_ge(tiles_filled, filled("y", e - 2))
                    act.wait_ge(tiles_filled, filled("hid", e, f2))
                    n = 2 * B * CAP
                    A(hid[e % 2][:, n * f2:n * f2 + n], bank("hid", e, f2)[:, 0:n], ACT.Silu).then_inc(act_evac, 1)
            for b2 in range(8):
                act.wait_ge(tiles_filled, filled("y_tok", b2))
                p = bank("y_tok", b2)
                A(y_tok[0:72, 2 * b2:2 * b2 + 2, :], p[0:72, :].rearrange("p (b n) -> p b n", b=2),
                  ACT.Copy).then_inc(act_evac, 1)

        @block.vector
        def _(dve):
            V = nc.vector
            stepped = [0]

            def settle(ins):
                ins.then_inc(dve_step, 1)
                stepped[0] += 1
                dve.wait_ge(dve_step, stepped[0])

            def norm(n, position_major=False):
                for hf in range(2):
                    dve.wait_ge(tiles_filled, filled("mean", n, hf))
                    p = bank("mean", n, hf)
                    if n:
                        dve.wait_ge(normed, 2 * (n - 1) + hf + 1)
                        dve.wait_ge(squared, 2 * (n - 1) + hf + 1)
                    V.tensor_tensor(hc[:, hf], h[:, :, hf * HT:(hf + 1) * HT],
                                    p[:, 0:HT].unsqueeze(1).to_broadcast([128, KC, HT]),
                                    ALU.subtract).then_inc(dve_evac, 1)
                for hf in range(2):
                    dve.wait_ge(act_evac, evacuated("var", n, hf))
                    if n or hf:
                        dve.wait_ge(normed, 2 * n + hf)
                    settle(V.reciprocal(rstd[:, :], std[:, hf]))
                    dve.wait_ge(dve_evac, evacuated("mean", n, hf))
                    if position_major:
                        for kc in range(KC):
                            o = hn[:, kc, :].rearrange("p (s b) -> p b s", b=B)[:, hf * HB:(hf + 1) * HB, :]
                            last = V.tensor_tensor(o, images(hc[:, hf, kc]), images(rstd[:, :]), ALU.mult)
                    else:
                        last = V.tensor_tensor(hn[:, :, hf * HT:(hf + 1) * HT], hc[:, hf],
                                               rstd[:, :].unsqueeze(1).to_broadcast([128, KC, HT]), ALU.mult)
                    last.then_inc(normed, 1)

            dve.wait_ge(loaded["vec"], 16)
            dve.wait_ge(loaded["pos"], 16)
            V.tensor_copy(tokadd[:, :, 0:1], cols("cls").unsqueeze(2))
            V.tensor_tensor(tokadd[:, :, 1:2], tokadd[:, :, 1:2], cols("class_tok").unsqueeze(2), ALU.add)
            for kc in range(KC):
                last = V.tensor_scalar(tokadd[:, kc, 2:S], tokadd[:, kc, 2:S], col("b_lin", kc), None, ALU.add)
            settle(last)
            for kc in range(KC):
                last = V.tensor_copy(h[:, kc, :].rearrange("p (b s) -> p b s", s=S)[:, :, 0:2],
                                     tokadd[:, kc, 0:2].unsqueeze(1).to_broadcast([128, B, 2]))
            last.then_inc(tok_added, 1)
            dve.wait_ge(tok_added, 1)
            for hf in range(2):
                for mc in range(KC):
                    dve.wait_ge(tiles_filled, filled("tok", hf, mc))
                    p = bank("tok", hf, mc)
                    o = h[:, mc, :].rearrange("p (b s) -> p b s", s=S)[:, hf * HB:(hf + 1) * HB, 2:S]
                    V.tensor_tensor(o, p[:, 0:HB * NP].rearrange("p (b s) -> p b s", s=NP),
                                    tokadd[:, mc, 2:S].unsqueeze(1).to_broadcast([128, HB, NP]),
                                    ALU.add).then_inc(dve_evac, 1)
            dve.wait_ge(dve_evac, evacuated("tok", 1, KC - 1))
            norm(0)
            for w in range(2):
                dve.wait_ge(loaded[f"dora{w}"], 16)
                for kc in range(KC):
                    dve.wait_ge(tiles_filled, filled("dora", w, kc))
                    p = bank("dora", w, kc)
                    V.tensor_tensor(dora_w[w][:, kc, :], dora_w[w][:, kc, :], p[:, 0:D], ALU.add).then_inc(dve_evac, 1)
            dve.wait_ge(tiles_filled, filled("fro"))
            p = bank("fro")
            V.tensor_copy(fro[:, 10:14], p[:, 0:4]).then_inc(dve_evac, 1)
            dve.wait_ge(dve_evac, evacuated("fro"))
            f2 = fro[:, 10:14].rearrange("p (w k) -> p w k", w=2)
            V.tensor_tensor(fro[:, 4:6], f2[:, :, 0], f2[:, :, 1], ALU.add).then_inc(fro_done, 1)
            V.tensor_scalar(kb_even_odd[:, 0, :], cols("k_b"), col("even"), None, ALU.mult)
            V.tensor_scalar(kb_even_odd[:, 1, :], cols("k_b"), col("odd"), None, ALU.mult)
            dve.wait_ge(dora_sq, 5)
            settle(V.tensor_scalar(fro[:, 6:8], fro[:, 6:8], 1e-8, None, ALU.add))
            settle(V.reciprocal(fro[:, 6:8], fro[:, 6:8]))
            mags = vec[:, VEC["mag_q"][0]:VEC["mag_q"][0] + 2]
            V.tensor_tensor(fro[:, 8:10], fro[:, 6:8], mags, ALU.mult).then_inc(dora_done, 1)

            def split_norm(n):
                for hf in range(2):
                    half = slice(hf * HT, (hf + 1) * HT)
                    dve.wait_ge(hn_hi_done, 2 * n + hf + 1)
                    V.tensor_tensor(hn_lo[:, :, half], hn[:, :, half], hn_hi[:, :, half].bitcast(F32),
                                    ALU.subtract).then_inc(hn_lo_done, 1)

            split_norm(0)
            V.tensor_scalar(half_b[:, :], cols("gn_b"), 0.5, None, ALU.mult)
            dve.wait_ge(loaded["rows"], 16)
            dve.wait_ge(tiles_filled, filled("la"))
            p = bank("la")
            both = ((GMAX, 0, 4), (76, 4, 6))
            for r, a, b in both:
                last = V.tensor_tensor(la[0:r, a:b, :], p[0:r, a * 16:b * 16].rearrange("p (g n) -> p g n", n=16),
                                       rows[0:r, 0:16].unsqueeze(1).to_broadcast([r, b - a, 16]), ALU.add)
            last.then_inc(dve_evac, 1)
            dve.wait_ge(dve_evac, evacuated("la"))
            for r, a, b in both:
                last = V.scalar_tensor_tensor(la_abs[0:r, a:b, :], la[0:r, a:b, :], -1.0, la[0:r, a:b, :],
                                              ALU.mult, ALU.max)
            last.then_inc(la_abs_done, 1)

            def v_tiles(quad):
                for gi, (_, r) in enumerate(GRP):
                    dve.wait_ge(tiles_filled, filled("v0", quad, gi))
                    V.tensor_copy(v0[quad][0:r, gi, :], bank("v0", quad, gi)[0:r, :]).then_inc(dve_evac, 1)

            dve.wait_ge(la_ln_done, 1)
            for r, a, b in both:
                last = V.scalar_tensor_tensor(la[0:r, a:b, :], la[0:r, a:b, :], 0.0, la_ln[0:r, a:b, :],
                                              ALU.max, ALU.add)
            last.then_inc(la_done, 1)

            for c in range(C0 + 2):
                if c < C0:
                    if c % 4 == 0:
                        v_tiles(c // 4)
                    for i in range(4):
                        name, hf = ("q0", "k0")[i // 2], i % 2
                        dst = (q0, k0)[i // 2][c % 2]
                        dve.wait_ge(tanh_done, 4 * c + i + 1)
                        V.scalar_tensor_tensor(dst[:, hf * HT:(hf + 1) * HT], tanh_qk[i], 1.0,
                                               bank(name, c, hf)[:, 0:HT], ALU.add, ALU.mult).then_inc(dve_evac, 1)
                if c >= 2:
                    l = c - 2
                    dve.wait_ge(gscale_done, l + 1)
                    o = osb[l % 2].rearrange("p (b s) -> p b s", s=S)
                    V.tensor_tensor(o, o, gscale[l % 2].unsqueeze(2).to_broadcast([128, B, S]),
                                    ALU.mult).then_inc(gn_scaled, 1)
                if 1 <= c <= C0:
                    l = c - 1
                    if l:
                        dve.wait_ge(tiles_filled, filled("gn", l - 1))
                    dve.wait_ge(act_evac, evacuated("pv0", l, 1))
                    V.tensor_reduce(gsum[:, 0:16], osb[l % 2].rearrange("p (b s) -> p b s", s=S), AXX, ALU.add)
                    dve.wait_ge(gsq_done, l + 1)
                    V.tensor_reduce(gsum[:, 16:32], gsq.rearrange("p (b s) -> p b s", s=S), AXX,
                                    ALU.add).then_inc(gsq_read, 1)
                if c < C0:
                    for i in range(4):
                        r = GMAX if i < 2 else 76
                        n = 4 * r if i < 2 else 2 * r
                        dve.wait_ge(act_evac, evacuated("decay", c, min(i, 2)))
                        if c:
                            dve.wait_ge(tiles_filled, filled("pv0", c - 1, 1))
                        dve.wait_ge(tiles_filled, filled("score0", c, i))
                        V.scalar_tensor_tensor(part1(att, i), bank("score0", c, i)[0:r, 0:n], 0.25,
                                               part1(decay, i), ALU.mult, ALU.mult).then_inc(dve_evac, 1)
                if c >= 2:
                    l = c - 2
                    dve.wait_ge(gn_shifted, l + 1)
                    if l < C0:
                        dve.wait_ge(act_evac, evacuated("g0", l, 1))
                    V.scalar_tensor_tensor(osb[l % 2], tanh_g[l % 3], 1.0, osb[l % 2], ALU.add,
                                           ALU.mult).then_inc(gn_gated, 1)
                if 1 <= c <= C0:
                    l = c - 1
                    dve.wait_ge(tiles_filled, filled("gn", l))
                    if l:
                        dve.wait_ge(gscale_done, l)
                    V.tensor_copy(gmean, bank("gn", l)[:, 0:32]).then_inc(dve_evac, 1)
                    dve.wait_ge(dve_evac, evacuated("gn", l))
                    settle(V.tensor_tensor(gvar, gmean[:, 0:16], gmean[:, 0:16], ALU.mult))
                    settle(V.tensor_tensor(gvar, gmean[:, 16:32], gvar, ALU.subtract))
                    V.tensor_scalar(gvar, gvar, 0.0, EPS, ALU.max, ALU.add).then_inc(gvar_done, 1)
                if c >= 2:
                    l = c - 2
                    o = 608 * (l % 4)
                    dve.wait_ge(og_hi_done, l + 1)
                    dve.wait_ge(gn_gated, l + 1)
                    V.tensor_tensor(act_lo[:, o:o + T], osb[l % 2], act_hi[:, o:o + T].bitcast(F32),
                                    ALU.subtract).then_inc(og_lo_done, 1)
            dve.wait_ge(wo_mms, C0)
            for hf in range(2):
                for mc in range(KC):
                    hh = h[:, mc, hf * HT:(hf + 1) * HT]
                    last = V.tensor_tensor(hh, hh, acc[mc][hf][:, 0:HT], ALU.add)
                last.then_inc(wo_added, 1)
            dve.wait_ge(wo_added, 2)
            norm(1)
            split_norm(1)

            dve.wait_ge(act_evac, evacuated("gate1"))
            for r, a, b in both:
                n = b - a
                eight = lambda t: t[0:r, a:b, :].rearrange("p g (h e) -> p (g h) e", e=E0)
                flat = lambda t: t[0:r, a:b, :].rearrange("p g n -> p (g n)")
                settle(V.tensor_reduce(flat(gmax), eight(gate), AXX, ALU.max))
                settle(V.tensor_tensor(eight(ohwork), eight(gate),
                                       flat(gmax).unsqueeze(2).to_broadcast([r, 8 * n, E0]), ALU.is_equal))
                settle(V.tensor_tensor(eight(ohwork), eight(ohwork),
                                       const("desc")[0:r, :].unsqueeze(1).to_broadcast([r, 8 * n, E0]), ALU.mult))
                settle(V.tensor_reduce(flat(ohmax), eight(ohwork), AXX, ALU.max))
                last = V.tensor_tensor(eight(onehot), eight(ohwork),
                                       flat(ohmax).unsqueeze(2).to_broadcast([r, 8 * n, E0]), ALU.is_equal)
            last.then_inc(onehot_done, 1)
            dve.wait_ge(onehot_done, 1)

            def scores1(c):
                for i in range(4):
                    r, n = (GMAX, 4) if i < 2 else (76, 2)
                    dve.wait_ge(tiles_filled, filled("score1", c, i))
                    p3 = bank("score1", c, i)[0:r, 0:n * r].rearrange("p (x j) -> p x j", x=n)
                    nm = negmax1[0:r, 4 * i:4 * i + n]
                    if c:
                        dve.wait_ge(dve_evac, evacuated("score1", c - 1, i))
                    settle(V.tensor_reduce(nm, p3, AXX, ALU.max, negate=True))
                    V.tensor_tensor(part1(prob1[c % 2], i).rearrange("p (x j) -> p x j", x=n), p3,
                                    nm.unsqueeze(2).to_broadcast([r, n, r]), ALU.add).then_inc(dve_evac, 1)
                for i in range(4):
                    r, n = (GMAX, 4) if i < 2 else (76, 2)
                    g0_, g1_ = (0, 4) if i < 2 else (4, 6)
                    dve.wait_ge(exp1_done, 4 * c + i + 1)
                    sm = sum1[c % 2][0:r, 4 * i:4 * i + n]
                    settle(V.tensor_reduce(sm, part1(prob1[c % 2], i).rearrange("p (x j) -> p x j", x=n),
                                           AXX, ALU.add))
                    settle(V.reciprocal(sm, sm))
                    V.tensor_tensor(sm, sm, gmax[0:r, g0_:g1_, 2 * c + i % 2], ALU.mult).then_inc(scale1_done, 1)

            def values1(c, eq):
                for gi, (_, r) in enumerate(GRP):
                    dve.wait_ge(tiles_filled, filled("val", c, eq, gi))
                    p = bank("val", c, eq, gi)
                    out = vals[c % 2][0:r, gi, :]
                    for e in range(4):
                        data = p[0:r, 128 * e:128 * e + 128]
                        if eq == 0 and e == 0:
                            settle(V.tensor_copy(out, data))
                            continue
                        pick8 = onehot[0:r, gi, E0 * 2 * c + 4 * eq + e:E0 * (2 * c + 2):E0]
                        if e == 0:
                            dve.wait_ge(dve_evac, evacuated("val", c, 0, gi))
                        last = V.copy_predicated(out.rearrange("p (h k) -> p h k", h=2),
                                                 pick8.bitcast(I32).unsqueeze(2).to_broadcast([r, 2, 64]),
                                                 data.rearrange("p (h k) -> p h k", h=2))
                        if e < 3:
                            settle(last)
                    last.then_inc(dve_evac, 1)

            scores1(0)
            values1(0, 0)
            for c in range(C1):
                values1(c, 1)
                if c + 1 < C1:
                    scores1(c + 1)
                dve.wait_ge(gout_hi_done, c + 1)
                if c:
                    dve.wait_ge(dve_evac, evacuated("sel", c - 1, E0 - 1, 1))
                V.tensor_tensor(gout_lo, gout, gout_hi, ALU.subtract).then_inc(gout_split, 1)
                if c + 1 < C1:
                    values1(c + 1, 0)
                dve.wait_ge(gout_split, c + 1)
                for e in range(E0):
                    i = E0 * c + e
                    if i >= 4:
                        dve.wait_ge(expert_mms, i - 3)
                    for hf in range(2):
                        o = 608 * (i % 4) + hf * HT
                        half = slice(hf * HT, (hf + 1) * HT)
                        dve.wait_ge(tiles_filled, filled("sel", c, e, hf))
                        p = bank("sel", c, e, hf)
                        V.tensor_tensor(act_hi[:, o:o + HT], gout_hi[:, half], p[:, 0:HT], ALU.mult)
                        V.tensor_tensor(act_lo[:, o:o + HT], gout_lo[:, half], p[:, 0:HT],
                                        ALU.mult).then_inc(dve_evac, 1)
            dve.wait_ge(expert_mms, E0 * C1)
            for hf in range(2):
                for mc in range(KC):
                    hh = h[:, mc, hf * HT:(hf + 1) * HT]
                    last = V.tensor_tensor(hh, hh, acc[mc][hf][:, 0:HT], ALU.add)
                last.then_inc(experts_added, 1)
            dve.wait_ge(experts_added, 2)
            norm(2, position_major=True)
            dve.wait_ge(dora_done, 1)
            dve.wait_ge(tiles_filled, filled("q2", 0, 0))
            V.memset(v2[:, :, :, 16:17], 1.0)
            for sg, (t0, r) in enumerate(SG):
                dve.wait_ge(tiles_filled, filled("v2", sg))
                p = bank("v2", sg)
                V.scalar_tensor_tensor(v2[0:r, sg, :, 0:16], p[0:r, 0:D].rearrange("p (h n) -> p h n", h=H2),
                                       fro[0:r, 9:10], rows[0:r, 16:16 + D].rearrange("p (h n) -> p h n", h=H2),
                                       ALU.mult, ALU.add).then_inc(dve_evac, 1)

            for part in range(2):
                rows2, n = (128, 512) if part == 0 else (96, 128)
                for j in range(4):
                    dve.wait_ge(tiles_filled, filled("score2", j, part))
                    p = bank("score2", j, part)
                    p3 = p[0:rows2, 0:n].rearrange("p (x j) -> p x j", j=32)
                    nm = negmax2[0:rows2, 16 * j + 64 * part:16 * j + 64 * part + n // 32]
                    settle(V.tensor_reduce(nm, p3, AXX, ALU.max, negate=True))
                    V.tensor_tensor(prob2[part][j][0:rows2, 0:n].rearrange("p (x j) -> p x j", j=32), p3,
                                    nm.unsqueeze(2).to_broadcast([rows2, n // 32, 32]), ALU.add).then_inc(dve_evac, 1)
                for j in range(4):
                    dve.wait_ge(exp2_done, 4 * part + j + 1)
                    V.transpose(prob2t[part][j][0:rows2, 0:n], prob2[part][j][0:rows2, 0:n]).then_inc(prob2t_done, 1)
            V.tensor_tensor(before, const("position").unsqueeze(2).to_broadcast([128, S, S]),
                            const("position").unsqueeze(1).to_broadcast([128, S, S]),
                            ALU.is_gt).then_inc(before_set, 1)
            for sg in range(5):
                for qd in range(SG[sg][1] // 32):
                    dve.wait_ge(tiles_filled, filled("pv2", sg, qd))
                    p = bank("pv2", sg, qd)
                    rows2 = slice(32 * qd, 32 * qd + 32)
                    p3 = p[rows2, 0:H2 * 17].rearrange("p (h n) -> p h n", n=17)
                    settle(V.reciprocal(rden2[rows2, sg, :], p3[:, :, 16]))
                    V.tensor_tensor(o2[rows2, sg, :].rearrange("p (h n) -> p h n", h=H2), p3[:, :, 0:16],
                                    rden2[rows2, sg, :].unsqueeze(2).to_broadcast([32, H2, 16]),
                                    ALU.mult).then_inc(dve_evac, 1)
            for hf in range(2):
                for mc in range(KC):
                    dve.wait_ge(tiles_filled, filled("out2", hf, mc))
                    p = bank("out2", hf, mc)
                    hh = h[:, mc, :].rearrange("p (b s) -> p s b", s=S)[:, 19 * hf:19 * hf + 19, :]
                    V.scalar_tensor_tensor(hh, p[:, 0:HT].rearrange("p (s b) -> p s b", b=B), col("out_b", mc), hh,
                                           ALU.add, ALU.add).then_inc(dve_evac, 1)
            dve.wait_ge(dve_evac, evacuated("out2", 1, KC - 1))
            norm(3)
            for hf in range(2):
                dve.wait_ge(tiles_filled, filled("route", hf))
                p = bank("route", hf)
                for r, a, b in segments(8):
                    n = b - a
                    last = V.tensor_copy(probs[0:r, 3 * hf + a:3 * hf + b, :],
                                         p[0:r, a * 8:b * 8].rearrange("p (g n) -> p g n", n=8))
                last.then_inc(dve_evac, 1)
                dve.wait_ge(dve_evac, evacuated("route", hf))
                for r, a, b in segments(8):
                    n = b - a
                    g = slice(3 * hf + a, 3 * hf + b)
                    settle(V.tensor_reduce(psum3[0:r, g, 0], probs[0:r, g, :], AXX, ALU.max))
                    last = V.tensor_tensor(pwork[0:r, g, :], probs[0:r, g, :],
                                           psum3[0:r, g, :].to_broadcast([r, n, 8]), ALU.subtract)
                last.then_inc(shifted3, 1)
            for hf in range(2):
                dve.wait_ge(exp3_done, hf + 1)
                for r, a, b in segments(8):
                    n = b - a
                    g = slice(3 * hf + a, 3 * hf + b)
                    settle(V.tensor_reduce(psum3[0:r, g, 0], pwork[0:r, g, :], AXX, ALU.add))
                    settle(V.reciprocal(psum3[0:r, g, :], psum3[0:r, g, :]))
                    last = V.tensor_tensor(probs[0:r, g, :], pwork[0:r, g, :],
                                           psum3[0:r, g, :].to_broadcast([r, n, 8]), ALU.mult)
                last.then_inc(probs_done, 1)
            dve.wait_ge(tiles_filled, filled("probs_t"))
            p = bank("probs_t")
            V.tensor_copy(pt[:, 0:S], p[:, 0:S]).then_inc(dve_evac, 1)
            dve.wait_ge(dve_evac, evacuated("probs_t"))
            mine = pt[:, 0:S].unsqueeze(2).to_broadcast([128, S, S])
            other = pt[:, 0:S].unsqueeze(1).to_broadcast([128, S, S])
            V.tensor_tensor(above, other, mine, ALU.is_gt)
            settle(V.tensor_tensor(equal, other, mine, ALU.is_equal))
            dve.wait_ge(before_set, 1)
            settle(V.tensor_tensor(equal, equal, before, ALU.mult))
            settle(V.tensor_tensor(above, above, equal, ALU.add))
            V.tensor_reduce(pt[:, S:2 * S], above, AXX, ALU.add).then_inc(rank_done, 1)
            dve.wait_ge(tiles_filled, filled("rank_t"))
            p = bank("rank_t")
            V.tensor_copy(ptt[0:S, :], p[0:S, 0:256]).then_inc(dve_evac, 1)
            dve.wait_ge(dve_evac, evacuated("rank_t"))
            V.tensor_tensor(pick[0:S, :].rearrange("p (a c) -> p a c", c=CAP),
                            ptt[0:S, 128:256].unsqueeze(2).to_broadcast([S, 128, CAP]),
                            const("iota")[0:S, :].unsqueeze(1).to_broadcast([S, 128, CAP]),
                            ALU.is_equal).then_inc(pick_done, 1)
            for kc in range(KC):
                for b4 in range(4):
                    dve.wait_ge(tiles_filled, filled("gather", kc, b4))
                    p = bank("gather", kc, b4)
                    V.tensor_copy(x_in[:, kc, :, 4 * b4:4 * b4 + 4, :].rearrange("p e b c -> p b e c"),
                                  p[:, 0:288].rearrange("p (b e c) -> p b e c", b=4, e=E3)).then_inc(dve_evac, 1)
            for e in range(E3):
                dve.wait_ge(tiles_filled, filled("y", e))
                p = bank("y", e)
                V.tensor_copy(y_t[:, :, :, e, :], p[:, 0:2 * B * CAP].rearrange("p (k b c) -> p k b c", k=KC, b=B)
                              ).then_inc(dve_evac, 1)
            for hf in range(2):
                for mc in range(KC):
                    dve.wait_ge(tiles_filled, filled("res3", hf, mc))
                    p = bank("res3", hf, mc)
                    V.tensor_tensor(res[:, mc, hf * HT:(hf + 1) * HT], h[:, mc, hf * HT:(hf + 1) * HT], p[:, 0:HT],
                                    ALU.add).then_inc(dve_evac, 1)

        @block.gpsimd
        def _(pool):
            G = nc.gpsimd
            G.memset(eps_col[:, :], EPS)
            G.memset(one_col[:, :], 1.0).then_inc(consts_set, 1)
            pool.wait_ge(loaded["cst"], 16)

            G.memset(minus_half[:, :], -0.5).then_inc(consts_set, 1)
            pool.wait_ge(consts_set, 2)
            stepped = [0]

            def settle(ins):
                ins.then_inc(pool_step, 1)
                stepped[0] += 1
                pool.wait_ge(pool_step, stepped[0])

            def split(n):
                width = PIECES[n][1]
                pool.wait_ge(hi_done, n + 1)
                G.tensor_tensor(w_lo[:, n % SPLIT, 0:width], raw[:, n % RAW, 0:width],
                                w_hi[:, n % SPLIT, 0:width].bitcast(F32), ALU.subtract).then_inc(lo_done, 1)

            def decay_steps(c):
                if c >= 2:
                    pool.wait_ge(tiles_filled, filled("decay", c - 2, 2))
                for i in range(3):
                    if i < 2:
                        r = GMAX
                        out = steps[c % 2][i][0:r, :].rearrange("p (x i) -> p x i", x=4)
                        take = la[0:r, 0:4, 2 * c + i].unsqueeze(2).to_broadcast([r, 4, r])
                        n = 4
                        G.tensor_tensor(out, take, const("neg_upto")[0:r, 0:r].unsqueeze(1).to_broadcast([r, n, r]),
                                        ALU.mult).then_inc(steps_done, 1)
                    else:
                        r = 76
                        for par in range(2):
                            out = steps[c % 2][2][0:r, 152 * par:152 * par + 152].rearrange("p (x i) -> p x i", x=2)
                            take = la[0:r, 4:6, 2 * c + par].unsqueeze(2).to_broadcast([r, 2, r])
                            last = G.tensor_tensor(out, take, const("neg_upto")[0:r, 0:r].unsqueeze(1)
                                                   .to_broadcast([r, 2, r]), ALU.mult)
                        last.then_inc(steps_done, 1)

            for n in range(SPLIT):
                split(n)
            pool.wait_ge(la_done, 1)
            decay_steps(0)
            for c in range(C0 + 2):
                if c + 1 < C0:
                    decay_steps(c + 1)
                if c >= 2:
                    l = c - 2
                    pool.wait_ge(gscale_done, l + 1)
                    pool.wait_ge(gn_scaled, l + 1)
                    o = osb[l % 2].rearrange("p (b s) -> p b s", s=S)
                    G.tensor_tensor(o, o, gshift[l % 2].unsqueeze(2).to_broadcast([128, B, S]),
                                    ALU.add).then_inc(gn_shifted, 1)
                for n in SPLITS0[c]:
                    split(n)
                if 1 <= c <= C0:
                    l = c - 1
                    pool.wait_ge(gvar_done, l + 1)
                    settle(G.tensor_tensor(gstd, gvar, minus_half[:, :], ALU.pow))
                    settle(G.tensor_scalar(gscale[l % 2], gstd, col("gn_w", l), 0.5, ALU.mult, ALU.mult))
                    settle(G.tensor_tensor(gtmp, gmean[:, 0:16], gscale[l % 2], ALU.mult))
                    settle(G.tensor_scalar(gtmp, gtmp, -1.0, None, ALU.mult))
                    G.tensor_scalar(gshift[l % 2], gtmp, half_b[:, l:l + 1], None, ALU.add).then_inc(gscale_done, 1)
            split(14)

            def weight1(c):
                for i in range(4):
                    r, n = (GMAX, 4) if i < 2 else (76, 2)
                    pool.wait_ge(scale1_done, 4 * c + i + 1)
                    p3 = part1(prob1[c % 2], i).rearrange("p (x j) -> p x j", x=n)
                    G.tensor_tensor(p3, p3, sum1[c % 2][0:r, 4 * i:4 * i + n].unsqueeze(2).to_broadcast([r, n, r]),
                                    ALU.mult).then_inc(prob1_done, 1)

            weight1(0)
            split(15)
            for c in range(C1):
                pool.wait_ge(dve_evac, evacuated("val", c, 1, 5))
                for r, a, b in ((GMAX, 0, 4), (76, 4, 6)):
                    for par in range(2):
                        v3 = vals[c % 2][0:r, a:b, 64 * par:64 * par + 64]
                        last = G.tensor_tensor(v3, v3, gmax[0:r, a:b, 2 * c + par].unsqueeze(2)
                                               .to_broadcast([r, b - a, 64]), ALU.mult)
                last.then_inc(vals_done, 1)
                for n in SPLITS1[c][0]:
                    split(n)
                if c + 1 < C1:
                    weight1(c + 1)
                for n in SPLITS1[c][1]:
                    split(n)
            for g in range(6):
                r = GROUPS[g % 3][1]
                pool.wait_ge(probs_done, g // 3 + 1)
                if g >= 2:
                    pool.wait_ge(spread_used, g - 1)
                G.tensor_tensor(pspread[g % 2][0:r, :].rearrange("p (b e) -> p b e", e=E3),
                                probs[0:r, g, :].unsqueeze(1).to_broadcast([r, B, E3]),
                                const("image_of")[0:r, g * B:(g + 1) * B].unsqueeze(2).to_broadcast([r, B, E3]),
                                ALU.mult).then_inc(spread_done, 1)
            pool.wait_ge(pick_done, 1)
            G.tensor_tensor(pickw[0:S, :].rearrange("p (a c) -> p a c", c=CAP),
                            pick[0:S, :].rearrange("p (a c) -> p a c", c=CAP),
                            ptt[0:S, 0:128].unsqueeze(2).to_broadcast([S, 128, CAP]), ALU.mult).then_inc(pickw_done, 1)


def constants():
    f = np.zeros((128, NCST), np.float32)
    b = np.zeros((128, NCSB), np.float32)

    def put(a, table, name, v):
        o, n = table[name]
        a[:v.shape[0], o:o + n] = v.reshape(v.shape[0], -1)

    i = np.arange(128)
    put(f, CST, "ident", np.eye(128))
    put(f, CST, "mean", np.full((128, 128), 1.0 / D))
    put(f, CST, "ones", np.ones((128, 128)))
    put(f, CST, "gn_block", (i[:, None] // 64 == i[None] // 64) / (64.0 * S))
    put(f, CST, "after", i[:, None] > i[None])
    put(f, CST, "neg_upto", -1.0 * (i[:, None] <= i[None]))
    t = np.arange(GMAX)
    put(f, CST, "pos_of", t[:, None] % S == np.arange(S)[None])
    first = [(hf * HT + off) // S for hf in range(2) for off, _ in GROUPS]
    put(f, CST, "image_of", np.stack([t[:, None] // S + b0 == np.arange(B)[None] for b0 in first], 1))
    put(f, CST, "iota", np.tile(np.arange(CAP), (128, 1)))
    put(f, CST, "position", np.tile(np.arange(S), (128, 1)))
    put(f, CST, "desc", np.tile(E0 - np.arange(E0), (128, 1)))
    put(b, CSB, "ident", np.eye(128))
    for suffix, r in (("", GMAX), ("2", 76)):
        t = np.arange(r)
        seen = (t[:, None] // S == t[None] // S) & (t[:, None] >= t[None])
        put(b, CSB, "causal" + suffix, np.tile(np.where(seen, 0, -1e30), (1, 4)))
        put(b, CSB, "causal_t" + suffix, np.tile(np.where(seen.T, 0, -30000.0), (1, 4)))
    put(b, CSB, "same_pos", np.tile(np.where(i[:, None] % 32 // B == np.arange(32)[None] // B, 0, -1e30), (1, 16)))
    sel = np.zeros((H1, E0, E0, C1, 2, 64))
    for e in range(E0):
        for hd in range(H1):
            sel[hd, e, e, hd // 2, hd % 2, :] = 1
    put(b, CSB, "select", sel.reshape(64, -1))
    bits = (b.view(np.uint32) >> 16).astype(np.uint16)
    return f, bits


def feat(a):
    return a.reshape(-1, 128, a.shape[-1]).transpose(1, 0, 2)


def part(g, kind, i, j=0):
    two = slice(128 * i, 128 * i + 128)
    if kind == "v0":
        return feat(g["L0_attn_Wv"][:, 512 * i:512 * i + 512])
    if kind == "qkgo":
        return np.concatenate([feat(g[n][:, two]).reshape(128, -1) for n in ("L0_attn_Wq", "L0_attn_Wk", "L0_attn_Wg")]
                              + [g["L0_attn_Wo"][two]], 1)
    if kind == "qk1":
        return np.concatenate([feat(g[n][:, two]).reshape(128, -1) for n in ("L0_ffn_w_q", "L0_ffn_w_k")], 1)
    if kind == "val":
        return feat(g["L0_ffn_value_experts"][4 * j:4 * j + 4, 2 * i:2 * i + 2].transpose(2, 0, 1, 3).reshape(D, -1))
    if kind == "oexp":
        return g["L0_ffn_output_experts"][4 * j:4 * j + 4, 2 * i:2 * i + 2].reshape(4, 128, D).transpose(1, 0, 2)
    raise ValueError(kind)


def lay_out(i):
    g = {k: np.asarray(v) for k, v in i.items()}
    f, b = constants()
    x = g["x"].reshape(B, 3, 6, 16, 6, 16).transpose(1, 3, 5, 0, 2, 4).reshape(768, B * NP)
    vec = np.zeros((128, NVEC), np.float32)

    def put(name, v):
        o, n = VEC[name]
        vec[:, o:o + n] = v

    def chunks(v):
        return v.reshape(-1, 128).T

    put("b_lin", chunks(g["L0_tok_b_lin"]))
    put("cls", chunks(g["cls_tok"]))
    put("class_tok", chunks(g["L0_tok_class_token"]))
    put("bias_q", chunks(g["L1_attn_bias_q"]))
    put("k_b", chunks(g["L1_attn_k_b"]))
    put("out_b", chunks(g["L1_attn_out_b"]))
    put("gn_w", chunks(g["L0_attn_gn_w"]))
    put("gn_b", chunks(g["L0_attn_gn_b"]))
    put("mag_q", g["L1_attn_mag_q"])
    put("mag_v", g["L1_attn_mag_v"])
    even = (np.arange(128) // HD2 % 2 == 0).astype(np.float32)[:, None]
    put("even", even)
    put("odd", 1 - even)
    rows = np.broadcast_to(np.concatenate([g["L0_attn_ba"], g["L1_attn_bias_v"]])[None], (128, 16 + D))
    lora = np.concatenate([g["L1_attn_A_q"], g["L1_attn_B_q"].T, g["L1_attn_A_v"], g["L1_attn_B_v"].T], 1)
    out = {
        "cst": f, "csb": b, "vec": vec, "rows": rows, "lora": lora,
        "pos": feat(g["L0_tok_position_embeddings"][0].T),
        "patches": feat(x), "wlin": feat(g["L0_tok_W_lin"].T),
        "wa": feat(g["L0_attn_Wa"]),
        "dora0": feat(g["L1_attn_dir_q"].T), "dora1": feat(g["L1_attn_dir_v"].T),
        "pieces": np.concatenate([part(g, *name).reshape(128, -1) for name, _ in PIECES], 1),
        "mlp": np.concatenate([w for e in range(E3) for w in (
            feat(g["L1_ffn_w1"][e]).reshape(128, -1),
            g["L1_ffn_w2"][e].reshape(4, 128, D).transpose(1, 0, 2).reshape(128, -1))], 1),
        "gate1": feat(g["L0_ffn_w_gate"]),
        "k2": feat(g["L1_attn_k_w"].T), "out2": feat(g["L1_attn_out_w"].T),
        "choice": feat(g["L1_ffn_choice_w"].T),
    }
    return {k: np.ascontiguousarray(v) for k, v in out.items()}


def kernel(**inputs):
    import concourse.bacc as bacc
    from concourse.bass_utils import run_bass_kernel_spmd

    nc = bacc.Bacc("TRN2", target_bir_lowering=False, num_devices=1)
    arrays = lay_out(inputs)
    io = {n: nc.dram_tensor(f"in_{n}", a.shape, mybir.dt.from_np(a.dtype), kind="ExternalInput").ap()
          for n, a in arrays.items()}
    io["out"] = nc.dram_tensor("out_t", (D, T), F32, kind="ExternalOutput").ap()
    build(nc, io)
    r = run_bass_kernel_spmd(nc, [{f"in_{n}": a for n, a in arrays.items()}], core_ids=[0])
    return r.results[0]["out_t"].reshape(D, B, S).transpose(1, 2, 0)
```

```python
from contextlib import ExitStack

import numpy as np
import concourse.bass as bass
from concourse import mybir

F32 = mybir.dt.float32
F32R = mybir.dt.float32r
BF16 = mybir.dt.bfloat16
I32 = mybir.dt.int32
ALU = mybir.AluOpType
ACT = mybir.ActivationFunctionType
AXX = mybir.AxisListType.X

B, S, D = 16, 38, 256
T = B * S
HB, HT = B // 2, T // 2
NP = 36
KC = D // 128
FC0 = 6
GMAX = 114
H0, C0 = 16, 8
H1, E0, C1 = 8, 8, 4
H2, HD2 = 16, 16
SG = ((0, 128), (128, 128), (256, 128), (384, 128), (512, 96))
E3, F3, CAP = 8, 512, S * 2 // 8
GRP = ((0, 114), (114, 114), (304, 114), (418, 114), (228, 76), (532, 76))
BY_HALF = (0, 1, 4, 2, 3, 5)
RING = 4
RAW, SPLIT, PIECE = 3, 5, 1024
NX = 20500
NACT = 4 * T
EPS = 1e-5

VEC = dict(b_lin=(0, 2), cls=(2, 2), class_tok=(4, 2), bias_q=(6, 2), k_b=(8, 2), out_b=(10, 2),
           gn_w=(12, 8), gn_b=(20, 8), mag_q=(28, 1), mag_v=(29, 1), even=(30, 1), odd=(31, 1))
NVEC = 32
CST = dict(ident=(0, 128), mean=(128, 128), ones=(256, 128), gn_block=(384, 128), after=(512, 128),
           neg_upto=(640, 128), pos_of=(768, S), image_of=(806, 6 * B), iota=(902, CAP), desc=(911, E0),
           position=(919, S))
NCST = 957
CSB = dict(ident=(0, 128), causal_t=(128, 4 * GMAX), causal_t2=(584, 4 * 76), causal=(888, 4 * GMAX),
           causal2=(1344, 4 * 76), same_pos=(1648, 512), other_image=(2160, 128), select=(2288, 4096))
NCSB = 6384


def psum_order():
    out = []
    add = lambda reader, *name: out.append((name, reader))
    halves = (0, 1)

    def norm(n):
        for hf in halves:
            add("dve", "mean", n, hf)
        for hf in halves:
            add("act", "var", n, hf)

    for hf in halves:
        for mc in range(KC):
            add("dve", "tok", hf, mc)
    norm(0)
    add("dve", "la")
    for c in range(C0 + 1):
        if c < C0:
            if c % 4 == 0:
                for gi in range(6):
                    add("dve", "v0", c // 4, gi)
            for name in ("q0", "k0"):
                for hf in halves:
                    add("dve", name, c, hf)
            for i in range(3):
                add("act", "decay", c, i)
        if c >= 1:
            for hf in halves:
                add("act", "pv0", c - 1, hf)
        if c < C0:
            for i in range(4):
                add("dve", "score0", c, i)
            for hf in halves:
                add("act", "g0", c, hf)
        if c >= 1:
            add("dve", "gn", c - 1)
    for w in range(2):
        for kc in range(KC):
            add("dve", "dora", w, kc)
    norm(1)
    add("dve", "fro")
    add("act", "gate1")

    def scores1(c):
        for name in ("q1", "k1"):
            for hf in halves:
                add("act", name, c, hf)
        for i in range(4):
            add("dve", "score1", c, i)

    scores1(0)
    for hf in halves:
        add("act", "onehot_t", hf)
    def values1(c, eq):
        for gi in range(6):
            add("dve", "val", c, eq, gi)

    values1(0, 0)
    for c in range(C1):
        values1(c, 1)
        for i in range(3):
            add("act", "pt1", c, i)
        if c + 1 < C1:
            scores1(c + 1)
        for hf in halves:
            add("act", "pv1", c, hf)
        for e in range(E0):
            for hf in halves:
                add("act", "sel", c, e, hf)
            if e == 2 and c + 1 < C1:
                values1(c + 1, 0)
    norm(2)
    for hf in halves:
        for mc in range(KC):
            add("act", "q2", hf, mc)
            add("act", "k2", hf, mc)
    for sg in range(5):
        add("dve", "v2", sg)
    for part in range(2):
        for j in range(4):
            add("dve", "score2", j, part)
    for sg in range(5):
        for qd in range(SG[sg][1] // 32):
            add("dve", "pv2", sg, qd)
    for sg in range(5):
        add("act", "o2t", sg)
    for hf in halves:
        for mc in range(KC):
            add("dve", "out2", hf, mc)
    norm(3)
    add("dve", "route")
    for g2 in range(3):
        add("act", "x_tok", g2)
    add("dve", "probs_t")
    add("dve", "rank_t")
    for g in range(6):
        add("dve", "gather", g)
    for hf in halves:
        add("act", "scatter_t", hf)
    for e in range(E3 + 1):
        if e < E3:
            for f2 in range(2):
                add("act", "hid", e, f2)
        if e >= 1:
            add("dve", "y", e - 1)
    for b2 in range(8):
        add("act", "y_tok", b2)
    for hf in halves:
        for mc in range(KC):
            add("dve", "res3", hf, mc)
    return out


PSUM_TILES = psum_order()
TILE_NO = {name: i for i, (name, _) in enumerate(PSUM_TILES)}
READ_NO = {}
_counts = {"act": 0, "dve": 0}
for _name, _reader in PSUM_TILES:
    _counts[_reader] += 1
    READ_NO[_name] = (_reader, _counts[_reader])


def pieces():
    out = []
    for c in range(C0):
        if c % 4 == 0:
            out.append((("v0", c // 4), KC * 512))
        out.append((("qkgo", c), 3 * KC * 128 + D))
    out += [(("qk1", 0), 2 * KC * 128), (("val", 0, 0), KC * 4 * 128)]
    for c in range(C1):
        out.append((("val", c, 1), KC * 4 * 128))
        if c + 1 < C1:
            out += [(("qk1", c + 1), 2 * KC * 128), (("val", c + 1, 0), KC * 4 * 128)]
        out += [(("oexp", c, eq), 4 * D) for eq in range(2)]
    return out


PIECES = pieces()
PIECE_NO = {name: n for n, (name, _) in enumerate(PIECES)}
FIRST_AT = [sum(w for _, w in PIECES[:n]) for n in range(len(PIECES) + 1)]
SPLITS0 = {0: (), 1: (5,), 2: (), 3: (6,), 4: (7,), 5: (8,), 6: (9, 10), 7: (11,), 8: (12,), 9: (13,)}
SPLITS1 = {0: {-1: (16, 17, 18), 3: (19,), 6: (20,), 7: (21,)}, 1: {-1: (22, 23), 3: (24,), 6: (25,), 7: (26,)},
           2: {-1: (27, 28), 3: (29,)}, 3: {}}


def build(nc, io):
    with ExitStack() as ctx:
        def sem(name):
            return ctx.enter_context(nc.semaphore(name))

        def sb(name, shape, dt=F32):
            return ctx.enter_context(nc.sbuf_tensor(name, shape, dt))

        h = sb("h", [128, KC, T])
        hn = sb("hn", [128, KC, T])
        hn_hi = sb("hn_hi", [128, KC, T], F32R)
        hn_lo = sb("hn_lo", [128, KC, T], F32R)
        raw = sb("raw", [128, RAW, PIECE])
        w_hi = sb("w_hi", [128, SPLIT, PIECE], F32R)
        w_lo = sb("w_lo", [128, SPLIT, PIECE], F32R)
        act_hi = sb("act_hi", [128, NACT], F32R)
        act_lo = sb("act_lo", [128, NACT], F32R)
        cst = sb("cst", [128, NCST])
        csb_bits = sb("csb", [128, NCSB], mybir.dt.uint16)
        csb = csb_bits[:, :].bitcast(BF16)
        vec = sb("vec", [128, NVEC])
        rows = sb("rows", [128, 16 + 256])
        tokadd = sb("tokadd", [128, KC, S])
        eps_col = sb("eps_col", [128, 1])
        one_col = sb("one_col", [128, 1])
        ln_one = sb("ln_one", [128, 1])
        after = sb("after", [128, 128], F32R)
        kb_even_odd = sb("kb_even_odd", [128, 2, KC])
        half_b = sb("half_b", [128, C0])
        minus_half = sb("minus_half", [128, B])
        exponents = sb("exponents", [128, 4])
        region_x = sb("region_x", [128, NX])
        small_w = sb("small_w", [128, 128 + 32 + 4 * 512 + 16])

        ident = cst[:, 0:128]

        def const(name):
            o, n = CST[name]
            return cst[:, o:o + n]

        def constb(name):
            o, n = CSB[name]
            return csb[:, o:o + n]

        def col(name, i=0):
            o = VEC[name][0] + i
            return vec[:, o:o + 1]

        def cols(name):
            o, n = VEC[name]
            return vec[:, o:o + n]

        class Cut:
            def __init__(self, region, at=0):
                self.region, self.at = region, at

            def __call__(self, n, pattern=None, dt=None, **sizes):
                piece = self.region[:, self.at:self.at + n]
                self.at += n
                if dt is not None:
                    piece = piece.bitcast(dt)
                return piece.rearrange(pattern, **sizes) if pattern else piece

        cut = Cut(small_w)
        wgate1 = cut(128, "p (k n) -> p k n", k=KC)
        wa0 = cut(32, "p (k n) -> p k n", k=KC)
        dora_w = [cut(512, "p (k n) -> p k n", k=KC) for _ in range(2)]
        wk2, wout2 = (cut(512, "p (k n) -> p k n", k=KC) for _ in range(2))
        choice3 = cut(16, "p (k n) -> p k n", k=KC)

        cut = Cut(region_x)
        hc, sq = (cut(2 * KC * HT, "p (f k n) -> p f k n", f=2, k=KC) for _ in range(2))
        rstd, log_var = (cut(2 * HT, "p (f n) -> p f n", f=2) for _ in range(2))
        patches = cut(FC0 * B * NP, "p (k n) -> p k n", k=FC0)
        wlin = cut(FC0 * D, "p (k n) -> p k n", k=FC0)
        cut = Cut(region_x)
        q0, k0 = ([cut(T) for _ in range(2)] for _ in range(2))
        tanh_qk = [cut(HT) for _ in range(4)]
        tanh_g = [cut(T) for _ in range(3)]
        osb = [cut(T) for _ in range(2)]
        gsq = cut(T)

        def by_group(piece):
            return (piece[:, 0:4 * GMAX], piece[:, 4 * GMAX:8 * GMAX], piece[:, 8 * GMAX:8 * GMAX + 4 * 76])

        steps = [by_group(a[:, 2 * T:2 * T + 1216]) for a in (act_hi, act_lo)]
        decay = by_group(cut(1216))
        att = by_group(cut(1216))
        v0 = [cut(6 * 512, "p (g n) -> p g n", g=6) for _ in range(2)]
        la, la_abs, la_exp, la_ln, la_hi, la_lo = (cut(96, "p (g n) -> p g n", g=6) for _ in range(6))
        gsum, gmean = cut(32), cut(32)
        gvar, gstd, gtmp = (cut(16) for _ in range(3))
        gscale, gshift = ([cut(16) for _ in range(2)] for _ in range(2))
        lora = region_x[0:8, cut.at:cut.at + 4 * D]
        cut(4 * D)
        junk = gsq[:, 0:D]
        assert cut.at <= NX
        fro = sb("fro", [128, 16])
        cut = Cut(region_x)
        q1, k1 = ([cut(T) for _ in range(2)] for _ in range(2))
        prob1 = [by_group(cut(1216)) for _ in range(2)]
        prob1t = by_group(cut(1216))
        vals = [cut(6 * 128, "p (g n) -> p g n", g=6) for _ in range(2)]
        gout, gout_hi, gout_lo = cut(T), cut(T), cut(T)
        gate, onehot, ohwork = (cut(6 * 64, "p (g n) -> p g n", g=6) for _ in range(3))
        gmax, ohmax = (cut(48, "p (g n) -> p g n", g=6) for _ in range(2))
        negmax1, sum1 = cut(32), [cut(16) for _ in range(2)]
        onehot_t = cut(T // 2, dt=BF16)
        chosen = [cut(T) for _ in range(3)]
        cut = Cut(region_x)
        q2, keven, kodd, o2t = (cut(KC * T, "p (k n) -> p k n", k=KC) for _ in range(4))
        v2 = cut(5 * H2 * 17, "p (g h n) -> p g h n", g=5, h=H2)
        prob2 = [[cut(n) for _ in range(4)] for n in (512, 128)]
        prob2t = [[cut(n) for _ in range(4)] for n in (512, 128)]
        o2 = cut(5 * D, "p (g n) -> p g n", g=5)
        rden2 = cut(5 * H2, "p (g n) -> p g n", g=5)
        negmax2 = cut(128)
        assert cut.at <= NX
        cut = Cut(region_x)
        probs = cut(6 * E3, "p (g n) -> p g n", g=6)
        pwork = cut(6 * E3, "p (g n) -> p g n", g=6)
        psum3 = cut(6, "p (g n) -> p g n", g=6)
        pspread = cut(6 * 128, "p (g n) -> p g n", g=6)
        pt = cut(2 * GMAX)
        above_space = region_x[:, cut.at:cut.at + 2 * S * S]
        above = cut(S * S, "p (a b) -> p a b", a=S)
        equal = cut(S * S, "p (a b) -> p a b", a=S)
        ptt = cut(256)
        pick = cut(B * E3 * CAP)
        pickw = cut(B * E3 * CAP)
        y_tok = cut(B * D, "p (b n) -> p b n", b=B)
        x_tok = y_tok.rearrange("p b n -> p (b n)")[:, 0:6 * D].rearrange("p (g n) -> p g n", g=6)
        y_t = cut(KC * B * E3 * CAP, "p (k b e c) -> p k b e c", k=KC, b=B, e=E3)
        scatter_t = cut(T)
        hid = [cut(4 * B * CAP) for _ in range(2)]
        res = cut(2 * HT * KC, "p (k n) -> p k n", k=KC)
        before = cut(S * S, "p (a b) -> p a b", a=S)
        assert cut.at <= NX
        x_in = above_space[:, 0:KC * E3 * B * CAP].rearrange("p (k e b c) -> p k e b c", k=KC, e=E3, b=B)
        w_mlp = [cut(PIECE) for _ in range(3)] + [raw[:, i, :] for i in range(RAW)]
        assert cut.at <= NX

        ring = [ctx.enter_context(nc.psum_tensor(f"ring{i}", [128, 512], F32)) for i in range(RING)]
        acc = [[ctx.enter_context(nc.psum_tensor(f"acc{i}{hf}", [128, 512], F32)) for hf in range(2)]
               for i in range(KC)]

        loaded = {n: sem(f"loaded_{n}") for n in (
            "cst", "csb", "vec", "rows", "pos", "wlin", "wa", "lora", "dora0", "dora1",
            "gate1", "k2", "out2", "choice")}
        patches_loaded = [sem(f"patches_loaded{hf}") for hf in range(2)]
        piece_loaded = [sem(f"piece_loaded{i}") for i in range(RAW)]
        mlp_loaded = [sem(f"mlp_loaded{i}") for i in range(6)]
        hi_done = sem("hi_done")
        lo_done = sem("lo_done")
        hn_hi_done = sem("hn_hi_done")
        hn_lo_done = sem("hn_lo_done")
        tiles_filled = sem("tiles_filled")
        act_evac = sem("act_evac")
        dve_evac = sem("dve_evac")
        consts_set = sem("consts_set")
        tok_added = sem("tok_added")
        rstd_done = sem("rstd_done")
        squared = sem("squared")
        normed = sem("normed")
        dve_step = sem("dve_step")
        act_step = sem("act_step")
        pool_step = sem("pool_step")
        la_abs_done = sem("la_abs_done")
        la_ln_done = sem("la_ln_done")
        la_done = sem("la_done")
        tanh_done = sem("tanh_done")
        steps_done = sem("steps_done")
        gsq_done = sem("gsq_done")
        gsq_read = sem("gsq_read")
        gvar_done = sem("gvar_done")
        gscale_done = sem("gscale_done")
        gn_scaled = sem("gn_scaled")
        gn_shifted = sem("gn_shifted")
        gn_gated = sem("gn_gated")
        og_hi_done = sem("og_hi_done")
        og_lo_done = sem("og_lo_done")
        wo_mms = sem("wo_mms")
        wo_added = sem("wo_added")
        onehot_done = sem("onehot_done")
        exp1_done = sem("exp1_done")
        scale1_done = sem("scale1_done")
        prob1_done = sem("prob1_done")
        vals_done = sem("vals_done")
        gout_split = sem("gout_split")
        masked_dve = sem("masked_dve")
        masked_pool = sem("masked_pool")
        expert_mms = sem("expert_mms")
        experts_added = sem("experts_added")
        dora_done = sem("dora_done")
        dora_sq = sem("dora_sq")
        fro_done = sem("fro_done")
        exp2_done = sem("exp2_done")
        prob2t_done = sem("prob2t_done")
        exp3_done = sem("exp3_done")
        shifted3 = sem("shifted3")
        probs_done = sem("probs_done")
        spread_done = sem("spread_done")
        rank_done = sem("rank_done")
        pick_done = sem("pick_done")
        pickw_done = sem("pickw_done")
        stored = sem("stored")
        gout_hi_done = sem("gout_hi_done")
        after_set = sem("after_set")
        la_hi_done = sem("la_hi_done")
        la_lo_done = sem("la_lo_done")
        vals_begun = sem("vals_begun")
        before_set = sem("before_set")

        def filled(*name):
            return TILE_NO[name] + 1

        def evacuated(*name):
            return READ_NO[name][1]

        def bank(*name):
            return ring[TILE_NO[name] % RING]

        def last_use(n):
            name = PIECES[n][0]
            kind, i = name[0], name[1]
            if kind == "qkgo":
                return wo_mms, i + 1
            if kind == "oexp":
                return expert_mms, E0 * i + 4 * name[2] + 4
            last = {"v0": ("v0", i, 5), "qk1": ("k1", i, 1),
                    "val": ("val", *name[1:], 5)}[kind]
            return tiles_filled, filled(*last)

        def part1(parts, i):
            if i < 2:
                return parts[i][0:GMAX, :]
            return parts[2][0:76, 152 * (i - 2):152 * (i - 1)]

        def images(ap, n=HB):
            return ap.rearrange("p (b s) -> p b s", s=S)

        block = ctx.enter_context(nc.Block())

        @block.sync
        def _(sp):

            def load(name, dst):
                sp.dma_start(dst, io[name]).then_inc(loaded[name], 16)

            for hf in range(2):
                half = slice(hf * HB * NP, (hf + 1) * HB * NP)
                sp.dma_start(patches[:, :, half], io["patches"][:, :, half]).then_inc(patches_loaded[hf], 16)
            load("wa", wa0)
            for n, (_, width) in enumerate(PIECES):
                if n >= RAW:
                    sp.wait_ge(lo_done, n - RAW + 1)
                sp.dma_start(raw[:, n % RAW, 0:width],
                             io["pieces"][:, FIRST_AT[n]:FIRST_AT[n + 1]]).then_inc(piece_loaded[n % RAW], 16)
                if n == RAW - 1:
                    load("csb", csb_bits[:, :])
                elif n == 2 * RAW:
                    for name, dst in (("dora0", dora_w[0]), ("dora1", dora_w[1]), ("gate1", wgate1), ("k2", wk2),
                                      ("out2", wout2), ("choice", choice3)):
                        load(name, dst)
            for m in range(2 * E3):
                if m == 0:
                    sp.wait_ge(wo_added, 2)
                elif 3 <= m < 6:
                    sp.wait_ge(lo_done, max(n for n in range(len(PIECES)) if n % RAW == m - 3) + 1)
                elif m >= 6:
                    last = ("y", (m - 6) // 2) if m % 2 else ("hid", (m - 6) // 2, 1)
                    sp.wait_ge(tiles_filled, filled(*last))
                sp.dma_start(w_mlp[m % 6], io["mlp"][:, m * PIECE:(m + 1) * PIECE]).then_inc(mlp_loaded[m % 6], 16)
            for hf in range(2):
                sp.wait_ge(dve_evac, evacuated("res3", hf, KC - 1))
                for kc in range(KC):
                    sp.dma_start(io["out"][kc * 128:(kc + 1) * 128, hf * HT:(hf + 1) * HT],
                                 res[:, kc, hf * HT:(hf + 1) * HT]).then_inc(stored, 16)
            sp.wait_ge(stored, 16 * 2 * KC)

        @block.tensor
        def _(pe):
            mm = nc.tensor.matmul
            next_tile = [0]

            def open_tile(*name):
                n = next_tile[0]
                assert PSUM_TILES[n][0] == name, (PSUM_TILES[n], name)
                next_tile[0] += 1
                if n >= RING:
                    before_it, reader = PSUM_TILES[n - RING]
                    if reader == "act":
                        pe.wait_ge(act_evac, evacuated(*before_it))
                    else:
                        pe.wait_ge(dve_evac, evacuated(*before_it))
                return ring[n % RING]

            def norm(n):
                pe.wait_ge(loaded["cst"], 16)
                for hf in range(2):
                    if n == 0:
                        pe.wait_ge(tok_added, 1)
                        pe.wait_ge(dve_evac, evacuated("tok", hf, KC - 1))
                    elif n == 1:
                        pe.wait_ge(wo_added, hf + 1)
                    elif n == 2:
                        pe.wait_ge(experts_added, hf + 1)
                    else:
                        pe.wait_ge(dve_evac, evacuated("out2", 1, KC - 1))
                    p = open_tile("mean", n, hf)
                    for kc in range(KC):
                        last = mm(p[:, 0:HT], const("mean"), h[:, kc, hf * HT:(hf + 1) * HT],
                                  start=(kc == 0), stop=(kc == KC - 1))
                    last.then_inc(tiles_filled, 1)
                for hf in range(2):
                    pe.wait_ge(squared, 2 * n + hf + 1)
                    p = open_tile("var", n, hf)
                    for kc in range(KC):
                        last = mm(p[:, 0:HT], const("mean"), sq[:, hf, kc, :],
                                  start=(kc == 0), stop=(kc == KC - 1))
                    last.then_inc(tiles_filled, 1)

            def project(name, w, rhs, n_out=1):
                p = open_tile(*name)
                for kc in range(KC):
                    last = mm(p[:, 0:rhs.shape[2]], w[:, kc, :], rhs[:, kc, :],
                              start=(kc == 0), stop=(kc == KC - 1))
                last.then_inc(tiles_filled, 1)

            pe.wait_ge(loaded["wlin"], 16)
            for hf in range(2):
                pe.wait_ge(patches_loaded[hf], 16)
                for mc in range(KC):
                    p = open_tile("tok", hf, mc)
                    for fc in range(FC0):
                        last = mm(p[:, 0:HB * NP], wlin[:, fc, mc * 128:(mc + 1) * 128],
                                  patches[:, fc, hf * HB * NP:(hf + 1) * HB * NP],
                                  start=(fc == 0), stop=(fc == FC0 - 1))
                    last.then_inc(tiles_filled, 1)
            norm(0)
            def three(out, w, x, cols_w, cols_x, start, stop):
                mm(out, w[0][cols_w], x[0][cols_x], start=start, stop=False)
                mm(out, w[0][cols_w], x[1][cols_x], start=False, stop=False)
                return mm(out, w[1][cols_w], x[0][cols_x], start=False, stop=stop)

            hn2 = (hn_hi, hn_lo)

            def piece(*name):
                n = PIECE_NO[name]
                pe.wait_ge(lo_done, n + 1)
                return w_hi[:, n % SPLIT, :], w_lo[:, n % SPLIT, :]

            def project2(name, w, at):
                hf = name[-1]
                p = open_tile(*name)
                for kc in range(KC):
                    last = three(p[:, 0:HT], w, hn2, (slice(None), slice(at + 128 * kc, at + 128 * kc + 128)),
                                 (slice(None), kc, slice(hf * HT, (hf + 1) * HT)), kc == 0, kc == KC - 1)
                last.then_inc(tiles_filled, 1)

            pe.wait_ge(loaded["wa"], 16)
            p = open_tile("la")
            for gi in BY_HALF:
                t0, n = GRP[gi]
                pe.wait_ge(normed, t0 // HT + 1)
                for kc in range(KC):
                    last = mm(p[0:n, gi * 16:gi * 16 + 16], hn[:, kc, t0:t0 + n], wa0[:, kc, :],
                              start=(kc == 0), stop=(kc == KC - 1))
            last.then_inc(tiles_filled, 1)
            pe.wait_ge(hn_lo_done, 2)
            pe.wait_ge(after_set, 1)

            def wo(c):
                w = piece("qkgo", c)
                pe.wait_ge(og_lo_done, c + 1)
                o = T * (c % 2)
                for mc in range(KC):
                    for hf in range(2):
                        last = three(acc[mc][hf][:, 0:HT], w, (act_hi, act_lo),
                                     (slice(None), slice(768 + 128 * mc, 896 + 128 * mc)),
                                     (slice(None), slice(o + hf * HT, o + (hf + 1) * HT)), c == 0, c == C0 - 1)
                last.then_inc(wo_mms, 1)

            for c in range(C0 + 3):
                if c < C0:
                    if c % 4 == 0:
                        w = piece("v0", c // 4)
                        for gi, (t0, r) in enumerate(GRP):
                            p = open_tile("v0", c // 4, gi)
                            for kc in range(KC):
                                tok = (slice(None), kc, slice(t0, t0 + r))
                                col512 = (slice(None), slice(512 * kc, 512 * kc + 512))
                                last = three(p[0:r, :], hn2, w, tok, col512, kc == 0, kc == KC - 1)
                            last.then_inc(tiles_filled, 1)
                    w = piece("qkgo", c)
                    for hf in range(2):
                        project2(("q0", c, hf), w, 0)
                    for hf in range(2):
                        project2(("k0", c, hf), w, 256)
                    pe.wait_ge(loaded["csb"], 16)
                    for i in range(3):
                        r = GMAX if i < 2 else 76
                        neg = constb("causal_t" if i < 2 else "causal_t2")
                        pe.wait_ge(steps_done, 3 * c + i + 1)
                        p = open_tile("decay", c, i)
                        for x in range(2):
                            mm(p[0:r, 0:4 * r], after[0:r, 0:r], steps[x][i][0:r, 0:4 * r],
                               start=(x == 0), stop=False)
                        mm(p[0:r, 0:4 * r], constb("ident")[0:r, 0:r], neg[0:r, :],
                           start=False, stop=True).then_inc(tiles_filled, 1)
                if c == C0 + 2:
                    pe.wait_ge(loaded["lora"], 16)
                    for w in range(2):
                        for kc in range(KC):
                            p = open_tile("dora", w, kc)
                            mm(p[:, 0:D], lora[:, (2 * w) * D + kc * 128:(2 * w) * D + (kc + 1) * 128],
                               lora[:, (2 * w + 1) * D:(2 * w + 2) * D], start=True, stop=True).then_inc(tiles_filled, 1)
                if c >= 3:
                    wo(c - 3)
                if 1 <= c <= C0:
                    l = c - 1
                    pe.wait_ge(dve_evac, evacuated("v0", l // 4, 5))
                    pe.wait_ge(dve_evac, evacuated("score0", l, 3))
                    for hf in range(2):
                        p = open_tile("pv0", l, hf)
                        for par in range(2):
                            for gi, (t0, r) in enumerate(GRP):
                                if t0 // HT == hf:
                                    big = gi < 4
                                    a = att[par] if big else att[2]
                                    o = (gi if big else 2 * par + gi - 4) * r
                                    hd = 128 * (l % 4) + 64 * par
                                    last = mm(p[64 * par:64 * par + 64, t0 - hf * HT:t0 - hf * HT + r],
                                              v0[l // 4][0:r, gi, hd:hd + 64], a[0:r, o:o + r],
                                              start=True, stop=True)
                        last.then_inc(tiles_filled, 1)
                if c < C0:
                    pe.wait_ge(dve_evac, evacuated("k0", c, 1))
                    for i in range(4):
                        par, small = i % 2, i // 2
                        p = open_tile("score0", c, i)
                        for x, (t0, r) in enumerate(GRP[4:] if small else GRP[:4]):
                            last = mm(p[0:r, x * r:(x + 1) * r], k0[c % 2][64 * par:64 * par + 64, t0:t0 + r],
                                      q0[c % 2][64 * par:64 * par + 64, t0:t0 + r], start=True, stop=True)
                        last.then_inc(tiles_filled, 1)
                    for hf in range(2):
                        project2(("g0", c, hf), w, 512)
                if 1 <= c <= C0:
                    pe.wait_ge(gsq_read, c)
                    p = open_tile("gn", c - 1)
                    mm(p[:, 0:32], const("gn_block"), gsum, start=True, stop=True).then_inc(tiles_filled, 1)
            norm(1)
            pe.wait_ge(dora_sq, 4)
            p = open_tile("fro")
            mm(p[:, 0:4], const("ones"), fro[:, 0:4], start=True, stop=True).then_inc(tiles_filled, 1)

            pe.wait_ge(loaded["gate1"], 16)
            p = open_tile("gate1")
            for gi in BY_HALF:
                t0, n = GRP[gi]
                pe.wait_ge(normed, 2 + t0 // HT + 1)
                for kc in range(KC):
                    last = mm(p[0:n, gi * 64:gi * 64 + 64], hn[:, kc, t0:t0 + n], wgate1[:, kc, :],
                              start=(kc == 0), stop=(kc == KC - 1))
            last.then_inc(tiles_filled, 1)
            pe.wait_ge(hn_lo_done, 4)

            def scores1(c):
                w = piece("qk1", c)
                for hf in range(2):
                    project2(("q1", c, hf), w, 0)
                for hf in range(2):
                    project2(("k1", c, hf), w, 256)
                pe.wait_ge(act_evac, evacuated("k1", c, 1))
                for i in range(4):
                    par, small = i % 2, i // 2
                    groups = GRP[4:] if small else GRP[:4]
                    r = groups[0][1]
                    n = len(groups) * r
                    neg = constb("causal2" if small else "causal")
                    p = open_tile("score1", c, i)
                    mm(p[0:r, 0:n], constb("ident")[0:r, 0:r], neg[0:r, 0:n], start=True, stop=True)
                    for x, (t0, r) in enumerate(groups):
                        last = mm(p[0:r, x * r:(x + 1) * r], q1[c % 2][64 * par:64 * par + 64, t0:t0 + r],
                                  k1[c % 2][64 * par:64 * par + 64, t0:t0 + r], start=False, stop=True,
                                  skip_group_check=True)
                    last.then_inc(tiles_filled, 1)

            def through_expert(c, e):
                w = piece("oexp", c, e // 4)
                i = E0 * c + e
                pe.wait_ge(masked_dve, i + 1)
                pe.wait_ge(masked_pool, i // 2 + 1)
                o = T * (i % 4)
                for mc in range(KC):
                    at = D * (e % 4) + 128 * mc
                    for hf in range(2):
                        last = three(acc[mc][hf][:, 0:HT], w, (act_hi, act_lo), (slice(None), slice(at, at + 128)),
                                     (slice(None), slice(o + hf * HT, o + (hf + 1) * HT)),
                                     i == 0, i == E0 * C1 - 1)
                last.then_inc(expert_mms, 1)

            def values1(c, eq):
                w = piece("val", c, eq)
                for gi, (t0, r) in enumerate(GRP):
                    p = open_tile("val", c, eq, gi)
                    for kc in range(KC):
                        last = three(p[0:r, :], hn2, w, (slice(None), kc, slice(t0, t0 + r)),
                                     (slice(None), slice(512 * kc, 512 * kc + 512)), kc == 0, kc == KC - 1)
                    last.then_inc(tiles_filled, 1)

            scores1(0)
            pe.wait_ge(onehot_done, 1)
            for hf in range(2):
                p = open_tile("onehot_t", hf)
                for gi, (t0, r) in enumerate(GRP):
                    if t0 // HT == hf:
                        o = t0 - hf * HT
                        last = nc.tensor.transpose(p[0:64, o:o + r], onehot[0:r, gi, :], ident[0:r, 0:r])
                last.then_inc(tiles_filled, 1)
            values1(0, 0)
            for c in range(C1):
                values1(c, 1)
                pe.wait_ge(prob1_done, 4 * c + 4)
                for i in range(3):
                    r = 76 if i == 2 else GMAX
                    p = open_tile("pt1", c, i)
                    for x in range(4):
                        last = nc.tensor.transpose(p[0:r, x * r:(x + 1) * r], prob1[c % 2][i][0:r, x * r:(x + 1) * r],
                                                   ident[0:r, 0:r])
                    last.then_inc(tiles_filled, 1)
                if c + 1 < C1:
                    scores1(c + 1)
                pe.wait_ge(vals_done, c + 1)
                pe.wait_ge(act_evac, evacuated("pt1", c, 2))
                for hf in range(2):
                    p = open_tile("pv1", c, hf)
                    for par in range(2):
                        for gi, (t0, r) in enumerate(GRP):
                            if t0 // HT == hf:
                                big = gi < 4
                                a = prob1t[par] if big else prob1t[2]
                                o = (gi if big else 2 * par + gi - 4) * r
                                last = mm(p[64 * par:64 * par + 64, t0 - hf * HT:t0 - hf * HT + r],
                                          vals[c % 2][0:r, gi, 64 * par:64 * par + 64], a[0:r, o:o + r],
                                          start=True, stop=True)
                    last.then_inc(tiles_filled, 1)
                pe.wait_ge(act_evac, evacuated("onehot_t", 1))
                for e in range(E0 + 3):
                    if e == 3:
                        if c + 1 < C1:
                            values1(c + 1, 0)
                        if c == 0:
                            pe.wait_ge(wo_added, 2)
                    if e >= 3:
                        through_expert(c, e - 3)
                    if e < E0:
                        sel = constb("select")[0:64, (e * C1 + c) * 128:(e * C1 + c + 1) * 128]
                        for hf in range(2):
                            p = open_tile("sel", c, e, hf)
                            mm(p[:, 0:HT], sel, onehot_t[0:64, hf * HT:(hf + 1) * HT],
                               start=True, stop=True).then_inc(tiles_filled, 1)
            norm(2)

            pe.wait_ge(normed, 6)
            pe.wait_ge(dora_done, 1)
            pe.wait_ge(loaded["k2"], 16)
            for hf in range(2):
                tok = hn[:, :, hf * HT:(hf + 1) * HT]
                for mc in range(KC):
                    project(("q2", hf, mc), dora_w[0][:, :, mc * 128:(mc + 1) * 128], tok)
                    project(("k2", hf, mc), wk2[:, :, mc * 128:(mc + 1) * 128], tok)
            for sg, (t0, r) in enumerate(SG):
                p = open_tile("v2", sg)
                for kc in range(KC):
                    last = mm(p[0:r, 0:D], hn[:, kc, t0:t0 + r], dora_w[1][:, kc, :],
                              start=(kc == 0), stop=(kc == KC - 1))
                last.then_inc(tiles_filled, 1)
            pe.wait_ge(act_evac, evacuated("k2", 1, KC - 1))
            for part in range(2):
                rows2, groups2 = (128, range(4)) if part == 0 else (96, range(4, 5))
                n = 128 * len(groups2)
                for j in range(4):
                    p = open_tile("score2", j, part)
                    mm(p[0:rows2, 0:n], constb("ident")[0:rows2, 0:rows2], constb("same_pos")[0:rows2, 0:n],
                       start=True, stop=True)
                    for sg in groups2:
                        for qd in range(SG[sg][1] // 32):
                            t0 = SG[sg][0] + 32 * qd
                            for x in range(4):
                                k = kodd if x % 2 else keven
                                o = 128 * (sg % 4) + 32 * x
                                last = mm(p[32 * qd:32 * qd + 32, o:o + 32],
                                          q2[32 * j:32 * j + 32, x // 2, t0:t0 + 32],
                                          k[32 * j:32 * j + 32, x // 2, t0:t0 + 32],
                                          start=False, stop=True, skip_group_check=True)
                    last.then_inc(tiles_filled, 1)
            pe.wait_ge(dve_evac, evacuated("v2", 4))
            for sg in range(5):
                part = sg // 4
                pe.wait_ge(prob2t_done, 4 * part + 4)
                for qd in range(SG[sg][1] // 32):
                    p = open_tile("pv2", sg, qd)
                    rows2 = slice(32 * qd, 32 * qd + 32)
                    for hd in range(H2):
                        j, x = hd % 8 // 2, 2 * (hd // 8) + hd % 2
                        o = 128 * (sg % 4) + 32 * x
                        last = mm(p[rows2, hd * 17:hd * 17 + 17], prob2t[part][j][rows2, o:o + 32],
                                  v2[rows2, sg, hd, :], start=True, stop=True)
                    last.then_inc(tiles_filled, 1)
            for sg, (t0, r) in enumerate(SG):
                pe.wait_ge(dve_evac, evacuated("pv2", sg, r // 32 - 1))
                p = open_tile("o2t", sg)
                for kc in range(KC):
                    last = nc.tensor.transpose(p[:, kc * r:(kc + 1) * r], o2[0:r, sg, kc * 128:(kc + 1) * 128],
                                               ident[0:r, 0:r])
                last.then_inc(tiles_filled, 1)
            pe.wait_ge(loaded["out2"], 16)
            pe.wait_ge(act_evac, evacuated("o2t", 4))
            for hf in range(2):
                for mc in range(KC):
                    project(("out2", hf, mc), wout2[:, :, mc * 128:(mc + 1) * 128],
                            o2t[:, :, hf * HT:(hf + 1) * HT])
            norm(3)

            pe.wait_ge(loaded["choice"], 16)
            p = open_tile("route")
            for gi in BY_HALF:
                t0, n = GRP[gi]
                pe.wait_ge(normed, 6 + t0 // HT + 1)
                for kc in range(KC):
                    last = mm(p[0:n, gi * E3:(gi + 1) * E3], hn[:, kc, t0:t0 + n], choice3[:, kc, :],
                              start=(kc == 0), stop=(kc == KC - 1))
            last.then_inc(tiles_filled, 1)
            for g2 in range(3):
                p = open_tile("x_tok", g2)
                for i in range(2):
                    t0, r = GRP[2 * g2 + i]
                    for kc in range(KC):
                        last = nc.tensor.transpose(p[0:r, i * D + kc * 128:i * D + (kc + 1) * 128],
                                                   hn[:, kc, t0:t0 + r], ident)
                last.then_inc(tiles_filled, 1)
            p = open_tile("probs_t")
            pe.wait_ge(spread_done, 1)
            for gi, (_, r) in enumerate(GRP):
                last = mm(p[:, 0:S], pspread[0:r, gi], const("pos_of")[0:r, :], start=(gi == 0), stop=(gi == 5))
            last.then_inc(tiles_filled, 1)
            pe.wait_ge(rank_done, 1)
            p = open_tile("rank_t")
            for i in range(2):
                mm(p[0:GMAX, i * 128:(i + 1) * 128], pt[:, i * GMAX:(i + 1) * GMAX], ident,
                   start=True, stop=(i == 0))
            mm(p[0:GMAX, 128:256], constb("ident")[0:GMAX, 0:GMAX], constb("other_image")[0:GMAX, :],
               start=False, stop=True).then_inc(tiles_filled, 1)
            pe.wait_ge(pick_done, 1)
            pe.wait_ge(act_evac, evacuated("x_tok", 2))
            for g, (t0, r) in enumerate(GRP):
                p = open_tile("gather", g)
                n = r // S * E3 * CAP
                at = t0 // S * E3 * CAP
                for kc in range(KC):
                    last = mm(p[:, kc * n:(kc + 1) * n], x_tok[0:r, g, kc * 128:(kc + 1) * 128],
                              pick[0:r, at:at + n], start=True, stop=True)
                last.then_inc(tiles_filled, 1)
            pe.wait_ge(pickw_done, 1)
            for hf in range(2):
                p = open_tile("scatter_t", hf)
                for g, (t0, r) in enumerate(GRP):
                    for b in range(t0 // S, (t0 + r) // S):
                        if t0 // HT == hf:
                            i = b - HB * hf
                            last = mm(p[0:72, i * S:(i + 1) * S], pickw[0:r, b * 72:(b + 1) * 72],
                                      const("pos_of")[0:r, :], start=True, stop=True)
                last.then_inc(tiles_filled, 1)
            pe.wait_ge(dve_evac, evacuated("gather", 5))
            n = B * CAP
            for e in range(E3 + 1):
                if e < E3:
                    m = 2 * e
                    pe.wait_ge(mlp_loaded[m % 6], 16 * (m // 6 + 1))
                    for f2 in range(2):
                        p = open_tile("hid", e, f2)
                        for i in range(2):
                            for kc in range(KC):
                                at = F3 * kc + 128 * (2 * f2 + i)
                                last = mm(p[:, i * n:(i + 1) * n], w_mlp[m % 6][:, at:at + 128], x_in[:, kc, e],
                                          start=(kc == 0), stop=(kc == KC - 1))
                        last.then_inc(tiles_filled, 1)
                if e >= 1:
                    m = 2 * e - 1
                    pe.wait_ge(mlp_loaded[m % 6], 16 * (m // 6 + 1))
                    pe.wait_ge(act_evac, evacuated("hid", e - 1, 1))
                    p = open_tile("y", e - 1)
                    for mc in range(KC):
                        for f in range(4):
                            at = D * f + 128 * mc
                            last = mm(p[:, mc * n:(mc + 1) * n], w_mlp[m % 6][:, at:at + 128],
                                      hid[(e - 1) % 2][:, f * n:(f + 1) * n], start=(f == 0), stop=(f == 3))
                    last.then_inc(tiles_filled, 1)
            pe.wait_ge(dve_evac, evacuated("y", E3 - 1))
            for b2 in range(8):
                p = open_tile("y_tok", b2)
                for i in range(2):
                    for kc in range(KC):
                        b = 2 * b2 + i
                        last = nc.tensor.transpose(p[0:72, i * D + kc * 128:i * D + (kc + 1) * 128],
                                                   y_t[:, kc, b, :, :].rearrange("p e c -> p (e c)"), ident)
                last.then_inc(tiles_filled, 1)
            pe.wait_ge(act_evac, evacuated("scatter_t", 1))
            for hf in range(2):
                pe.wait_ge(act_evac, evacuated("y_tok", 4 * hf + 3))
                for mc in range(KC):
                    p = open_tile("res3", hf, mc)
                    for i in range(HB):
                        b = HB * hf + i
                        last = mm(p[:, i * S:(i + 1) * S], y_tok[0:72, b, mc * 128:(mc + 1) * 128],
                                  scatter_t[0:72, b * S:(b + 1) * S], start=True, stop=True)
                    last.then_inc(tiles_filled, 1)

        @block.scalar
        def _(act):
            stepped = [0]
            A = nc.scalar.activation

            def load(name, dst):
                act.dma_start(dst, io[name]).then_inc(loaded[name], 16)

            load("wlin", wlin)
            load("vec", vec[:, :])
            load("pos", tokadd[:, :, 1:S])
            load("cst", cst[:, :])
            load("rows", rows[:, :])
            load("lora", lora)

            def norm(n):
                act.wait_ge(consts_set, 1)
                A(ln_one[:, :], one_col[:, :], ACT.Ln)
                for hf in range(2):
                    act.wait_ge(dve_evac, evacuated("mean", n, hf))
                    if n:
                        act.wait_ge(tiles_filled, filled("var", n - 1, hf))
                    A(sq[:, hf], hc[:, hf], ACT.Square).then_inc(squared, 1)
                for hf in range(2):
                    act.wait_ge(tiles_filled, filled("var", n, hf))
                    A(log_var[:, hf], bank("var", n, hf)[:, 0:HT], ACT.Ln, bias=eps_col[:, 0:1]).then_inc(act_evac, 1)
                for hf in range(2):
                    act.wait_ge(act_evac, evacuated("var", n, hf))
                    if n:
                        act.wait_ge(normed, 2 * (n - 1) + hf + 1)
                    A(rstd[:, hf], log_var[:, hf], ACT.Exp, scale=-0.5).then_inc(rstd_done, 1)

            def split(n):
                act.wait_ge(piece_loaded[n % RAW], 16 * (n // RAW + 1))
                if n >= SPLIT:
                    s, v = last_use(n - SPLIT)
                    act.wait_ge(s, v)
                width = PIECES[n][1]
                A(w_hi[:, n % SPLIT, 0:width], raw[:, n % RAW, 0:width], ACT.Copy).then_inc(hi_done, 1)

            def split_norm(n):
                for hf in range(2):
                    act.wait_ge(normed, 2 * n + hf + 1)
                    A(hn_hi[:, :, hf * HT:(hf + 1) * HT], hn[:, :, hf * HT:(hf + 1) * HT],
                      ACT.Copy).then_inc(hn_hi_done, 1)

            split(0)
            norm(0)
            split_norm(0)
            split(1)
            split(2)
            act.wait_ge(loaded["cst"], 16)
            A(after[:, :], const("after"), ACT.Copy).then_inc(after_set, 1)
            act.wait_ge(la_abs_done, 1)
            for r, a, b in ((GMAX, 0, 4), (76, 4, 6)):
                last = A(la_exp[0:r, a:b], la_abs[0:r, a:b], ACT.Exp, scale=-1.0)
            last.then_inc(act_step, 1)
            act.wait_ge(act_step, 1)
            for r, a, b in ((GMAX, 0, 4), (76, 4, 6)):
                last = A(la_ln[0:r, a:b], la_exp[0:r, a:b], ACT.Ln, bias=one_col[0:r, 0:1])
            last.then_inc(la_ln_done, 1)
            act.wait_ge(la_done, 1)
            for r, a, b in ((GMAX, 0, 4), (76, 4, 6)):
                last = A(la_hi[0:r, a:b].bitcast(F32R), la[0:r, a:b], ACT.Copy)
            last.then_inc(la_hi_done, 1)
            split(3)
            split(4)
            for c in range(C0 + 2):
                if c < C0:
                    for i in range(4):
                        name, hf = ("q0", "k0")[i // 2], i % 2
                        if c:
                            act.wait_ge(dve_evac, evacuated(name, c - 1, hf))
                        act.wait_ge(tiles_filled, filled(name, c, hf))
                        A(tanh_qk[i], bank(name, c, hf)[:, 0:HT], ACT.Tanh, scale=0.5).then_inc(tanh_done, 1)
                    for i in range(3):
                        r = GMAX if i < 2 else 76
                        if c:
                            act.wait_ge(dve_evac, evacuated("score0", c - 1, min(i + 1, 3) if i else 0))
                        act.wait_ge(tiles_filled, filled("decay", c, i))
                        A(decay[i][0:r, :], bank("decay", c, i)[0:r, 0:4 * r], ACT.Exp).then_inc(act_evac, 1)
                if 1 <= c <= C0:
                    for hf in range(2):
                        if c >= 3:
                            act.wait_ge(og_lo_done, c - 2)
                        act.wait_ge(tiles_filled, filled("pv0", c - 1, hf))
                        A(osb[(c - 1) % 2][:, hf * HT:(hf + 1) * HT], bank("pv0", c - 1, hf)[:, 0:HT],
                          ACT.Copy).then_inc(act_evac, 1)
                    act.wait_ge(act_evac, evacuated("pv0", c - 1, 1))
                    if c >= 2:
                        act.wait_ge(gsq_read, c - 1)
                    A(gsq, osb[(c - 1) % 2], ACT.Square).then_inc(gsq_done, 1)
                for n in SPLITS0[c]:
                    split(n)
                if c < C0:
                    for hf in range(2):
                        if c >= 3:
                            act.wait_ge(gn_gated, c - 2)
                        act.wait_ge(tiles_filled, filled("g0", c, hf))
                        A(tanh_g[c % 3][:, hf * HT:(hf + 1) * HT], bank("g0", c, hf)[:, 0:HT], ACT.Tanh,
                          scale=0.5).then_inc(act_evac, 1)
                if c >= 2:
                    l = c - 2
                    act.wait_ge(gn_gated, l + 1)
                    if l >= 2:
                        act.wait_ge(wo_mms, l - 1)
                    o = T * (l % 2)
                    A(act_hi[:, o:o + T], osb[l % 2], ACT.Copy).then_inc(og_hi_done, 1)
            act.wait_ge(dve_evac, evacuated("dora", 1, 1))
            for w in range(2):
                for kc in range(KC):
                    A(junk[:, :], dora_w[w][:, kc, :], ACT.Square,
                      accum_out=fro[:, 2 * w + kc:2 * w + kc + 1]).then_inc(dora_sq, 1)
                    act.wait_ge(dora_sq, 2 * w + kc + 1)
            norm(1)
            split_norm(1)
            split(14)
            act.wait_ge(tiles_filled, filled("gate1"))
            p = bank("gate1")
            for r, a, b in ((GMAX, 0, 4), (76, 4, 6)):
                last = A(gate[0:r, a:b, :], p[0:r, a * 64:b * 64].rearrange("p (g n) -> p g n", n=64), ACT.Sigmoid)
            last.then_inc(act_evac, 1)

            def scores1(c):
                for name, dst in (("q1", q1), ("k1", k1)):
                    for hf in range(2):
                        act.wait_ge(tiles_filled, filled(name, c, hf))
                        A(dst[c % 2][:, hf * HT:(hf + 1) * HT], bank(name, c, hf)[:, 0:HT],
                          ACT.Copy).then_inc(act_evac, 1)
                for i in range(4):
                    pr = part1(prob1[c % 2], i)
                    act.wait_ge(dve_evac, evacuated("score1", c, i))
                    A(pr, pr, ACT.Exp, scale=64 ** -0.5).then_inc(exp1_done, 1)

            def begin_values1(c):
                for gi, (_, r) in enumerate(GRP):
                    act.wait_ge(tiles_filled, filled("val", c, 0, gi))
                    A(vals[c % 2][0:r, gi, :], bank("val", c, 0, gi)[0:r, 0:128], ACT.Copy).then_inc(vals_begun, 1)

            scores1(0)
            for hf in range(2):
                act.wait_ge(tiles_filled, filled("onehot_t", hf))
                A(onehot_t[0:64, hf * HT:(hf + 1) * HT], bank("onehot_t", hf)[0:64, 0:HT],
                  ACT.Copy).then_inc(act_evac, 1)
            begin_values1(0)
            split(15)
            for c in range(C1):
                for i in range(3):
                    r = GMAX if i < 2 else 76
                    if c:
                        act.wait_ge(tiles_filled, filled("pv1", c - 1, 1))
                    act.wait_ge(tiles_filled, filled("pt1", c, i))
                    A(prob1t[i][0:r, :], bank("pt1", c, i)[0:r, 0:4 * r], ACT.Copy).then_inc(act_evac, 1)
                if c + 1 < C1:
                    scores1(c + 1)
                for hf in range(2):
                    if c:
                        act.wait_ge(gout_split, c)
                    act.wait_ge(tiles_filled, filled("pv1", c, hf))
                    A(gout[:, hf * HT:(hf + 1) * HT], bank("pv1", c, hf)[:, 0:HT], ACT.Copy).then_inc(act_evac, 1)
                for e in range(E0):
                    i = E0 * c + e
                    if i >= 3:
                        act.wait_ge(masked_dve, i - 2)
                        act.wait_ge(masked_pool, (i - 3) // 2 + 1)
                    for hf in range(2):
                        act.wait_ge(tiles_filled, filled("sel", c, e, hf))
                        A(chosen[i % 3][:, hf * HT:(hf + 1) * HT], bank("sel", c, e, hf)[:, 0:HT],
                          ACT.Copy).then_inc(act_evac, 1)
                    if e == 2:
                        for n in SPLITS1[c].get(-1, ()):
                            split(n)
                        act.wait_ge(act_evac, evacuated("pv1", c, 1))
                        if c:
                            act.wait_ge(masked_dve, E0 * c)
                        A(gout_hi.bitcast(F32R), gout, ACT.Copy).then_inc(gout_hi_done, 1)
                        if c + 1 < C1:
                            begin_values1(c + 1)
                    for n in SPLITS1[c].get(e, ()):
                        split(n)
            norm(2)
            act.wait_ge(dora_done, 1)
            for hf in range(2):
                t0 = hf * HT
                for mc in range(KC):
                    act.wait_ge(tiles_filled, filled("q2", hf, mc))
                    p = bank("q2", hf, mc)
                    A(q2[:, mc, t0:t0 + HT], p[:, 0:HT], ACT.Identity, bias=col("bias_q", mc),
                      scale=fro[:, 8:9]).then_inc(act_evac, 1)
                    act.wait_ge(tiles_filled, filled("k2", hf, mc))
                    p = bank("k2", hf, mc)
                    A(keven[:, mc, t0:t0 + HT], p[:, 0:HT], ACT.Identity, bias=kb_even_odd[:, 0, mc:mc + 1],
                      scale=col("even"))
                    A(kodd[:, mc, t0:t0 + HT], p[:, 0:HT], ACT.Identity, bias=kb_even_odd[:, 1, mc:mc + 1],
                      scale=col("odd")).then_inc(act_evac, 1)
            for part in range(2):
                rows2, n = (128, 512) if part == 0 else (96, 128)
                for j in range(4):
                    act.wait_ge(dve_evac, evacuated("score2", j, part))
                    pr = prob2[part][j][0:rows2, 0:n]
                    A(pr, pr, ACT.Exp, scale=HD2 ** -0.5).then_inc(exp2_done, 1)
            for sg, (t0, r) in enumerate(SG):
                act.wait_ge(tiles_filled, filled("o2t", sg))
                p = bank("o2t", sg)
                A(o2t[:, :, t0:t0 + r], p[:, 0:2 * r].rearrange("p (k i) -> p k i", k=KC),
                  ACT.Copy).then_inc(act_evac, 1)
            norm(3)
            act.wait_ge(shifted3, 1)
            for r, a, b in ((GMAX, 0, 4), (76, 4, 6)):
                last = A(pwork[0:r, a:b, :], pwork[0:r, a:b, :], ACT.Exp)
            last.then_inc(exp3_done, 1)
            for g2 in range(3):
                r = GRP[2 * g2][1]
                act.wait_ge(tiles_filled, filled("x_tok", g2))
                A(x_tok[0:r, 2 * g2:2 * g2 + 2, :], bank("x_tok", g2)[0:r, :].rearrange("p (g n) -> p g n", g=2),
                  ACT.Copy).then_inc(act_evac, 1)
            for hf in range(2):
                act.wait_ge(tiles_filled, filled("scatter_t", hf))
                p = bank("scatter_t", hf)
                A(scatter_t[0:72, hf * HT:(hf + 1) * HT], p[0:72, 0:HT], ACT.Copy).then_inc(act_evac, 1)
            for e in range(E3):
                for f2 in range(2):
                    if e >= 2:
                        act.wait_ge(tiles_filled, filled("y", e - 2))
                    act.wait_ge(tiles_filled, filled("hid", e, f2))
                    n = 2 * B * CAP
                    A(hid[e % 2][:, n * f2:n * f2 + n], bank("hid", e, f2)[:, 0:n], ACT.Silu).then_inc(act_evac, 1)
            for b2 in range(8):
                act.wait_ge(tiles_filled, filled("y_tok", b2))
                p = bank("y_tok", b2)
                A(y_tok[0:72, 2 * b2:2 * b2 + 2, :], p[0:72, :].rearrange("p (b n) -> p b n", b=2),
                  ACT.Copy).then_inc(act_evac, 1)

        @block.vector
        def _(dve):
            V = nc.vector
            stepped = [0]

            def settle(ins):
                ins.then_inc(dve_step, 1)
                stepped[0] += 1
                dve.wait_ge(dve_step, stepped[0])

            def norm(n, position_major=False):
                for hf in range(2):
                    dve.wait_ge(tiles_filled, filled("mean", n, hf))
                    p = bank("mean", n, hf)
                    if n:
                        dve.wait_ge(normed, 2 * (n - 1) + hf + 1)
                        dve.wait_ge(squared, 2 * (n - 1) + hf + 1)
                    V.tensor_tensor(hc[:, hf], h[:, :, hf * HT:(hf + 1) * HT],
                                    p[:, 0:HT].unsqueeze(1).to_broadcast([128, KC, HT]),
                                    ALU.subtract).then_inc(dve_evac, 1)
                for hf in range(2):
                    dve.wait_ge(rstd_done, 2 * n + hf + 1)
                    dve.wait_ge(dve_evac, evacuated("mean", n, hf))
                    if position_major:
                        for kc in range(KC):
                            o = hn[:, kc, :].rearrange("p (s b) -> p b s", b=B)[:, hf * HB:(hf + 1) * HB, :]
                            last = V.tensor_tensor(o, images(hc[:, hf, kc]), images(rstd[:, hf]), ALU.mult)
                    else:
                        last = V.tensor_tensor(hn[:, :, hf * HT:(hf + 1) * HT], hc[:, hf],
                                               rstd[:, hf].unsqueeze(1).to_broadcast([128, KC, HT]), ALU.mult)
                    last.then_inc(normed, 1)

            dve.wait_ge(loaded["vec"], 16)
            dve.wait_ge(loaded["pos"], 16)
            V.tensor_copy(tokadd[:, :, 0:1], cols("cls").unsqueeze(2))
            V.tensor_tensor(tokadd[:, :, 1:2], tokadd[:, :, 1:2], cols("class_tok").unsqueeze(2), ALU.add)
            for kc in range(KC):
                last = V.tensor_scalar(tokadd[:, kc, 2:S], tokadd[:, kc, 2:S], col("b_lin", kc), None, ALU.add)
            settle(last)
            for kc in range(KC):
                last = V.tensor_copy(h[:, kc, :].rearrange("p (b s) -> p b s", s=S)[:, :, 0:2],
                                     tokadd[:, kc, 0:2].unsqueeze(1).to_broadcast([128, B, 2]))
            last.then_inc(tok_added, 1)
            dve.wait_ge(tok_added, 1)
            for hf in range(2):
                for mc in range(KC):
                    dve.wait_ge(tiles_filled, filled("tok", hf, mc))
                    p = bank("tok", hf, mc)
                    o = h[:, mc, :].rearrange("p (b s) -> p b s", s=S)[:, hf * HB:(hf + 1) * HB, 2:S]
                    V.tensor_tensor(o, p[:, 0:HB * NP].rearrange("p (b s) -> p b s", s=NP),
                                    tokadd[:, mc, 2:S].unsqueeze(1).to_broadcast([128, HB, NP]),
                                    ALU.add).then_inc(dve_evac, 1)
            dve.wait_ge(dve_evac, evacuated("tok", 1, KC - 1))
            norm(0)
            def split_norm(n):
                for hf in range(2):
                    half = slice(hf * HT, (hf + 1) * HT)
                    dve.wait_ge(hn_hi_done, 2 * n + hf + 1)
                    V.tensor_tensor(hn_lo[:, :, half], hn[:, :, half], hn_hi[:, :, half].bitcast(F32),
                                    ALU.subtract).then_inc(hn_lo_done, 1)

            split_norm(0)
            V.tensor_scalar(kb_even_odd[:, 0, :], cols("k_b"), col("even"), None, ALU.mult)
            V.tensor_scalar(kb_even_odd[:, 1, :], cols("k_b"), col("odd"), None, ALU.mult)
            V.tensor_scalar(half_b[:, :], cols("gn_b"), 0.5, None, ALU.mult)
            dve.wait_ge(loaded["rows"], 16)
            dve.wait_ge(tiles_filled, filled("la"))
            p = bank("la")
            both = ((GMAX, 0, 4), (76, 4, 6))
            for r, a, b in both:
                last = V.tensor_tensor(la[0:r, a:b, :], p[0:r, a * 16:b * 16].rearrange("p (g n) -> p g n", n=16),
                                       rows[0:r, 0:16].unsqueeze(1).to_broadcast([r, b - a, 16]), ALU.add)
            last.then_inc(dve_evac, 1)
            dve.wait_ge(dve_evac, evacuated("la"))
            for r, a, b in both:
                last = V.scalar_tensor_tensor(la_abs[0:r, a:b, :], la[0:r, a:b, :], -1.0, la[0:r, a:b, :],
                                              ALU.mult, ALU.max)
            last.then_inc(la_abs_done, 1)

            def v_tiles(quad, some=range(6)):
                for gi in some:
                    r = GRP[gi][1]
                    dve.wait_ge(tiles_filled, filled("v0", quad, gi))
                    V.tensor_copy(v0[quad][0:r, gi, :], bank("v0", quad, gi)[0:r, :]).then_inc(dve_evac, 1)

            v_tiles(0, range(2))
            dve.wait_ge(la_ln_done, 1)
            for r, a, b in both:
                last = V.scalar_tensor_tensor(la[0:r, a:b, :], la[0:r, a:b, :], 0.0, la_ln[0:r, a:b, :],
                                              ALU.max, ALU.add)
            last.then_inc(la_done, 1)

            v_tiles(0, range(2, 6))
            for c in range(C0 + 2):
                if c < C0:
                    if c == 4:
                        v_tiles(1)
                    for i in range(4):
                        name, hf = ("q0", "k0")[i // 2], i % 2
                        dst = (q0, k0)[i // 2][c % 2]
                        dve.wait_ge(tanh_done, 4 * c + i + 1)
                        V.scalar_tensor_tensor(dst[:, hf * HT:(hf + 1) * HT], tanh_qk[i], 1.0,
                                               bank(name, c, hf)[:, 0:HT], ALU.add, ALU.mult).then_inc(dve_evac, 1)
                if c >= 2:
                    l = c - 2
                    dve.wait_ge(gscale_done, l + 1)
                    o = osb[l % 2].rearrange("p (b s) -> p b s", s=S)
                    V.tensor_tensor(o, o, gscale[l % 2].unsqueeze(2).to_broadcast([128, B, S]),
                                    ALU.mult).then_inc(gn_scaled, 1)
                if 1 <= c <= C0:
                    l = c - 1
                    if l:
                        dve.wait_ge(tiles_filled, filled("gn", l - 1))
                    dve.wait_ge(act_evac, evacuated("pv0", l, 1))
                    V.tensor_reduce(gsum[:, 0:16], osb[l % 2].rearrange("p (b s) -> p b s", s=S), AXX, ALU.add)
                    dve.wait_ge(gsq_done, l + 1)
                    V.tensor_reduce(gsum[:, 16:32], gsq.rearrange("p (b s) -> p b s", s=S), AXX,
                                    ALU.add).then_inc(gsq_read, 1)
                if c < C0:
                    for i in range(4):
                        r = GMAX if i < 2 else 76
                        n = 4 * r if i < 2 else 2 * r
                        dve.wait_ge(act_evac, evacuated("decay", c, min(i, 2)))
                        if c:
                            dve.wait_ge(tiles_filled, filled("pv0", c - 1, 1))
                        dve.wait_ge(tiles_filled, filled("score0", c, i))
                        V.scalar_tensor_tensor(part1(att, i), bank("score0", c, i)[0:r, 0:n], 0.25,
                                               part1(decay, i), ALU.mult, ALU.mult).then_inc(dve_evac, 1)
                if c >= 2:
                    l = c - 2
                    dve.wait_ge(gn_shifted, l + 1)
                    if l < C0:
                        dve.wait_ge(act_evac, evacuated("g0", l, 1))
                    V.scalar_tensor_tensor(osb[l % 2], tanh_g[l % 3], 1.0, osb[l % 2], ALU.add,
                                           ALU.mult).then_inc(gn_gated, 1)
                if 1 <= c <= C0:
                    l = c - 1
                    dve.wait_ge(tiles_filled, filled("gn", l))
                    if l:
                        dve.wait_ge(gscale_done, l)
                    V.tensor_copy(gmean, bank("gn", l)[:, 0:32]).then_inc(dve_evac, 1)
                    dve.wait_ge(dve_evac, evacuated("gn", l))
                    settle(V.tensor_tensor(gvar, gmean[:, 0:16], gmean[:, 0:16], ALU.mult))
                    settle(V.tensor_tensor(gvar, gmean[:, 16:32], gvar, ALU.subtract))
                    V.tensor_scalar(gvar, gvar, 0.0, EPS, ALU.max, ALU.add).then_inc(gvar_done, 1)
                if c >= 2:
                    l = c - 2
                    o = T * (l % 2)
                    dve.wait_ge(og_hi_done, l + 1)
                    dve.wait_ge(gn_gated, l + 1)
                    V.tensor_tensor(act_lo[:, o:o + T], osb[l % 2], act_hi[:, o:o + T].bitcast(F32),
                                    ALU.subtract).then_inc(og_lo_done, 1)
            for w in range(2):
                dve.wait_ge(loaded[f"dora{w}"], 16)
                for kc in range(KC):
                    dve.wait_ge(tiles_filled, filled("dora", w, kc))
                    p = bank("dora", w, kc)
                    V.tensor_tensor(dora_w[w][:, kc, :], dora_w[w][:, kc, :], p[:, 0:D], ALU.add).then_inc(dve_evac, 1)
            dve.wait_ge(wo_mms, C0)
            for hf in range(2):
                for mc in range(KC):
                    hh = h[:, mc, hf * HT:(hf + 1) * HT]
                    last = V.tensor_tensor(hh, hh, acc[mc][hf][:, 0:HT], ALU.add)
                last.then_inc(wo_added, 1)
            dve.wait_ge(wo_added, 2)
            norm(1)
            split_norm(1)
            dve.wait_ge(tiles_filled, filled("fro"))
            p = bank("fro")
            V.tensor_copy(fro[:, 10:14], p[:, 0:4]).then_inc(dve_evac, 1)
            dve.wait_ge(dve_evac, evacuated("fro"))
            f2 = fro[:, 10:14].rearrange("p (w k) -> p w k", w=2)
            V.tensor_tensor(fro[:, 4:6], f2[:, :, 0], f2[:, :, 1], ALU.add).then_inc(fro_done, 1)

            dve.wait_ge(act_evac, evacuated("gate1"))
            for r, a, b in both:
                n = b - a
                eight = lambda t: t[0:r, a:b, :].rearrange("p g (h e) -> p (g h) e", e=E0)
                flat = lambda t: t[0:r, a:b, :].rearrange("p g n -> p (g n)")
                settle(V.tensor_reduce(flat(gmax), eight(gate), AXX, ALU.max))
                settle(V.tensor_tensor(eight(ohwork), eight(gate),
                                       flat(gmax).unsqueeze(2).to_broadcast([r, 8 * n, E0]), ALU.is_equal))
                settle(V.tensor_tensor(eight(ohwork), eight(ohwork),
                                       const("desc")[0:r, :].unsqueeze(1).to_broadcast([r, 8 * n, E0]), ALU.mult))
                settle(V.tensor_reduce(flat(ohmax), eight(ohwork), AXX, ALU.max))
                last = V.tensor_tensor(eight(onehot), eight(ohwork),
                                       flat(ohmax).unsqueeze(2).to_broadcast([r, 8 * n, E0]), ALU.is_equal)
            last.then_inc(onehot_done, 1)
            dve.wait_ge(onehot_done, 1)

            def scores1(c):
                for i in range(4):
                    r, n = (GMAX, 4) if i < 2 else (76, 2)
                    dve.wait_ge(tiles_filled, filled("score1", c, i))
                    p3 = bank("score1", c, i)[0:r, 0:n * r].rearrange("p (x j) -> p x j", x=n)
                    nm = negmax1[0:r, 4 * i:4 * i + n]
                    if c:
                        dve.wait_ge(dve_evac, evacuated("score1", c - 1, i))
                    settle(V.tensor_reduce(nm, p3, AXX, ALU.max, negate=True))
                    V.tensor_tensor(part1(prob1[c % 2], i).rearrange("p (x j) -> p x j", x=n), p3,
                                    nm.unsqueeze(2).to_broadcast([r, n, r]), ALU.add).then_inc(dve_evac, 1)

            def weights1(c, some=range(4)):
                for i in some:
                    r, n = (GMAX, 4) if i < 2 else (76, 2)
                    g0_, g1_ = (0, 4) if i < 2 else (4, 6)
                    dve.wait_ge(exp1_done, 4 * c + i + 1)
                    sm = sum1[c % 2][0:r, 4 * i:4 * i + n]
                    settle(V.tensor_reduce(sm, part1(prob1[c % 2], i).rearrange("p (x j) -> p x j", x=n),
                                           AXX, ALU.add))
                    settle(V.reciprocal(sm, sm))
                    V.tensor_tensor(sm, sm, gmax[0:r, g0_:g1_, 2 * c + i % 2], ALU.mult).then_inc(scale1_done, 1)

            def values1(c, eq, some=range(6)):
                for gi in some:
                    r = GRP[gi][1]
                    dve.wait_ge(tiles_filled, filled("val", c, eq, gi))
                    p = bank("val", c, eq, gi)
                    out = vals[c % 2][0:r, gi, :]
                    for e in range(4):
                        data = p[0:r, 128 * e:128 * e + 128]
                        if eq == 0 and e == 0:
                            dve.wait_ge(vals_begun, 6 * c + gi + 1)
                            continue
                        pick8 = onehot[0:r, gi, E0 * 2 * c + 4 * eq + e:E0 * (2 * c + 2):E0]
                        if e == 0:
                            dve.wait_ge(dve_evac, evacuated("val", c, 0, gi))
                        last = V.copy_predicated(out.rearrange("p (h k) -> p h k", h=2),
                                                 pick8.bitcast(I32).unsqueeze(2).to_broadcast([r, 2, 64]),
                                                 data.rearrange("p (h k) -> p h k", h=2))
                        if e < 3:
                            settle(last)
                    last.then_inc(dve_evac, 1)

            scores1(0)
            weights1(0)
            values1(0, 0)
            for c in range(C1):
                values1(c, 1)
                if c + 1 < C1:
                    scores1(c + 1)
                if c + 1 < C1:
                    values1(c + 1, 0, range(3))
                dve.wait_ge(gout_hi_done, c + 1)
                if c:
                    dve.wait_ge(masked_pool, E0 // 2 * c)
                V.tensor_tensor(gout_lo, gout, gout_hi, ALU.subtract).then_inc(gout_split, 1)
                for e in range(E0):
                    i = E0 * c + e
                    if e == 3 and c + 1 < C1:
                        values1(c + 1, 0, range(3, 6))
                    if i >= 4:
                        dve.wait_ge(expert_mms, i - 3)
                    o = T * (i % 4)
                    dve.wait_ge(gout_split, c + 1)
                    dve.wait_ge(act_evac, evacuated("sel", c, e, 1))
                    last = V.tensor_tensor(act_hi[:, o:o + T], gout_hi, chosen[i % 3], ALU.mult)
                    if e % 2:
                        last = V.tensor_tensor(act_lo[:, o:o + T], gout_lo, chosen[i % 3], ALU.mult)
                    last.then_inc(masked_dve, 1)
                    if 3 <= e < 7 and c + 1 < C1:
                        weights1(c + 1, (e - 3,))
            dve.wait_ge(expert_mms, E0 * C1)
            for hf in range(2):
                for mc in range(KC):
                    hh = h[:, mc, hf * HT:(hf + 1) * HT]
                    last = V.tensor_tensor(hh, hh, acc[mc][hf][:, 0:HT], ALU.add)
                last.then_inc(experts_added, 1)
            dve.wait_ge(experts_added, 2)
            norm(2, position_major=True)
            dve.wait_ge(dora_done, 1)
            dve.wait_ge(tiles_filled, filled("q2", 0, 0))
            V.memset(v2[:, :, :, 16:17], 1.0)
            for sg, (t0, r) in enumerate(SG):
                dve.wait_ge(tiles_filled, filled("v2", sg))
                p = bank("v2", sg)
                V.scalar_tensor_tensor(v2[0:r, sg, :, 0:16], p[0:r, 0:D].rearrange("p (h n) -> p h n", h=H2),
                                       fro[0:r, 9:10], rows[0:r, 16:16 + D].rearrange("p (h n) -> p h n", h=H2),
                                       ALU.mult, ALU.add).then_inc(dve_evac, 1)

            for part in range(2):
                rows2, n = (128, 512) if part == 0 else (96, 128)
                for j in range(4):
                    dve.wait_ge(tiles_filled, filled("score2", j, part))
                    p = bank("score2", j, part)
                    p3 = p[0:rows2, 0:n].rearrange("p (x j) -> p x j", j=32)
                    nm = negmax2[0:rows2, 16 * j + 64 * part:16 * j + 64 * part + n // 32]
                    settle(V.tensor_reduce(nm, p3, AXX, ALU.max, negate=True))
                    V.tensor_tensor(prob2[part][j][0:rows2, 0:n].rearrange("p (x j) -> p x j", j=32), p3,
                                    nm.unsqueeze(2).to_broadcast([rows2, n // 32, 32]), ALU.add).then_inc(dve_evac, 1)
                for j in range(4):
                    dve.wait_ge(exp2_done, 4 * part + j + 1)
                    V.transpose(prob2t[part][j][0:rows2, 0:n], prob2[part][j][0:rows2, 0:n]).then_inc(prob2t_done, 1)
            V.tensor_tensor(before, const("position").unsqueeze(2).to_broadcast([128, S, S]),
                            const("position").unsqueeze(1).to_broadcast([128, S, S]),
                            ALU.is_gt).then_inc(before_set, 1)
            for sg in range(5):
                for qd in range(SG[sg][1] // 32):
                    dve.wait_ge(tiles_filled, filled("pv2", sg, qd))
                    p = bank("pv2", sg, qd)
                    rows2 = slice(32 * qd, 32 * qd + 32)
                    p3 = p[rows2, 0:H2 * 17].rearrange("p (h n) -> p h n", n=17)
                    settle(V.reciprocal(rden2[rows2, sg, :], p3[:, :, 16]))
                    V.tensor_tensor(o2[rows2, sg, :].rearrange("p (h n) -> p h n", h=H2), p3[:, :, 0:16],
                                    rden2[rows2, sg, :].unsqueeze(2).to_broadcast([32, H2, 16]),
                                    ALU.mult).then_inc(dve_evac, 1)
            for hf in range(2):
                for mc in range(KC):
                    dve.wait_ge(tiles_filled, filled("out2", hf, mc))
                    p = bank("out2", hf, mc)
                    hh = h[:, mc, :].rearrange("p (b s) -> p s b", s=S)[:, 19 * hf:19 * hf + 19, :]
                    V.scalar_tensor_tensor(hh, p[:, 0:HT].rearrange("p (s b) -> p s b", b=B), col("out_b", mc), hh,
                                           ALU.add, ALU.add).then_inc(dve_evac, 1)
            dve.wait_ge(dve_evac, evacuated("out2", 1, KC - 1))
            norm(3)
            dve.wait_ge(tiles_filled, filled("route"))
            p = bank("route")
            for r, a, b in both:
                last = V.tensor_reduce(psum3[0:r, a:b, 0], p[0:r, a * E3:b * E3].rearrange("p (g n) -> p g n", n=E3),
                                       AXX, ALU.max)
            settle(last)
            for r, a, b in both:
                last = V.tensor_tensor(pwork[0:r, a:b, :], p[0:r, a * E3:b * E3].rearrange("p (g n) -> p g n", n=E3),
                                       psum3[0:r, a:b, :].to_broadcast([r, b - a, E3]), ALU.subtract)
                last.then_inc(*((dve_evac, 1) if a == 0 else (shifted3, 1)))
            dve.wait_ge(exp3_done, 1)
            for r, a, b in both:
                last = V.tensor_reduce(psum3[0:r, a:b, 0], pwork[0:r, a:b, :], AXX, ALU.add)
            settle(last)
            for r, a, b in both:
                last = V.reciprocal(psum3[0:r, a:b, :], psum3[0:r, a:b, :])
            settle(last)
            for r, a, b in both:
                last = V.tensor_tensor(probs[0:r, a:b, :], pwork[0:r, a:b, :],
                                       psum3[0:r, a:b, :].to_broadcast([r, b - a, E3]), ALU.mult)
            last.then_inc(probs_done, 1)
            dve.wait_ge(tiles_filled, filled("probs_t"))
            p = bank("probs_t")
            V.tensor_copy(pt[:, 0:GMAX].rearrange("p (i s) -> p i s", i=3),
                          p[:, 0:S].unsqueeze(1).to_broadcast([128, 3, S])).then_inc(dve_evac, 1)
            dve.wait_ge(dve_evac, evacuated("probs_t"))
            mine = pt[:, 0:S].unsqueeze(2).to_broadcast([128, S, S])
            other = pt[:, 0:S].unsqueeze(1).to_broadcast([128, S, S])
            V.tensor_tensor(above, other, mine, ALU.is_gt)
            settle(V.tensor_tensor(equal, other, mine, ALU.is_ge))
            dve.wait_ge(before_set, 1)
            settle(V.copy_predicated(above, before.bitcast(I32), equal))
            ranks = pt[:, GMAX:2 * GMAX].rearrange("p (i s) -> p i s", i=3)
            settle(V.tensor_reduce(ranks[:, 0], above, AXX, ALU.add))
            V.tensor_copy(ranks[:, 1:3], ranks[:, 0:1].to_broadcast([128, 2, S])).then_inc(rank_done, 1)
            dve.wait_ge(tiles_filled, filled("rank_t"))
            p = bank("rank_t")
            V.tensor_copy(ptt[0:GMAX, :], p[0:GMAX, 0:256]).then_inc(dve_evac, 1)
            dve.wait_ge(dve_evac, evacuated("rank_t"))
            V.tensor_tensor(pick[0:GMAX, :].rearrange("p (a c) -> p a c", c=CAP),
                            ptt[0:GMAX, 128:256].unsqueeze(2).to_broadcast([GMAX, 128, CAP]),
                            const("iota")[0:GMAX, :].unsqueeze(1).to_broadcast([GMAX, 128, CAP]),
                            ALU.is_equal).then_inc(pick_done, 1)
            for g, (t0, r) in enumerate(GRP):
                dve.wait_ge(tiles_filled, filled("gather", g))
                n = r // S * E3 * CAP
                b0, b1 = t0 // S, (t0 + r) // S
                for kc in range(KC):
                    last = V.tensor_copy(x_in[:, kc, :, b0:b1, :].rearrange("p e b c -> p b e c"),
                                         bank("gather", g)[:, kc * n:(kc + 1) * n]
                                         .rearrange("p (b e c) -> p b e c", b=b1 - b0, e=E3))
                last.then_inc(dve_evac, 1)
            for e in range(E3):
                dve.wait_ge(tiles_filled, filled("y", e))
                p = bank("y", e)
                V.tensor_copy(y_t[:, :, :, e, :], p[:, 0:2 * B * CAP].rearrange("p (k b c) -> p k b c", k=KC, b=B)
                              ).then_inc(dve_evac, 1)
            for hf in range(2):
                for mc in range(KC):
                    dve.wait_ge(tiles_filled, filled("res3", hf, mc))
                    p = bank("res3", hf, mc)
                    V.tensor_tensor(res[:, mc, hf * HT:(hf + 1) * HT], h[:, mc, hf * HT:(hf + 1) * HT], p[:, 0:HT],
                                    ALU.add).then_inc(dve_evac, 1)

        @block.gpsimd
        def _(pool):
            G = nc.gpsimd
            G.memset(eps_col[:, :], EPS)
            G.memset(one_col[:, :], 1.0).then_inc(consts_set, 1)
            pool.wait_ge(loaded["cst"], 16)

            G.memset(minus_half[:, :], -0.5)
            G.memset(exponents[:, 0:2], 0.5)
            G.memset(exponents[:, 2:4], -1.0).then_inc(consts_set, 1)
            pool.wait_ge(consts_set, 2)
            stepped = [0]

            def settle(ins):
                ins.then_inc(pool_step, 1)
                stepped[0] += 1
                pool.wait_ge(pool_step, stepped[0])

            def split(n):
                width = PIECES[n][1]
                pool.wait_ge(hi_done, n + 1)
                G.tensor_tensor(w_lo[:, n % SPLIT, 0:width], raw[:, n % RAW, 0:width],
                                w_hi[:, n % SPLIT, 0:width].bitcast(F32), ALU.subtract).then_inc(lo_done, 1)

            def decay_steps(c):
                if c >= 1:
                    pool.wait_ge(tiles_filled, filled("decay", c - 1, 2))
                for i in range(3):
                    r, g0, n, heads = (GMAX, 0, 4, (2 * c + i,)) if i < 2 else (76, 4, 2, (2 * c, 2 * c + 1))
                    upto = const("neg_upto")[0:r, 0:r].unsqueeze(1).to_broadcast([r, n, r])
                    for part, la_part in zip(steps, (la_hi, la_lo)):
                        for x, hd in enumerate(heads):
                            out = part[i][0:r, x * n * r:(x + 1) * n * r].rearrange("p (x i) -> p x i", x=n)
                            take = la_part[0:r, g0:g0 + n, hd].unsqueeze(2).to_broadcast([r, n, r])
                            last = G.tensor_tensor(out, take, upto, ALU.mult)
                    last.then_inc(steps_done, 1)

            for n in range(3):
                split(n)
            pool.wait_ge(la_hi_done, 1)
            for r, a, b in ((GMAX, 0, 4), (76, 4, 6)):
                last = G.tensor_tensor(la_lo[0:r, a:b], la[0:r, a:b], la_hi[0:r, a:b], ALU.subtract)
            last.then_inc(la_lo_done, 1)
            pool.wait_ge(la_lo_done, 1)
            decay_steps(0)
            split(3)
            split(4)
            for c in range(C0 + 2):
                if c + 1 < C0:
                    decay_steps(c + 1)
                if c >= 2:
                    l = c - 2
                    pool.wait_ge(gscale_done, l + 1)
                    pool.wait_ge(gn_scaled, l + 1)
                    o = osb[l % 2].rearrange("p (b s) -> p b s", s=S)
                    G.tensor_tensor(o, o, gshift[l % 2].unsqueeze(2).to_broadcast([128, B, S]),
                                    ALU.add).then_inc(gn_shifted, 1)
                for n in SPLITS0[c]:
                    split(n)
                if 1 <= c <= C0:
                    l = c - 1
                    pool.wait_ge(gvar_done, l + 1)
                    settle(G.tensor_tensor(gstd, gvar, minus_half[:, :], ALU.pow))
                    settle(G.tensor_scalar(gscale[l % 2], gstd, col("gn_w", l), 0.5, ALU.mult, ALU.mult))
                    settle(G.tensor_tensor(gtmp, gmean[:, 0:16], gscale[l % 2], ALU.mult))
                    settle(G.tensor_scalar(gtmp, gtmp, -1.0, None, ALU.mult))
                    G.tensor_scalar(gshift[l % 2], gtmp, half_b[:, l:l + 1], None, ALU.add).then_inc(gscale_done, 1)
            split(14)
            pool.wait_ge(fro_done, 1)
            settle(G.tensor_tensor(fro[:, 6:8], fro[:, 4:6], exponents[:, 0:2], ALU.pow))
            settle(G.tensor_scalar(fro[:, 6:8], fro[:, 6:8], 1e-8, None, ALU.add))
            settle(G.tensor_tensor(fro[:, 6:8], fro[:, 6:8], exponents[:, 2:4], ALU.pow))
            mags = vec[:, VEC["mag_q"][0]:VEC["mag_q"][0] + 2]
            G.tensor_tensor(fro[:, 8:10], fro[:, 6:8], mags, ALU.mult).then_inc(dora_done, 1)

            def weight1(c):
                for i in range(4):
                    r, n = (GMAX, 4) if i < 2 else (76, 2)
                    pool.wait_ge(scale1_done, 4 * c + i + 1)
                    p3 = part1(prob1[c % 2], i).rearrange("p (x j) -> p x j", x=n)
                    G.tensor_tensor(p3, p3, sum1[c % 2][0:r, 4 * i:4 * i + n].unsqueeze(2).to_broadcast([r, n, r]),
                                    ALU.mult).then_inc(prob1_done, 1)

            weight1(0)
            split(15)
            for c in range(C1):
                pool.wait_ge(dve_evac, evacuated("val", c, 1, 5))
                for r, a, b in ((GMAX, 0, 4), (76, 4, 6)):
                    for par in range(2):
                        v3 = vals[c % 2][0:r, a:b, 64 * par:64 * par + 64]
                        last = G.tensor_tensor(v3, v3, gmax[0:r, a:b, 2 * c + par].unsqueeze(2)
                                               .to_broadcast([r, b - a, 64]), ALU.mult)
                last.then_inc(vals_done, 1)
                for n in SPLITS1[c].get(-1, ()):
                    split(n)
                for e in range(E0):
                    if e % 2 == 0:
                        i = E0 * c + e
                        if i >= 4:
                            pool.wait_ge(expert_mms, i - 3)
                        o = T * (i % 4)
                        pool.wait_ge(gout_split, c + 1)
                        pool.wait_ge(act_evac, evacuated("sel", c, e, 1))
                        G.tensor_tensor(act_lo[:, o:o + T], gout_lo, chosen[i % 3], ALU.mult).then_inc(masked_pool, 1)
                    elif e == E0 - 1 and c + 1 < C1:
                        weight1(c + 1)
                    for n in SPLITS1[c].get(e, ()):
                        split(n)
            pool.wait_ge(probs_done, 1)
            image_of = const("image_of").rearrange("p (g b) -> p g b", g=6)
            for r, g in ((GRP[g][1], g) for g in range(6)):
                last = G.tensor_tensor(pspread[0:r, g].rearrange("p (b e) -> p b e", e=E3),
                                       probs[0:r, g, :].unsqueeze(1).to_broadcast([r, B, E3]),
                                       image_of[0:r, g].unsqueeze(2).to_broadcast([r, B, E3]), ALU.mult)
            last.then_inc(spread_done, 1)
            pool.wait_ge(pick_done, 1)
            G.tensor_tensor(pickw[0:GMAX, :].rearrange("p (a c) -> p a c", c=CAP),
                            pick[0:GMAX, :].rearrange("p (a c) -> p a c", c=CAP),
                            ptt[0:GMAX, 0:128].unsqueeze(2).to_broadcast([GMAX, 128, CAP]),
                            ALU.mult).then_inc(pickw_done, 1)


def constants():
    f = np.zeros((128, NCST), np.float32)
    b = np.zeros((128, NCSB), np.float32)

    def put(a, table, name, v):
        o, n = table[name]
        a[:v.shape[0], o:o + n] = v.reshape(v.shape[0], -1)

    i = np.arange(128)
    put(f, CST, "ident", np.eye(128))
    put(f, CST, "mean", np.full((128, 128), 1.0 / D))
    put(f, CST, "ones", np.ones((128, 128)))
    put(f, CST, "gn_block", (i[:, None] // 64 == i[None] // 64) / (64.0 * S))
    put(f, CST, "after", i[:, None] > i[None])
    put(f, CST, "neg_upto", -1.0 * (i[:, None] <= i[None]))
    t = np.arange(GMAX)
    put(f, CST, "pos_of", t[:, None] % S == np.arange(S)[None])
    first = [t0 // S for t0, _ in GRP]
    put(f, CST, "image_of", np.stack([t[:, None] // S + b0 == np.arange(B)[None] for b0 in first], 1))
    put(f, CST, "iota", np.tile(np.arange(CAP), (128, 1)))
    put(f, CST, "position", np.tile(np.arange(S), (128, 1)))
    put(f, CST, "desc", np.tile(E0 - np.arange(E0), (128, 1)))
    put(b, CSB, "ident", np.eye(128))
    for suffix, r in (("", GMAX), ("2", 76)):
        t = np.arange(r)
        seen = (t[:, None] // S == t[None] // S) & (t[:, None] >= t[None])
        put(b, CSB, "causal" + suffix, np.tile(np.where(seen, 0, -1e30), (1, 4)))
        put(b, CSB, "causal_t" + suffix, np.tile(np.where(seen.T, 0, -30000.0), (1, 4)))
    put(b, CSB, "same_pos", np.tile(np.where(i[:, None] % 32 // B == np.arange(32)[None] // B, 0, -1e30), (1, 16)))
    group_of = np.repeat([g for g, (_, r) in sorted(enumerate(GRP), key=lambda x: x[1][0])],
                         [r // S for _, r in sorted(GRP)])
    within = np.arange(B) - np.array(first)[group_of]
    other = np.arange(GMAX)[:, None] // S != within[None]
    put(b, CSB, "other_image", np.repeat(1024.0 * other, E3, 1))
    sel = np.zeros((H1, E0, E0, C1, 2, 64))
    for e in range(E0):
        for hd in range(H1):
            sel[hd, e, e, hd // 2, hd % 2, :] = 1
    put(b, CSB, "select", sel.reshape(64, -1))
    bits = (b.view(np.uint32) >> 16).astype(np.uint16)
    return f, bits


def feat(a):
    return a.reshape(-1, 128, a.shape[-1]).transpose(1, 0, 2)


def part(g, kind, i, j=0):
    two = slice(128 * i, 128 * i + 128)
    if kind == "v0":
        return feat(g["L0_attn_Wv"][:, 512 * i:512 * i + 512])
    if kind == "qkgo":
        return np.concatenate([feat(g[n][:, two]).reshape(128, -1) for n in ("L0_attn_Wq", "L0_attn_Wk", "L0_attn_Wg")]
                              + [g["L0_attn_Wo"][two]], 1)
    if kind == "qk1":
        return np.concatenate([feat(g[n][:, two]).reshape(128, -1) for n in ("L0_ffn_w_q", "L0_ffn_w_k")], 1)
    if kind == "val":
        return feat(g["L0_ffn_value_experts"][4 * j:4 * j + 4, 2 * i:2 * i + 2].transpose(2, 0, 1, 3).reshape(D, -1))
    if kind == "oexp":
        return g["L0_ffn_output_experts"][4 * j:4 * j + 4, 2 * i:2 * i + 2].reshape(4, 128, D).transpose(1, 0, 2)
    raise ValueError(kind)


def lay_out(i):
    g = {k: np.asarray(v) for k, v in i.items()}
    f, b = constants()
    x = g["x"].reshape(B, 3, 6, 16, 6, 16).transpose(1, 3, 5, 0, 2, 4).reshape(768, B * NP)
    vec = np.zeros((128, NVEC), np.float32)

    def put(name, v):
        o, n = VEC[name]
        vec[:, o:o + n] = v

    def chunks(v):
        return v.reshape(-1, 128).T

    put("b_lin", chunks(g["L0_tok_b_lin"]))
    put("cls", chunks(g["cls_tok"]))
    put("class_tok", chunks(g["L0_tok_class_token"]))
    put("bias_q", chunks(g["L1_attn_bias_q"]))
    put("k_b", chunks(g["L1_attn_k_b"]))
    put("out_b", chunks(g["L1_attn_out_b"]))
    put("gn_w", chunks(g["L0_attn_gn_w"]))
    put("gn_b", chunks(g["L0_attn_gn_b"]))
    put("mag_q", g["L1_attn_mag_q"])
    put("mag_v", g["L1_attn_mag_v"])
    even = (np.arange(128) // HD2 % 2 == 0).astype(np.float32)[:, None]
    put("even", even)
    put("odd", 1 - even)
    rows = np.broadcast_to(np.concatenate([g["L0_attn_ba"], g["L1_attn_bias_v"]])[None], (128, 16 + D))
    lora = np.concatenate([g["L1_attn_A_q"], g["L1_attn_B_q"].T, g["L1_attn_A_v"], g["L1_attn_B_v"].T], 1)
    out = {
        "cst": f, "csb": b, "vec": vec, "rows": rows, "lora": lora,
        "pos": feat(g["L0_tok_position_embeddings"][0].T),
        "patches": feat(x), "wlin": feat(g["L0_tok_W_lin"].T),
        "wa": feat(g["L0_attn_Wa"]),
        "dora0": feat(g["L1_attn_dir_q"].T), "dora1": feat(g["L1_attn_dir_v"].T),
        "pieces": np.concatenate([part(g, *name).reshape(128, -1) for name, _ in PIECES], 1),
        "mlp": np.concatenate([w for e in range(E3) for w in (
            feat(g["L1_ffn_w1"][e]).reshape(128, -1),
            g["L1_ffn_w2"][e].reshape(4, 128, D).transpose(1, 0, 2).reshape(128, -1))], 1),
        "gate1": feat(g["L0_ffn_w_gate"]),
        "k2": feat(g["L1_attn_k_w"].T), "out2": feat(g["L1_attn_out_w"].T),
        "choice": feat(g["L1_ffn_choice_w"].T),
    }
    return {k: np.ascontiguousarray(v) for k, v in out.items()}


def kernel(**inputs):
    import concourse.bacc as bacc
    from concourse.bass_utils import run_bass_kernel_spmd

    nc = bacc.Bacc("TRN2", target_bir_lowering=False, num_devices=1)
    arrays = lay_out(inputs)
    io = {n: nc.dram_tensor(f"in_{n}", a.shape, mybir.dt.from_np(a.dtype), kind="ExternalInput").ap()
          for n, a in arrays.items()}
    io["out"] = nc.dram_tensor("out_t", (D, T), F32, kind="ExternalOutput").ap()
    build(nc, io)
    r = run_bass_kernel_spmd(nc, [{f"in_{n}": a for n, a in arrays.items()}], core_ids=[0])
    return r.results[0]["out_t"].reshape(D, B, S).transpose(1, 2, 0)
```
